# Optimizing a Trainium2 kernel written in Bass

```python
import numpy as np
import jax
import jax.numpy as jnp

def _softmax(x, axis=-1):
    return jax.nn.softmax(x, axis=axis)

def _gelu(x):
    return jax.nn.gelu(x, approximate=True)

def _silu(x):
    return jax.nn.silu(x)

def _sigmoid(x):
    return jax.nn.sigmoid(x)

def _layernorm(x, axis=-1, eps=1e-05):
    m = jnp.mean(x, axis=axis, keepdims=True)
    v = jnp.var(x, axis=axis, keepdims=True)
    return (x - m) / jnp.sqrt(v + eps)

def _scatter_add(tgt, idx, src, axis=0):
    return tgt.at[idx].add(src)

def _segment_sum(src, seg, n):
    return jax.ops.segment_sum(src, seg, n)
kernel_name = 'mk_perceiver_d1_seqx_r8_103062'

def setup_inputs(seed: int=0):
    np.random.seed(seed)
    _w = jnp.asarray

    def _rec_inputs():
        import jax
        import jax.numpy as jnp
        _rk = jax.random.key(seed)
        x = -0.0002928 + 1 * jax.random.normal(jax.random.fold_in(_rk, 1), (128, 32, 256), jnp.float32)
        _lenS = 32 - jax.random.randint(jax.random.fold_in(_rk, 7), (128,), 0, max(1, 32 // 4) + 1, jnp.int32)
        _lenS2 = 257 - jax.random.randint(jax.random.fold_in(_rk, 8), (128,), 0, max(1, 257 // 4) + 1, jnp.int32)
        _ctx_512P = jax.random.normal(jax.random.fold_in(_rk, 11), (128, 16, 64), jnp.float32)
        _ctx_512c = jax.random.dirichlet(jax.random.fold_in(_rk, 511), 0.3 * jnp.ones((16,), jnp.float32), (128, 257))
        _ctx_512t = jnp.einsum('bsk,bkd->bsd', _ctx_512c, _ctx_512P)
        _ctx_512t = _ctx_512t * jax.lax.rsqrt(jnp.mean(jnp.square(_ctx_512t)) + 1e-12) * 0.953939
        ctx_512 = 0.000227908 + 0.99994 * (_ctx_512t + 0.3 * jax.random.normal(jax.random.fold_in(_rk, 611), (128, 257, 64), jnp.float32))
        return (x, ctx_512)
    x, ctx_512 = _rec_inputs()

    def _L0_xattn_setup():
        import jax, jax.numpy as jnp
        import numpy as np
        B, S, L = (2, 128, 128)
        DIM_Q, H, K, D_C, D_CQ, R = (256, 16, 128, 64, 192, 64)

        def _rope_tables(length, dim):
            inv = 1.0 / 10000.0 ** (jnp.arange(0, dim, 2, dtype=jnp.float32) / dim)
            f = jnp.arange(length, dtype=jnp.float32)[:, None] * inv[None, :]
            sin = jnp.repeat(jnp.sin(f), 2, axis=-1)
            cos = jnp.repeat(jnp.cos(f), 2, axis=-1)
            return (sin, cos)

        def _rotate_half(x):
            half = x.shape[-1] // 2
            return jnp.concatenate([-x[..., half:], x[..., :half]], axis=-1)

        def _apply_rope(x, sin, cos):
            return x * cos + _rotate_half(x) * sin
        key = jax.random.key(seed)
        ks = jax.random.split(key, 8)
        return {'hidden_q': jax.random.normal(ks[0], (B, S, DIM_Q), jnp.float32), 'kv_c': jax.random.normal(ks[1], (B, L, D_C), jnp.float32), 'Wq': jax.random.normal(ks[2], (H * K, DIM_Q), jnp.float32) / np.sqrt(DIM_Q).astype(np.float32), 'w_kc_q': jax.random.normal(ks[3], (H, K, D_CQ), jnp.float32) / np.sqrt(K).astype(np.float32), 'w_kc_kv': jax.random.normal(ks[4], (H, K, D_C), jnp.float32) / np.sqrt(K).astype(np.float32), 'W_qr': jax.random.normal(ks[5], (H, D_CQ, R), jnp.float32) / np.float32(np.sqrt(D_CQ) * np.sqrt(R)), 'W_kr': jax.random.normal(ks[6], (H, D_C, R), jnp.float32) / np.sqrt(D_C).astype(np.float32), 'Wo': jax.random.normal(ks[7], (DIM_Q, H * K), jnp.float32) / np.sqrt(H * K).astype(np.float32)}
    _L0_xattn_all = _L0_xattn_setup()
    _L0_xattn_in = {k: v for k, v in _L0_xattn_all.items() if k in ('Wq', 'w_kc_q', 'w_kc_kv', 'W_qr', 'W_kr', 'Wo')}
    del _L0_xattn_all

    def _L0_attn_setup():
        import jax, jax.numpy as jnp
        import numpy as np
        B, T, D = (1, 256, 256)
        H, DK, DV, M = (16, 64, 128, 64)
        KEY_DIM, VALUE_DIM = (H * DK, H * DV)
        EPS = 1e-05
        CLAMP_MIN, CLAMP_MAX = (-32.0, 32.0)
        XAVIER_GAIN = 2.0 ** (-2.5)

        def _chunk_abc(q, k, v, s):
            scale = q.shape[-1] ** (-0.5)
            z = jax.lax.cumlogsumexp(s, axis=2)
            g = jnp.exp(jnp.concatenate([z[:, :, :1], z[:, :, :-1]], axis=2) - z)
            p = jnp.exp(s - z)
            tfirst = lambda x: jnp.moveaxis(x, 2, 0)
            qT, kT, vT, pT, gT = map(tfirst, (q * scale, k, v, p, g))
            b, h = (q.shape[0], q.shape[1])
            hk0 = jnp.zeros((b, h, q.shape[-1], s.shape[-1]), q.dtype)

            def step_k(hk, x):
                q_t, k_t, p_t, g_t = x
                hk = hk * g_t[:, :, None, :] + k_t[..., None] * p_t[:, :, None, :]
                return (hk, jnp.einsum('bhk,bhkm->bhm', q_t, hk))
            _, okT = jax.lax.scan(step_k, hk0, (qT, kT, pT, gT))
            pvT = jax.nn.softmax(okT, axis=-1)
            hv0 = jnp.zeros((b, h, s.shape[-1], v.shape[-1]), q.dtype)

            def step_v(hv, x):
                pv_t, v_t, p_t, g_t = x
                hv = hv * g_t[..., None] + p_t[..., None] * v_t[:, :, None, :]
                return (hv, jnp.einsum('bhm,bhmv->bhv', pv_t, hv))
            _, ovT = jax.lax.scan(step_v, hv0, (pvT, vT, pT, gT))
            return jnp.moveaxis(ovT, 0, 2)
        key = jax.random.key(seed)
        ks = jax.random.split(key, 8)

        def w(k, fan_in, fan_out):
            std = XAVIER_GAIN * np.sqrt(2.0 / (fan_in + fan_out))
            return jax.random.normal(k, (fan_in, fan_out), jnp.float32) * std
        return {'hidden_states': jax.random.normal(ks[0], (B, T, D), jnp.float32), 'Wq': w(ks[1], D, KEY_DIM), 'Wk': w(ks[2], D, KEY_DIM), 'Wv': w(ks[3], D, VALUE_DIM), 'Wg': w(ks[4], D, VALUE_DIM), 'Ws': w(ks[5], D, H * M), 'Wo': w(ks[6], VALUE_DIM, D), 'g_norm_weight': jnp.ones((DV,), jnp.float32)}
    _L0_attn_all = _L0_attn_setup()
    _L0_attn_in = {k: v for k, v in _L0_attn_all.items() if k in ('Wq', 'Wk', 'Wv', 'Wg', 'Ws', 'Wo', 'g_norm_weight')}
    del _L0_attn_all

    def _L0_ffn_setup():
        import jax, jax.numpy as jnp
        import numpy as np
        COST_LAMBDA = 1e-07
        HID = [128, 256, 384, 512, 128, 256, 384, 512]
        TOP_K = 2

        def _gelu(v):
            return jax.nn.gelu(v, approximate=False)

        def _forward(x, down_w, down_b, up_w, up_b, router_w, router_b, shared_w1, shared_b1, shared_w2, shared_b2, core_w, core_b, expert_params):
            E = len(expert_params)
            h = x @ down_w + down_b
            cost = jnp.array([w1.shape[0] * w1.shape[1] + w2.shape[0] * w2.shape[1] for w1, _, w2, _ in expert_params], jnp.float32)
            logits = x @ router_w + router_b - COST_LAMBDA * cost
            probs = jax.nn.softmax(logits, axis=-1)
            topv, topi = jax.lax.top_k(probs, TOP_K)
            gate = jax.nn.softmax(topv, axis=-1)
            out = jnp.zeros_like(h)
            for k in range(TOP_K):
                mask = jax.nn.one_hot(topi[..., k], E, dtype=h.dtype)
                acc = jnp.zeros_like(h)
                for e, (w1, b1, w2, b2) in enumerate(expert_params):
                    hm = h * mask[..., e:e + 1]
                    acc = acc + (_gelu(_gelu(hm) @ w1 + b1) @ w2 + b2)
                out = out + acc * gate[..., k:k + 1]
            out = out + 0.1 * (_gelu(_gelu(h) @ shared_w1 + shared_b1) @ shared_w2 + shared_b2)
            out = out @ up_w + up_b
            out = out + (_gelu(x) @ core_w + core_b)
            return out
        key = jax.random.key(seed)
        ks = iter(jax.random.split(key, 80))

        def W(shape):
            return jax.random.normal(next(ks), shape, jnp.float32) * 0.02
        B, T, D, L = (4, 256, 256, 128)
        inp = {'x': jax.random.normal(next(ks), (B, T, D), jnp.float32)}
        inp['down_w'] = W((D, L))
        inp['down_b'] = jnp.zeros((L,), jnp.float32)
        inp['up_w'] = W((L, D))
        inp['up_b'] = jnp.zeros((D,), jnp.float32)
        inp['router_w'] = W((D, len(HID)))
        inp['router_b'] = jnp.zeros((len(HID),), jnp.float32)
        inp['shared_w1'] = W((L, L))
        inp['shared_b1'] = jnp.zeros((L,), jnp.float32)
        inp['shared_w2'] = W((L, L))
        inp['shared_b2'] = jnp.zeros((L,), jnp.float32)
        inp['core_w'] = W((D, D))
        inp['core_b'] = jnp.zeros((D,), jnp.float32)
        for e, h in enumerate(HID):
            inp[f'e{e}_w1'] = W((L, h))
            inp[f'e{e}_b1'] = jnp.zeros((h,), jnp.float32)
            inp[f'e{e}_w2'] = W((h, L))
            inp[f'e{e}_b2'] = jnp.zeros((L,), jnp.float32)
        return inp
    _L0_ffn_all = _L0_ffn_setup()
    _L0_ffn_in = {k: v for k, v in _L0_ffn_all.items() if k in ('down_w', 'down_b', 'up_w', 'up_b', 'router_w', 'router_b', 'shared_w1', 'shared_b1', 'shared_w2', 'shared_b2', 'core_w', 'core_b', 'e0_w1', 'e0_b1', 'e0_w2', 'e0_b2', 'e1_w1', 'e1_b1', 'e1_w2', 'e1_b2', 'e2_w1', 'e2_b1', 'e2_w2', 'e2_b2', 'e3_w1', 'e3_b1', 'e3_w2', 'e3_b2', 'e4_w1', 'e4_b1', 'e4_w2', 'e4_b2', 'e5_w1', 'e5_b1', 'e5_w2', 'e5_b2', 'e6_w1', 'e6_b1', 'e6_w2', 'e6_b2', 'e7_w1', 'e7_b1', 'e7_w2', 'e7_b2')}
    del _L0_ffn_all
    return {'x': x, 'ctx_512': ctx_512, 'L0_xattn_Wq': _L0_xattn_in['Wq'], 'L0_xattn_w_kc_q': _L0_xattn_in['w_kc_q'], 'L0_xattn_w_kc_kv': _L0_xattn_in['w_kc_kv'], 'L0_xattn_W_qr': _L0_xattn_in['W_qr'], 'L0_xattn_W_kr': _L0_xattn_in['W_kr'], 'L0_xattn_Wo': _L0_xattn_in['Wo'], 'L0_attn_Wq': _L0_attn_in['Wq'], 'L0_attn_Wk': _L0_attn_in['Wk'], 'L0_attn_Wv': _L0_attn_in['Wv'], 'L0_attn_Wg': _L0_attn_in['Wg'], 'L0_attn_Ws': _L0_attn_in['Ws'], 'L0_attn_Wo': _L0_attn_in['Wo'], 'L0_attn_g_norm_weight': _L0_attn_in['g_norm_weight'], 'L0_ffn_down_w': _L0_ffn_in['down_w'], 'L0_ffn_down_b': _L0_ffn_in['down_b'], 'L0_ffn_up_w': _L0_ffn_in['up_w'], 'L0_ffn_up_b': _L0_ffn_in['up_b'], 'L0_ffn_router_w': _L0_ffn_in['router_w'], 'L0_ffn_router_b': _L0_ffn_in['router_b'], 'L0_ffn_shared_w1': _L0_ffn_in['shared_w1'], 'L0_ffn_shared_b1': _L0_ffn_in['shared_b1'], 'L0_ffn_shared_w2': _L0_ffn_in['shared_w2'], 'L0_ffn_shared_b2': _L0_ffn_in['shared_b2'], 'L0_ffn_core_w': _L0_ffn_in['core_w'], 'L0_ffn_core_b': _L0_ffn_in['core_b'], 'L0_ffn_e0_w1': _L0_ffn_in['e0_w1'], 'L0_ffn_e0_b1': _L0_ffn_in['e0_b1'], 'L0_ffn_e0_w2': _L0_ffn_in['e0_w2'], 'L0_ffn_e0_b2': _L0_ffn_in['e0_b2'], 'L0_ffn_e1_w1': _L0_ffn_in['e1_w1'], 'L0_ffn_e1_b1': _L0_ffn_in['e1_b1'], 'L0_ffn_e1_w2': _L0_ffn_in['e1_w2'], 'L0_ffn_e1_b2': _L0_ffn_in['e1_b2'], 'L0_ffn_e2_w1': _L0_ffn_in['e2_w1'], 'L0_ffn_e2_b1': _L0_ffn_in['e2_b1'], 'L0_ffn_e2_w2': _L0_ffn_in['e2_w2'], 'L0_ffn_e2_b2': _L0_ffn_in['e2_b2'], 'L0_ffn_e3_w1': _L0_ffn_in['e3_w1'], 'L0_ffn_e3_b1': _L0_ffn_in['e3_b1'], 'L0_ffn_e3_w2': _L0_ffn_in['e3_w2'], 'L0_ffn_e3_b2': _L0_ffn_in['e3_b2'], 'L0_ffn_e4_w1': _L0_ffn_in['e4_w1'], 'L0_ffn_e4_b1': _L0_ffn_in['e4_b1'], 'L0_ffn_e4_w2': _L0_ffn_in['e4_w2'], 'L0_ffn_e4_b2': _L0_ffn_in['e4_b2'], 'L0_ffn_e5_w1': _L0_ffn_in['e5_w1'], 'L0_ffn_e5_b1': _L0_ffn_in['e5_b1'], 'L0_ffn_e5_w2': _L0_ffn_in['e5_w2'], 'L0_ffn_e5_b2': _L0_ffn_in['e5_b2'], 'L0_ffn_e6_w1': _L0_ffn_in['e6_w1'], 'L0_ffn_e6_b1': _L0_ffn_in['e6_b1'], 'L0_ffn_e6_w2': _L0_ffn_in['e6_w2'], 'L0_ffn_e6_b2': _L0_ffn_in['e6_b2'], 'L0_ffn_e7_w1': _L0_ffn_in['e7_w1'], 'L0_ffn_e7_b1': _L0_ffn_in['e7_b1'], 'L0_ffn_e7_w2': _L0_ffn_in['e7_w2'], 'L0_ffn_e7_b2': _L0_ffn_in['e7_b2']}

def reference(x, ctx_512, L0_xattn_Wq, L0_xattn_w_kc_q, L0_xattn_w_kc_kv, L0_xattn_W_qr, L0_xattn_W_kr, L0_xattn_Wo, L0_attn_Wq, L0_attn_Wk, L0_attn_Wv, L0_attn_Wg, L0_attn_Ws, L0_attn_Wo, L0_attn_g_norm_weight, L0_ffn_down_w, L0_ffn_down_b, L0_ffn_up_w, L0_ffn_up_b, L0_ffn_router_w, L0_ffn_router_b, L0_ffn_shared_w1, L0_ffn_shared_b1, L0_ffn_shared_w2, L0_ffn_shared_b2, L0_ffn_core_w, L0_ffn_core_b, L0_ffn_e0_w1, L0_ffn_e0_b1, L0_ffn_e0_w2, L0_ffn_e0_b2, L0_ffn_e1_w1, L0_ffn_e1_b1, L0_ffn_e1_w2, L0_ffn_e1_b2, L0_ffn_e2_w1, L0_ffn_e2_b1, L0_ffn_e2_w2, L0_ffn_e2_b2, L0_ffn_e3_w1, L0_ffn_e3_b1, L0_ffn_e3_w2, L0_ffn_e3_b2, L0_ffn_e4_w1, L0_ffn_e4_b1, L0_ffn_e4_w2, L0_ffn_e4_b2, L0_ffn_e5_w1, L0_ffn_e5_b1, L0_ffn_e5_w2, L0_ffn_e5_b2, L0_ffn_e6_w1, L0_ffn_e6_b1, L0_ffn_e6_w2, L0_ffn_e6_b2, L0_ffn_e7_w1, L0_ffn_e7_b1, L0_ffn_e7_w2, L0_ffn_e7_b2):
    import jax
    import jax.numpy as jnp

    def _L0_xattn_ref(hidden_q, kv_c, Wq, w_kc_q, w_kc_kv, W_qr, W_kr, Wo):
        import jax, jax.numpy as jnp
        import numpy as np
        B, S, L = (2, 128, 128)
        DIM_Q, H, K, D_C, D_CQ, R = (256, 16, 128, 64, 192, 64)

        def _rope_tables(length, dim):
            inv = 1.0 / 10000.0 ** (jnp.arange(0, dim, 2, dtype=jnp.float32) / dim)
            f = jnp.arange(length, dtype=jnp.float32)[:, None] * inv[None, :]
            sin = jnp.repeat(jnp.sin(f), 2, axis=-1)
            cos = jnp.repeat(jnp.cos(f), 2, axis=-1)
            return (sin, cos)

        def _rotate_half(x):
            half = x.shape[-1] // 2
            return jnp.concatenate([-x[..., half:], x[..., :half]], axis=-1)

        def _apply_rope(x, sin, cos):
            return x * cos + _rotate_half(x) * sin
        Bv, Sv, _ = hidden_q.shape
        _, Lv, _ = kv_c.shape
        q_hk = (hidden_q @ Wq.T).reshape(Bv, Sv, H, K)
        q_big = jnp.einsum('bshk,hkq->bshq', q_hk, w_kc_q)
        sin_q, cos_q = _rope_tables(Sv, D_CQ)
        q_big = _apply_rope(q_big, sin_q[None, :, None, :], cos_q[None, :, None, :])
        sin_k, cos_k = _rope_tables(Lv, D_C)
        kv_r = _apply_rope(kv_c, sin_k[None], cos_k[None])
        q_r = jnp.einsum('bshq,hqr->bhsr', q_big, W_qr)
        k_r = jnp.einsum('bld,hdr->bhlr', kv_r, W_kr)
        scores = jnp.einsum('bhsr,bhlr->bhsl', q_r, k_r)
        attn = jax.nn.softmax(scores, axis=-1)
        ctx_c = jnp.einsum('bhsl,bld->bhsd', attn, kv_r)
        ctx_lat = jnp.einsum('bhsd,hkd->bhsk', ctx_c, w_kc_kv)
        ctx = ctx_lat.transpose(0, 2, 1, 3).reshape(Bv, Sv, H * K)
        return ctx @ Wo.T

    def _L0_attn_ref(hidden_states, Wq, Wk, Wv, Wg, Ws, Wo, g_norm_weight):
        import jax, jax.numpy as jnp
        import numpy as np
        B, T, D = (1, 256, 256)
        H, DK, DV, M = (16, 64, 128, 64)
        KEY_DIM, VALUE_DIM = (H * DK, H * DV)
        EPS = 1e-05
        CLAMP_MIN, CLAMP_MAX = (-32.0, 32.0)
        XAVIER_GAIN = 2.0 ** (-2.5)

        def _chunk_abc(q, k, v, s):
            scale = q.shape[-1] ** (-0.5)
            z = jax.lax.cumlogsumexp(s, axis=2)
            g = jnp.exp(jnp.concatenate([z[:, :, :1], z[:, :, :-1]], axis=2) - z)
            p = jnp.exp(s - z)
            tfirst = lambda x: jnp.moveaxis(x, 2, 0)
            qT, kT, vT, pT, gT = map(tfirst, (q * scale, k, v, p, g))
            b, h = (q.shape[0], q.shape[1])
            hk0 = jnp.zeros((b, h, q.shape[-1], s.shape[-1]), q.dtype)

            def step_k(hk, x):
                q_t, k_t, p_t, g_t = x
                hk = hk * g_t[:, :, None, :] + k_t[..., None] * p_t[:, :, None, :]
                return (hk, jnp.einsum('bhk,bhkm->bhm', q_t, hk))
            _, okT = jax.lax.scan(step_k, hk0, (qT, kT, pT, gT))
            pvT = jax.nn.softmax(okT, axis=-1)
            hv0 = jnp.zeros((b, h, s.shape[-1], v.shape[-1]), q.dtype)

            def step_v(hv, x):
                pv_t, v_t, p_t, g_t = x
                hv = hv * g_t[..., None] + p_t[..., None] * v_t[:, :, None, :]
                return (hv, jnp.einsum('bhm,bhmv->bhv', pv_t, hv))
            _, ovT = jax.lax.scan(step_v, hv0, (pvT, vT, pT, gT))
            return jnp.moveaxis(ovT, 0, 2)
        b, t, _ = hidden_states.shape
        to_heads = lambda x, d: jnp.transpose(x.reshape(b, t, H, d), (0, 2, 1, 3))
        q = to_heads(hidden_states @ Wq, DK)
        k = to_heads(hidden_states @ Wk, DK)
        v = to_heads(hidden_states @ Wv, DV)
        s = jnp.clip(to_heads(hidden_states @ Ws, M), CLAMP_MIN, CLAMP_MAX)
        o = jnp.transpose(_chunk_abc(q, k, v, s), (0, 2, 1, 3))
        g = (hidden_states @ Wg).reshape(b, t, H, DV)
        o = o * jax.lax.rsqrt(jnp.mean(jnp.square(o), axis=-1, keepdims=True) + EPS) * g_norm_weight
        o = o * (g * jax.nn.sigmoid(g))
        return o.reshape(b, t, VALUE_DIM) @ Wo

    def _L0_ffn_ref(x, down_w, down_b, up_w, up_b, router_w, router_b, shared_w1, shared_b1, shared_w2, shared_b2, core_w, core_b, e0_w1, e0_b1, e0_w2, e0_b2, e1_w1, e1_b1, e1_w2, e1_b2, e2_w1, e2_b1, e2_w2, e2_b2, e3_w1, e3_b1, e3_w2, e3_b2, e4_w1, e4_b1, e4_w2, e4_b2, e5_w1, e5_b1, e5_w2, e5_b2, e6_w1, e6_b1, e6_w2, e6_b2, e7_w1, e7_b1, e7_w2, e7_b2):
        import jax, jax.numpy as jnp
        import numpy as np
        COST_LAMBDA = 1e-07
        HID = [128, 256, 384, 512, 128, 256, 384, 512]
        TOP_K = 2

        def _gelu(v):
            return jax.nn.gelu(v, approximate=False)

        def _forward(x, down_w, down_b, up_w, up_b, router_w, router_b, shared_w1, shared_b1, shared_w2, shared_b2, core_w, core_b, expert_params):
            E = len(expert_params)
            h = x @ down_w + down_b
            cost = jnp.array([w1.shape[0] * w1.shape[1] + w2.shape[0] * w2.shape[1] for w1, _, w2, _ in expert_params], jnp.float32)
            logits = x @ router_w + router_b - COST_LAMBDA * cost
            probs = jax.nn.softmax(logits, axis=-1)
            topv, topi = jax.lax.top_k(probs, TOP_K)
            gate = jax.nn.softmax(topv, axis=-1)
            out = jnp.zeros_like(h)
            for k in range(TOP_K):
                mask = jax.nn.one_hot(topi[..., k], E, dtype=h.dtype)
                acc = jnp.zeros_like(h)
                for e, (w1, b1, w2, b2) in enumerate(expert_params):
                    hm = h * mask[..., e:e + 1]
                    acc = acc + (_gelu(_gelu(hm) @ w1 + b1) @ w2 + b2)
                out = out + acc * gate[..., k:k + 1]
            out = out + 0.1 * (_gelu(_gelu(h) @ shared_w1 + shared_b1) @ shared_w2 + shared_b2)
            out = out @ up_w + up_b
            out = out + (_gelu(x) @ core_w + core_b)
            return out
        ep = [(e0_w1, e0_b1, e0_w2, e0_b2), (e1_w1, e1_b1, e1_w2, e1_b2), (e2_w1, e2_b1, e2_w2, e2_b2), (e3_w1, e3_b1, e3_w2, e3_b2), (e4_w1, e4_b1, e4_w2, e4_b2), (e5_w1, e5_b1, e5_w2, e5_b2), (e6_w1, e6_b1, e6_w2, e6_b2), (e7_w1, e7_b1, e7_w2, e7_b2)]
        return _forward(x, down_w, down_b, up_w, up_b, router_w, router_b, shared_w1, shared_b1, shared_w2, shared_b2, core_w, core_b, ep)
    x = x + _L0_xattn_ref(_layernorm(x, axis=-1), ctx_512, L0_xattn_Wq, L0_xattn_w_kc_q, L0_xattn_w_kc_kv, L0_xattn_W_qr, L0_xattn_W_kr, L0_xattn_Wo)
    x = x + _L0_attn_ref(_layernorm(x, axis=-1), L0_attn_Wq, L0_attn_Wk, L0_attn_Wv, L0_attn_Wg, L0_attn_Ws, L0_attn_Wo, L0_attn_g_norm_weight)
    x = x + _L0_ffn_ref(_layernorm(x, axis=-1), L0_ffn_down_w, L0_ffn_down_b, L0_ffn_up_w, L0_ffn_up_b, L0_ffn_router_w, L0_ffn_router_b, L0_ffn_shared_w1, L0_ffn_shared_b1, L0_ffn_shared_w2, L0_ffn_shared_b2, L0_ffn_core_w, L0_ffn_core_b, L0_ffn_e0_w1, L0_ffn_e0_b1, L0_ffn_e0_w2, L0_ffn_e0_b2, L0_ffn_e1_w1, L0_ffn_e1_b1, L0_ffn_e1_w2, L0_ffn_e1_b2, L0_ffn_e2_w1, L0_ffn_e2_b1, L0_ffn_e2_w2, L0_ffn_e2_b2, L0_ffn_e3_w1, L0_ffn_e3_b1, L0_ffn_e3_w2, L0_ffn_e3_b2, L0_ffn_e4_w1, L0_ffn_e4_b1, L0_ffn_e4_w2, L0_ffn_e4_b2, L0_ffn_e5_w1, L0_ffn_e5_b1, L0_ffn_e5_w2, L0_ffn_e5_b2, L0_ffn_e6_w1, L0_ffn_e6_b1, L0_ffn_e6_w2, L0_ffn_e6_b2, L0_ffn_e7_w1, L0_ffn_e7_b1, L0_ffn_e7_w2, L0_ffn_e7_b2)
    return x

_drawn_inputs = setup_inputs


def setup_inputs(seed=0):
    import zlib

    import numpy as np

    out = dict(_drawn_inputs(seed))
    spreads = {'L0_attn_g_norm_weight': (1.0, 0.6),
     'L0_ffn_down_b': (0.0, 0.8),
     'L0_ffn_up_b': (0.0, 0.1),
     'L0_ffn_router_b': (0.0, 0.8),
     'L0_ffn_shared_b1': (0.0, 0.8),
     'L0_ffn_shared_b2': (0.0, 0.8),
     'L0_ffn_core_b': (0.0, 0.1),
     'L0_ffn_e0_b1': (0.0, 0.8),
     'L0_ffn_e0_b2': (0.0, 0.372),
     'L0_ffn_e1_b1': (0.0, 0.8),
     'L0_ffn_e1_b2': (0.0, 0.373),
     'L0_ffn_e2_b1': (0.0, 0.8),
     'L0_ffn_e2_b2': (0.0, 0.359),
     'L0_ffn_e3_b1': (0.0, 0.8),
     'L0_ffn_e3_b2': (0.0, 0.42),
     'L0_ffn_e4_b1': (0.0, 0.8),
     'L0_ffn_e4_b2': (0.0, 0.345),
     'L0_ffn_e5_b1': (0.0, 0.8),
     'L0_ffn_e5_b2': (0.0, 0.413),
     'L0_ffn_e6_b1': (0.0, 0.8),
     'L0_ffn_e6_b2': (0.0, 0.334),
     'L0_ffn_e7_b1': (0.0, 0.8),
     'L0_ffn_e7_b2': (0.0, 0.377)}
    factors = {'L0_attn_Wq': 8.0,
     'L0_attn_Wk': 8.0,
     'L0_attn_Wv': 5.853,
     'L0_attn_Wg': 5.856,
     'L0_attn_Ws': 8.0,
     'L0_attn_Wo': 5.865,
     'L0_ffn_down_w': 8.0,
     'L0_ffn_router_w': 8.0,
     'L0_ffn_shared_w1': 8.0,
     'L0_ffn_shared_w2': 8.0,
     'L0_ffn_e0_w1': 8.0,
     'L0_ffn_e0_w2': 8.0,
     'L0_ffn_e1_w1': 8.0,
     'L0_ffn_e1_w2': 8.0,
     'L0_ffn_e2_w1': 8.0,
     'L0_ffn_e2_w2': 8.0,
     'L0_ffn_e3_w1': 8.0,
     'L0_ffn_e3_w2': 8.0,
     'L0_ffn_e4_w1': 8.0,
     'L0_ffn_e4_w2': 8.0,
     'L0_ffn_e5_w1': 8.0,
     'L0_ffn_e5_w2': 8.0,
     'L0_ffn_e6_w1': 8.0,
     'L0_ffn_e6_w2': 8.0,
     'L0_ffn_e7_w1': 8.0,
     'L0_ffn_e7_w2': 8.0}
    for name, (base, spread) in spreads.items():
        noise = np.random.default_rng([zlib.crc32(name.encode()), seed]).standard_normal(out[name].shape)
        drawn = base * np.exp(spread * noise) if base else spread * noise
        out[name] = jnp.asarray(drawn.astype(out[name].dtype))
    for name, factor in factors.items():
        out[name] = (out[name] * factor).astype(out[name].dtype)
    return out
```

```python
from contextlib import ExitStack

import numpy as np

import concourse.bass as bass
from concourse import mybir

F32 = mybir.dt.float32
ALU = mybir.AluOpType
ACT = mybir.ActivationFunctionType
X = mybir.AxisListType.X

P = 128
B, S, D = 128, 32, 256
ROWS = B * S
NT = ROWS // P
BT = P // S
DC = D // P
EPS = 1e-5

L, H, HK, CD, CQ, R = 257, 16, 128, 64, 192, 64
QC = CQ // 2
HH = H // 2
NP = HH // 2
LC, LN = 3, 86
SG = 4

AH, DK, DV, M = 16, 64, 128, 64
GH = 4
NG = AH // GH

HID = [128, 256, 384, 512, 128, 256, 384, 512]
NE = len(HID)
FL = 128
NCH = sum(HID) // P
CHUNK_EXPERT = [e for e, h in enumerate(HID) for _ in range(h // P)]
TG = 4
COST_LAMBDA = 1e-07


def until(eng, sem, count):
    if not (isinstance(count, int) and count <= 0):
        eng.wait_ge(sem, count)


def steps(eng, step, units, group, lead, lag, loop=True):
    assert lead <= group and lag <= group and units % group == 0

    def offset(t, b, i):
        def at(o):
            u = t + o
            if isinstance(u, int) and not 0 <= u < units:
                return None
            return u, (b + o) % group, i + (b + o) // group
        return at

    if not loop:
        for t in range(-lead, units + lag):
            step(offset(t, t % group, t // group))
        return
    for t in range(-lead, group):
        step(offset(t, t % group, t // group))
    with eng.Fori(1, units // group - 1) as i:
        for b in range(group):
            step(offset(i * group + b, b, i))
    for t in range(units - group, units + lag):
        step(offset(t, t % group, t // group))



def row_statistics(nc, sem, x_sb, mean, rstd, half, tag):
    with ExitStack() as ctx:
        stats = ctx.enter_context(nc.sbuf_tensor(f"{tag}_stats", [P, NT, 6], F32))
        diff = ctx.enter_context(nc.sbuf_tensor(f"{tag}_diff", [P, NT], F32))
        var = ctx.enter_context(nc.sbuf_tensor(f"{tag}_var", [P, NT], F32))
        stats_done, step_done, var_done, rstd_done = (
            sem(f"{tag}_stats_done"), sem(f"{tag}_step_done"), sem(f"{tag}_var_done"), sem(f"{tag}_rstd_done"))
        block = ctx.enter_context(nc.Block())

        @block.vector
        def _(dve):
            with dve.Fori(0, NT) as i:
                dve.bn_stats(stats[:, i, :], x_sb[:, i, :]).then_inc(stats_done, 1)
            dve.wait_ge(stats_done, NT)
            dve.tensor_tensor(mean[:, :], stats[:, :, 1], stats[:, :, 4], ALU.add).then_inc(step_done, 1)
            dve.tensor_tensor(diff[:, :], stats[:, :, 1], stats[:, :, 4], ALU.subtract).then_inc(step_done, 1)
            dve.tensor_tensor(var[:, :], stats[:, :, 2], stats[:, :, 5], ALU.add).then_inc(step_done, 1)
            dve.wait_ge(step_done, 3)
            dve.tensor_scalar(mean[:, :], mean[:, :], 0.5, None, ALU.mult).then_inc(step_done, 1)
            dve.scalar_tensor_tensor(diff[:, :], diff[:, :], 0.25, diff[:, :], ALU.mult, ALU.mult).then_inc(step_done, 1)
            dve.tensor_scalar(var[:, :], var[:, :], 1.0 / D, EPS, ALU.mult, ALU.add).then_inc(step_done, 1)
            dve.wait_ge(step_done, 6)
            dve.tensor_tensor(var[:, :], var[:, :], diff[:, :], ALU.add).then_inc(var_done, 1)

        @block.gpsimd
        def _(pool):
            pool.wait_ge(var_done, 1)
            pool.tensor_tensor(rstd[:, :], var[:, :], half[:, 0:NT], ALU.pow).then_inc(rstd_done, 1)


def transposed_rows(nc, sem, x_sb, mean, rstd, ident, place, tag):
    with ExitStack() as ctx:
        xn = ctx.enter_context(nc.sbuf_tensor(f"{tag}_xn", [P, 2, D], F32))
        turned = ctx.enter_context(nc.psum_tensor(f"{tag}_turned", [P, 2, 512], F32))
        xn_ready, turn_done, place_done = sem(f"{tag}_xn_ready"), sem(f"{tag}_turn_done"), sem(f"{tag}_place_done")
        block = ctx.enter_context(nc.Block())

        @block.vector
        def _(dve):
            def step(at):
                i, b, _ = at(0)
                until(dve, turn_done, i - 1)
                dve.tensor_scalar(xn[:, b, :], x_sb[:, i, :], mean[:, bass.ds(i, 1)], rstd[:, bass.ds(i, 1)],
                                  ALU.subtract, ALU.mult).then_inc(xn_ready, 1)
            steps(dve, step, NT, 2, 0, 0)

        @block.tensor
        def _(pe):
            def step(at):
                i, b, _ = at(0)
                until(pe, xn_ready, i + 1)
                until(pe, place_done, i - 1)
                for c in range(DC):
                    last = pe.transpose(turned[:, b, c * P:(c + 1) * P], xn[:, b, c * P:(c + 1) * P], ident[:, :])
                last.then_inc(turn_done, 1)
            steps(pe, step, NT, 2, 0, 0)

        @block.scalar
        def _(act):
            def step(at):
                i, b, _ = at(0)
                until(act, turn_done, i + 1)
                act.activation(place(i), turned[:, b, 0:D].rearrange("p (c b s) -> p c b s", c=DC, b=BT),
                               ACT.Copy).then_inc(place_done, 1)
            steps(act, step, NT, 2, 0, 0)



def fold_weights(nc, sem, w, hh, qmap, gmap, omap, tag):
    with ExitStack() as ctx:
        def sb(name, shape):
            return ctx.enter_context(nc.sbuf_tensor(f"{tag}_{name}", shape, F32))

        wq, wkq, wkv, wo = sb("wq", [P, HH, D]), sb("wkq", [P, HH, CQ]), sb("wkv", [P, HH, CD]), sb("wo", [P, HH, D])
        wqr, wkr = sb("wqr", [R, HH, CQ]), sb("wkr", [R, HH, CD])
        bank = ctx.enter_context(nc.psum_tensor(f"{tag}_bank", [P, 3, 512], F32))
        loaded = [sem(f"{tag}_{n}_loaded") for n in ("q", "g", "o")]
        product_done, q_copied, g_copied, o_copied = (
            sem(f"{tag}_product_done"), sem(f"{tag}_q_copied"), sem(f"{tag}_g_copied"), sem(f"{tag}_o_copied"))
        block = ctx.enter_context(nc.Block())
        h0 = hh * HH

        @block.sync
        def _(sp):
            sp.dma_start(wq[:, :, :], w["wq"][h0 * HK:(h0 + HH) * HK, :].rearrange("(h k) d -> k h d", k=HK)).then_inc(loaded[0], 16)
            sp.dma_start(wkq[:, :, :], w["wkq"][h0:h0 + HH].rearrange("h k q -> k h q")).then_inc(loaded[0], 16)
            sp.dma_start(wqr[:, :, :], w["wqr_t"][h0:h0 + HH].rearrange("h r q -> r h q")).then_inc(loaded[1], 16)
            sp.dma_start(wkr[:, :, :], w["wkr_t"][h0:h0 + HH].rearrange("h r d -> r h d")).then_inc(loaded[1], 16)
            sp.dma_start(wkv[:, :, :], w["wkv"][h0:h0 + HH].rearrange("h k d -> k h d")).then_inc(loaded[2], 16)
            sp.dma_start(wo[:, :, :], w["xwo_t"][h0 * HK:(h0 + HH) * HK, :].rearrange("(h k) d -> k h d", k=HK)).then_inc(loaded[2], 16)

        @block.tensor
        def _(pe):
            pe.wait_ge(loaded[0], 32)
            for h in range(HH):
                until(pe, q_copied, h)
                for c in range(2):
                    last = pe.matmul(bank[0:QC, 0, c * D:(c + 1) * D], wkq[:, h, c * QC:(c + 1) * QC], wq[:, h, :],
                                     start=True, stop=True)
                last.then_inc(product_done, 1)
                if h == 0:
                    pe.wait_ge(loaded[1], 32)
                    pe.wait_ge(loaded[2], 32)
                until(pe, g_copied, h)
                for c in range(2):
                    last = pe.matmul(bank[0:QC, 1, c * CD:(c + 1) * CD], wqr[:, h, c * QC:(c + 1) * QC], wkr[:, h, :],
                                     start=True, stop=True)
                last.then_inc(product_done, 1)
                e = h % 2 * CD
                until(pe, o_copied, h)
                pe.matmul(bank[e:e + CD, 2, 0:D], wkv[:, h, :], wo[:, h, :], start=True, stop=True).then_inc(product_done, 1)

        @block.vector
        def _(dve):
            for h in range(HH):
                dve.wait_ge(product_done, 3 * h + 2)
                dve.tensor_copy(gmap[:, :, h, :], bank[0:QC, 1, 0:2 * CD].rearrange("p (c d) -> p c d", c=2)).then_inc(g_copied, 1)
                dve.wait_ge(product_done, 3 * h + 3)
                e = h % 2 * CD
                dve.tensor_copy(omap[e:e + CD, h // 2, :], bank[e:e + CD, 2, 0:D]).then_inc(o_copied, 1)

        @block.scalar
        def _(act):
            for h in range(HH):
                act.wait_ge(product_done, 3 * h + 1)
                act.activation(qmap[:, :, h, :], bank[0:QC, 0, :].rearrange("p (c d) -> p c d", c=2), ACT.Copy).then_inc(q_copied, 1)


def make_queries(nc, sem, qmap, gmap, cos_q, sin_q, xnt, queries, tag):
    units = S // SG * NP
    with ExitStack() as ctx:
        def sb(name, shape):
            return ctx.enter_context(nc.sbuf_tensor(f"{tag}_{name}", shape, F32))

        turned = [sb(f"turned{n}", [QC, 2, 2, SG, CD]) for n in range(2)]
        maps = [sb(f"maps{n}", [P, DC, SG, 2, CD]) for n in range(2)]
        map_ps = [ctx.enter_context(nc.psum_tensor(f"{tag}_map_ps{n}", [P, DC, SG, CD], F32)) for n in range(2)]
        query_ps = [ctx.enter_context(nc.psum_tensor(f"{tag}_query_ps{n}", [P, SG, B], F32)) for n in range(2)]
        cos_done, turned_ready = sem(f"{tag}_cos_done"), sem(f"{tag}_turned_ready")
        map_done = [sem(f"{tag}_map_done{n}") for n in range(2)]
        map_copied = [sem(f"{tag}_map_copied{n}") for n in range(2)]
        query_done, query_copied = sem(f"{tag}_query_done"), sem(f"{tag}_query_copied")
        block = ctx.enter_context(nc.Block())

        @block.scalar
        def _(act):
            def step(at):
                if at(2):
                    u, n, g = at(2)
                    for k in range(2):
                        for s in range(SG):
                            s_at = g * SG + s
                            last = act.activation(turned[n % 2][:, k, :, s, :], gmap[:, k, 2 * n:2 * n + 2, :], ACT.Copy,
                                                  scale=cos_q[:, k, bass.ds(s_at, 1)])
                    last.then_inc(cos_done, 1)
                if at(1):
                    u, n, g = at(1)
                    act.wait_ge(map_done[1], u + 1)
                    until(act, query_done, u - 1)
                    act.activation(maps[n % 2][:, :, :, 0, :], map_ps[0][:, :, :, :], ACT.Copy).then_inc(map_copied[0], 1)
            steps(act, step, units, NP, 2, 0)

        @block.vector
        def _(dve):
            def step(at):
                if at(2):
                    u, n, g = at(2)
                    dve.wait_ge(cos_done, u + 1)
                    for k in range(2):
                        for s in range(SG):
                            s_at = g * SG + s
                            out = turned[n % 2][:, k, :, s, :]
                            last = dve.scalar_tensor_tensor(out, gmap[:, 1 - k, 2 * n:2 * n + 2, :], sin_q[:, k, bass.ds(s_at, 1)],
                                                            out, ALU.mult, ALU.add)
                    last.then_inc(turned_ready, 1)
                if at(1):
                    u, n, g = at(1)
                    dve.wait_ge(map_done[1], u + 1)
                    until(dve, query_done, u - 1)
                    dve.tensor_copy(maps[n % 2][:, :, :, 1, :], map_ps[1][:, :, :, :]).then_inc(map_copied[1], 1)
                if at(0):
                    u, n, g = at(0)
                    dve.wait_ge(query_done, u + 1)
                    s_at = g * SG
                    dve.tensor_copy(queries[:, n, bass.ds(s_at, SG), :], query_ps[n % 2][:, :, :]).then_inc(query_copied, 1)
            steps(dve, step, units, NP, 2, 0)

        @block.tensor
        def _(pe):
            def step(at):
                if at(1):
                    u, n, g = at(1)
                    pe.wait_ge(turned_ready, u + 1)
                    for e in range(2):
                        until(pe, map_copied[e], u)
                        for m in range(DC):
                            for k in range(2):
                                last = pe.matmul(map_ps[e][:, m, :, :], qmap[:, k, 2 * n + e, m * P:(m + 1) * P],
                                                 turned[n % 2][:, k, e, :, :], start=k == 0, stop=k == 1)
                        last.then_inc(map_done[e], 1)
                if at(0):
                    u, n, g = at(0)
                    for e in range(2):
                        pe.wait_ge(map_copied[e], u + 1)
                    until(pe, query_copied, u - 1)
                    for s in range(SG):
                        s_at = g * SG + s
                        for m in range(DC):
                            last = pe.matmul(query_ps[n % 2][:, s, :], maps[n % 2][:, m, s, :, :],
                                             xnt[:, m, bass.ds(s_at, 1), :], start=m == 0, stop=m == DC - 1)
                    last.then_inc(query_done, 1)
            steps(pe, step, units, NP, 1, 0)


def attend(nc, sem, w, x_sb, queries, omap, cos_k, sin_k, ident, tag):
    with ExitStack() as ctx:
        def sb(name, shape):
            return ctx.enter_context(nc.sbuf_tensor(f"{tag}_{name}", shape, F32))

        def ps(name, shape):
            return ctx.enter_context(nc.psum_tensor(f"{tag}_{name}", shape, F32))

        raw = [sb(f"raw{n}", [LN, LC, CD]) for n in range(4)]
        swap = sb("swap", [LN, LC, CD])
        direct = sb("direct", [LN, LC, CD])
        keys = [sb(f"keys{n}", [LN, LC, 2, CD]) for n in range(4)]
        keys_t = [sb(f"keys_t{n}", [P, LC * LN]) for n in range(2)]
        query = [sb(f"query{n}", [P, NP, S]) for n in range(2)]
        peak = sb("peak", [P, 2, 2])
        total = sb("total", [P, 2, 2])
        inverse = sb("inverse", [P, 2, 2])
        weights = [sb(f"weights{n}", [P, 2, LC * LN]) for n in range(2)]
        weights_t = [sb(f"weights_t{n}", [LN, 2, LC, P]) for n in range(2)]
        context = [sb(f"context{n}", [P, 2, CD]) for n in range(2)]
        context_t = sb("context_t", [P, NP, BT, S])

        turn_ps = ps("turn_ps", [P, 512])
        score_ps = [ps(f"score_ps{n}", [P, 2, 512]) for n in range(2)]
        weight_ps = ps("weight_ps", [P, 2, 512])
        sum_ps = ps("sum_ps", [P, 512])

        raw_loaded = [sem(f"{tag}_raw_loaded{n}") for n in range(4)]
        names = ("cleared", "product", "swapped", "keys_ready", "query_ready", "keys_turned", "keys_t_ready", "scored", "peak_ready",
                 "padded", "weighed", "weights_turned", "weights_t0", "weights_t1", "summed", "inverted", "context_ready",
                 "context_turned", "context_t_ready", "projected", "added")
        s = {n: sem(f"{tag}_{n}") for n in names}
        block = ctx.enter_context(nc.Block())

        @block.sync
        def _(sp):
            sp.wait_ge(s["cleared"], 1)
            def step(at):
                if at(4):
                    u, n, g = at(4)
                    until(sp, s["product"], u - 3)
                    until(sp, s["swapped"], u - 3)
                    full = (LC - 1) * LN
                    kv = w["ctx"][bass.ds(u, 1), :, :]
                    sp.dma_start(raw[n][:, 0:LC - 1, :], kv[:, 0:full, :].rearrange("o (c p) d -> p (o c) d", p=LN)).then_inc(raw_loaded[n], 16)
                    sp.dma_start(raw[n][0:L - full, LC - 1, :], kv[:, full:L, :].rearrange("o p d -> p (o d)")).then_inc(raw_loaded[n], 16)
            steps(sp, step, B, 4, 4, 0)

        @block.gpsimd
        def _(pool):
            for n in range(4):
                last = pool.memset(raw[n][:, LC - 1, :], 0.0)
            last.then_inc(s["cleared"], 1)

            def step(at):
                if at(3):
                    u, n, g = at(3)
                    pool.wait_ge(raw_loaded[n], g * 32 + 32)
                    until(pool, s["keys_ready"], u)
                    h = CD // 2
                    pool.tensor_tensor(direct[:, :, :], raw[n][:, :, :], cos_k[:, :, :], ALU.mult).then_inc(s["product"], 1)
                    pool.tensor_tensor(swap[:, :, 0:h], raw[n][:, :, h:CD], sin_k[:, :, 0:h], ALU.mult)
                    pool.tensor_tensor(swap[:, :, h:CD], raw[n][:, :, 0:h], sin_k[:, :, h:CD], ALU.mult).then_inc(s["swapped"], 1)
                if at(2):
                    u, n, g = at(2)
                    until(pool, s["scored"], u - 1)
                    pool.tensor_copy(query[n % 2][:, :, :], queries[:, :, :, bass.ds(u, 1)].rearrange("p a s o -> p a (s o)")).then_inc(s["query_ready"], 1)
                if at(3):
                    u, n, g = at(3)
                    pool.wait_ge(s["product"], u + 1)
                    pool.wait_ge(s["swapped"], u + 1)
                    until(pool, s["summed"], u - 3)
                    for e in range(2):
                        last = pool.tensor_tensor(keys[n][:, :, e, :], direct[:, :, :], swap[:, :, :], ALU.add)
                    last.then_inc(s["keys_ready"], 1)
            steps(pool, step, B, 4, 3, 0)

        @block.tensor
        def _(pe):
            def step(at):
                if at(1):
                    u, n, g = at(1)
                    pe.wait_ge(s["keys_t_ready"], u + 1)
                    pe.wait_ge(s["query_ready"], u + 1)
                    until(pe, s["weighed"], u - 1)
                    for e in range(2):
                        a = e * CD
                        last = pe.matmul(score_ps[n % 2][:, e, 0:L], query[n % 2][a:a + CD, :, :], keys_t[n % 2][a:a + CD, 0:L],
                                         start=True, stop=True)
                    last.then_inc(s["scored"], 1)
                if at(-2):
                    u, n, g = at(-2)
                    pe.wait_ge(s["context_ready"], u + 1)
                    pe.wait_ge(s["keys_t_ready"], min(u + 4, B) if isinstance(u, int) else u + 4)
                    until(pe, s["context_t_ready"], u)
                    pe.transpose(turn_ps[:, 0:P], context[n % 2][:, :, :].rearrange("p e d -> p (e d)"), ident[:, :]).then_inc(s["context_turned"], 1)
                if at(0):
                    u, n, g = at(0)
                    pe.wait_ge(s["weighed"], u + 1)
                    until(pe, s["weights_t0"], u)
                    until(pe, s["weights_t1"], u)
                    for e in range(2):
                        for c in range(LC):
                            last = pe.transpose(weight_ps[0:LN, e, c * P:(c + 1) * P], weights[n % 2][:, e, c * LN:(c + 1) * LN], ident[:, :])
                    last.then_inc(s["weights_turned"], 1)
                if at(2):
                    u, n, g = at(2)
                    pe.wait_ge(s["keys_ready"], u + 1)
                    until(pe, s["keys_t_ready"], u)
                    until(pe, s["context_t_ready"], u - 3)
                    for c in range(LC):
                        last = pe.transpose(turn_ps[:, c * LN:(c + 1) * LN], keys[n][:, c, :, :].rearrange("p e d -> p (e d)"),
                                            ident[0:LN, 0:LN])
                    last.then_inc(s["keys_turned"], 1)
                if at(-2) and at(-2)[1] == BT - 1:
                    u, n, g = at(-2)
                    pe.wait_ge(s["context_t_ready"], u + 1)
                    pe.wait_ge(s["context_ready"], u + 1)
                    for a in range(NP):
                        last = pe.matmul(sum_ps[:, 0:D], context_t[:, a, :, :], omap[:, a, :], start=a == 0, stop=a == NP - 1)
                    last.then_inc(s["projected"], 1)
                if at(-1):
                    u, n, g = at(-1)
                    pe.wait_ge(s["weights_t0"], u + 1)
                    pe.wait_ge(s["weights_t1"], u + 1)
                    until(pe, s["context_ready"], u)
                    if n == 0:
                        until(pe, s["added"], g)
                    for e in range(2):
                        for c in range(LC):
                            last = pe.matmul(sum_ps[:, e * CD:(e + 1) * CD], weights_t[n % 2][:, e, c, :], keys[n][:, c, 0, :],
                                             start=c == 0, stop=c == LC - 1)
                    last.then_inc(s["summed"], 1)
            pe.wait_ge(s["padded"], 1)
            steps(pe, step, B, 4, 2, 2)

        @block.scalar
        def _(act):
            def step(at):
                if at(-2):
                    u, n, g = at(-2)
                    act.wait_ge(s["context_turned"], u + 1)
                    if n == 0:
                        until(act, s["projected"], g)
                    act.activation(context_t[:, :, n, :], turn_ps[:, 0:P].rearrange("p (a s) -> p a s", a=NP), ACT.Copy).then_inc(s["context_t_ready"], 1)
                if at(0):
                    u, n, g = at(0)
                    act.wait_ge(s["weights_turned"], u + 1)
                    until(act, s["summed"], u - 1)
                    act.activation(weights_t[n % 2][:, 0, :, :], weight_ps[0:LN, 0, 0:LC * P].rearrange("p (c q) -> p c q", c=LC), ACT.Copy).then_inc(s["weights_t0"], 1)
                if at(2):
                    u, n, g = at(2)
                    act.wait_ge(s["keys_turned"], u + 1)
                    until(act, s["scored"], u - 1)
                    act.activation(keys_t[n % 2][:, :], turn_ps[:, 0:LC * LN], ACT.Copy).then_inc(s["keys_t_ready"], 1)
                if at(1):
                    u, n, g = at(1)
                    act.wait_ge(s["peak_ready"], u + 1)
                    until(act, s["weights_turned"], u - 1)
                    until(act, s["inverted"], u - 1)
                    for e in range(2):
                        last = act.activation(weights[n % 2][:, e, 0:L], score_ps[n % 2][:, e, 0:L], ACT.Exp, bias=peak[:, n % 2, e:e + 1],
                                              accum_out=total[:, n % 2, e:e + 1])
                    last.then_inc(s["weighed"], 1)
            steps(act, step, B, 4, 2, 2)

        @block.vector
        def _(dve):
            for n in range(2):
                last = dve.memset(weights[n][:, :, L:LC * LN], 0.0)
            last.then_inc(s["padded"], 1)

            def step(at):
                if at(1):
                    u, n, g = at(1)
                    dve.wait_ge(s["scored"], u + 1)
                    until(dve, s["weighed"], u - 1)
                    dve.tensor_reduce(peak[:, n % 2, :], score_ps[n % 2][:, :, 0:L], X, ALU.max, negate=True).then_inc(s["peak_ready"], 1)
                if at(0):
                    u, n, g = at(0)
                    dve.wait_ge(s["weights_turned"], u + 1)
                    until(dve, s["summed"], u - 1)
                    dve.tensor_copy(weights_t[n % 2][:, 1, :, :], weight_ps[0:LN, 1, 0:LC * P].rearrange("p (c q) -> p c q", c=LC)).then_inc(s["weights_t1"], 1)
                if at(-1):
                    u, n, g = at(-1)
                    dve.wait_ge(s["weighed"], u + 1)
                    dve.reciprocal(inverse[:, n % 2, :], total[:, n % 2, :]).then_inc(s["inverted"], 1)
                if at(-2) and at(-2)[1] == BT - 1:
                    u, n, g = at(-2)
                    dve.wait_ge(s["projected"], g + 1)
                    dve.tensor_tensor(x_sb[:, g, :], sum_ps[:, 0:D], x_sb[:, g, :], ALU.add).then_inc(s["added"], 1)
                if at(-1):
                    u, n, g = at(-1)
                    dve.wait_ge(s["summed"], u + 1)
                    dve.wait_ge(s["inverted"], u + 1)
                    until(dve, s["context_turned"], u - 1)
                    dve.tensor_tensor(context[n % 2][:, :, :], sum_ps[:, 0:2 * CD].rearrange("p (e d) -> p e d", e=2),
                                      inverse[:, n % 2, :].unsqueeze(2).to_broadcast([P, 2, CD]), ALU.mult).then_inc(s["context_ready"], 1)
            steps(dve, step, B, 4, 1, 2)



def slot_attention(nc, sem, w, x_sb, mean, rstd, ident, mask, tag="s"):
    units = NT * NG
    with ExitStack() as ctx:
        def sb(name, shape):
            return ctx.enter_context(nc.sbuf_tensor(f"{tag}_{name}", shape, F32))

        def ring(name, n, shape):
            return [sb(f"{name}{k}", shape) for k in range(n)]

        def ps(name, shape):
            return ctx.enter_context(nc.psum_tensor(f"{tag}_{name}", shape, F32))

        GK, GM, GV = GH * DK, GH * M, GH * DV
        wq, wk, ws = sb("wq", [P, DC, AH * DK]), sb("wk", [P, DC, AH * DK]), sb("ws", [P, DC, AH * M])
        wv, wg = sb("wv", [P, DC, AH * DV]), sb("wg", [P, DC, AH * DV])
        wo, norm_w = sb("wo", [DV, AH, D]), sb("norm_w", [DV, 1])
        mask_q = sb("mask_q", [P, P])

        rows = sb("rows", [P, D])
        rows_t = sb("rows_t", [P, DC, P])
        qk = ring("qk", 2, [P, 2, 2, P])
        clipped = sb("clipped", [P, GM])
        slots = ring("slots", 2, [P, GM])
        slots_t = ring("slots_t", 2, [P, 2, P])
        values = ring("values", 4, [P, GV])
        tanh = sb("tanh", [P, GV])
        gate = ring("gate", 4, [P, GV])
        inv_z = ring("inv_z", 2, [P, GM])
        first = sb("first", [P, 2, 2, P])
        ok = sb("ok", [P, GM])
        shifted = sb("shifted", [P, GM])
        peak = sb("peak", [P, GH])
        prob = sb("prob", [P, GM])
        total = ring("total", 2, [P, GH])
        prob_z = sb("prob_z", [P, GM])
        prob_t = sb("prob_t", [P, 2, P])
        second = sb("second", [P, 2, 2, P])
        squares = sb("squares", [P, GV])
        square_sum, eps_sum, mean_sq, root = (sb(n, [P, GH]) for n in ("square_sum", "eps_sum", "mean_sq", "root"))
        minus_half = sb("power", [P, GH])
        heads = sb("heads", [P, GV])
        heads_t = ring("heads_t", 2, [P, GH, P])

        s_ps, qk_ps, vg_ps, out_ps = ps("s_ps", [P, 512]), ps("qk_ps", [P, 512]), ps("vg_ps", [P, 512]), ps("out_ps", [P, 512])
        pair_ps = ps("pair_ps", [P, 2, 512])
        slot_ps = ps("slot_ps", [P, 512])
        head_ps = ps("head_ps", [P, 512])

        names = ("loaded", "wo_loaded", "wo_scaled", "mask_ready", "power_ready",
                 "rows_ready", "rows_turned", "rows_t_ready", "s_done", "clipped_ready", "slots_ready",
                 "qk_done", "qk_ready", "v_done", "v_ready", "g_done", "tanh_ready", "gate_ready",
                 "z_done", "inv_z_ready", "first_done", "first_ready", "slots_turned", "slots_t_ready",
                 "ok_done", "ok_ready", "peak_ready", "shifted_ready", "prob_ready", "total_ready", "prob_z_ready",
                 "prob_turned", "prob_t_ready", "second_done", "second_ready", "head_done", "squared", "eps_ready",
                 "mean_sq_ready", "root_ready", "heads_ready", "heads_turned", "heads_t_ready", "projected", "added")
        s = {n: sem(f"{tag}_{n}") for n in names}
        block = ctx.enter_context(nc.Block())

        def upto(n):
            return min(n, units) if isinstance(n, int) else n

        def by_head(ap, width):
            return ap.rearrange("p (h k) -> p h k", k=width)

        def over(ap, width):
            return ap.unsqueeze(2).to_broadcast([P, GH, width])

        @block.sync
        def _(sp):
            for n, t in (("awq", wq), ("awk", wk), ("aws", ws), ("awv", wv), ("awg", wg)):
                sp.dma_start(t[:, :, :], w[n].rearrange("(c p) n -> p c n", p=P)).then_inc(s["loaded"], 16)
            sp.dma_start(wo[:, :, :], w["awo"].rearrange("(h v) n -> v h n", v=DV)).then_inc(s["wo_loaded"], 16)
            sp.dma_start(norm_w[:, :], w["norm_w"].rearrange("(v o) -> v o", o=1)).then_inc(s["wo_loaded"], 16)

        @block.gpsimd
        def _(pool):
            pool.memset(minus_half[:, :], -0.5).then_inc(s["power_ready"], 1)
            pool.wait_ge(s["power_ready"], 1)

            def step(at):
                if at(-1):
                    u, n, g = at(-1)
                    pool.wait_ge(s["prob_ready"], u + 1)
                    until(pool, s["prob_turned"], u)
                    pool.tensor_tensor(prob_z[:, :], prob[:, :], inv_z[n % 2][:, :], ALU.mult).then_inc(s["prob_z_ready"], 1)
                if at(-2):
                    u, n, g = at(-2)
                    pool.wait_ge(s["mean_sq_ready"], u + 1)
                    until(pool, s["heads_ready"], u)
                    pool.tensor_tensor(root[:, :], mean_sq[:, :], minus_half[:, :], ALU.pow).then_inc(s["root_ready"], 1)
            steps(pool, step, units, NG, 0, 2)

        @block.tensor
        def _(pe):
            pe.wait_ge(s["loaded"], 16 * 5)
            pe.wait_ge(s["wo_scaled"], 1)

            def step(at):
                if at(1):
                    u, n, g = at(1)
                    pe.wait_ge(s["rows_t_ready"], g + 1)
                    until(pe, s["inv_z_ready"], u - 1)
                    until(pe, s["clipped_ready"], u)
                    for c in range(DC):
                        last = pe.matmul(s_ps[:, 0:GM], rows_t[:, c, :], ws[:, c, n * GM:(n + 1) * GM], start=c == 0, stop=c == DC - 1)
                    last.then_inc(s["s_done"], 1)
                    until(pe, s["qk_ready"], u)
                    until(pe, s["heads_t_ready"], u - 3)
                    for a, weight in enumerate((wq, wk)):
                        for j in range(2):
                            for c in range(DC):
                                last = pe.matmul(qk_ps[:, (2 * a + j) * P:(2 * a + j + 1) * P],
                                                 weight[:, c, n * GK + j * P:n * GK + (j + 1) * P], rows_t[:, c, :],
                                                 start=c == 0, stop=c == DC - 1)
                    last.then_inc(s["qk_done"], 1)
                if at(-2):
                    u, n, g = at(-2)
                    pe.wait_ge(s["second_ready"], u + 1)
                    pe.wait_ge(s["v_ready"], u + 1)
                    until(pe, s["heads_ready"], u)
                    for h in range(GH):
                        last = pe.matmul(head_ps[:, h * DV:(h + 1) * DV], second[:, h % 2, h // 2, :],
                                         values[n][:, h * DV:(h + 1) * DV], start=True, stop=True)
                    last.then_inc(s["head_done"], 1)
                if at(0):
                    u, n, g = at(0)
                    pe.wait_ge(s["slots_ready"], u + 1)
                    pe.wait_ge(s["clipped_ready"], upto(u + 2))
                    until(pe, s["inv_z_ready"], u)
                    pe.matmul(s_ps[:, 256:256 + GM], mask[:, :], slots[n % 2][:, :], start=True, stop=True).then_inc(s["z_done"], 1)
                    pe.wait_ge(s["qk_ready"], u + 1)
                    until(pe, s["second_ready"], u - 1)
                    until(pe, s["first_ready"], u)
                    for j in range(2):
                        for e in range(2):
                            a = e * DK
                            last = pe.matmul(pair_ps[:, e, j * P:(j + 1) * P], qk[n % 2][a:a + DK, 1, j, :], qk[n % 2][a:a + DK, 0, j, :],
                                             start=True, stop=True)
                    last.then_inc(s["first_done"], 1)
                    until(pe, s["ok_ready"], u)
                    for j in range(2):
                        last = pe.transpose(slot_ps[:, j * P:(j + 1) * P], slots[n % 2][:, j * P:(j + 1) * P], ident[:, :])
                    last.then_inc(s["slots_turned"], 1)
                if at(1):
                    u, n, g = at(1)
                    until(pe, s["gate_ready"], u)
                    for c in range(DC):
                        last = pe.matmul(vg_ps[:, :], rows_t[:, c, :], wv[:, c, n * GV:(n + 1) * GV], start=c == 0, stop=c == DC - 1)
                    last.then_inc(s["v_done"], 1)
                if at(-1):
                    u, n, g = at(-1)
                    pe.wait_ge(s["prob_z_ready"], u + 1)
                    pe.wait_ge(s["slots_t_ready"], upto(u + 2))
                    for j in range(2):
                        last = pe.transpose(slot_ps[:, j * P:(j + 1) * P], prob_z[:, j * P:(j + 1) * P], ident[:, :])
                    last.then_inc(s["prob_turned"], 1)
                if at(1):
                    u, n, g = at(1)
                    pe.wait_ge(s["v_ready"], u + 1)
                    for c in range(DC):
                        last = pe.matmul(vg_ps[:, :], rows_t[:, c, :], wg[:, c, n * GV:(n + 1) * GV], start=c == 0, stop=c == DC - 1)
                    last.then_inc(s["g_done"], 1)
                if at(0):
                    u, n, g = at(0)
                    pe.wait_ge(s["first_ready"], u + 1)
                    pe.wait_ge(s["slots_t_ready"], u + 1)
                    until(pe, s["prob_t_ready"], u)
                    for h in range(GH):
                        last = pe.matmul(slot_ps[:, 256 + h * M:256 + (h + 1) * M], first[:, h % 2, h // 2, :],
                                         slots[n % 2][:, h * M:(h + 1) * M], start=True, stop=True)
                    last.then_inc(s["ok_done"], 1)
                if at(-1):
                    u, n, g = at(-1)
                    pe.wait_ge(s["prob_t_ready"], u + 1)
                    pe.wait_ge(s["first_ready"], upto(u + 2))
                    until(pe, s["second_ready"], u)
                    for j in range(2):
                        for e in range(2):
                            a = e * M
                            last = pe.matmul(pair_ps[:, e, j * P:(j + 1) * P], slots_t[n % 2][a:a + M, j, :], prob_t[a:a + M, j, :],
                                             start=True, stop=True)
                    last.then_inc(s["second_done"], 1)
                if at(-2):
                    u, n, g = at(-2)
                    pe.wait_ge(s["heads_ready"], u + 1)
                    pe.wait_ge(s["qk_ready"], upto(u + 4))
                    until(pe, s["heads_t_ready"], u)
                    for h in range(GH):
                        last = pe.transpose(qk_ps[:, h * P:(h + 1) * P], heads[:, h * DV:(h + 1) * DV], ident[:, :])
                    last.then_inc(s["heads_turned"], 1)
                if at(-3):
                    u, n, g = at(-3)
                    pe.wait_ge(s["heads_t_ready"], u + 1)
                    if n == 0:
                        until(pe, s["added"], g)
                    for h in range(GH):
                        last = pe.matmul(out_ps[:, 0:D], heads_t[n % 2][:, h, :], wo[:, n * GH + h, :],
                                         start=n == 0 and h == 0, stop=n == NG - 1 and h == GH - 1)
                    last.then_inc(s["projected"], 1)
                if at(2) and at(2)[1] == 0:
                    u, n, g = at(2)
                    pe.wait_ge(s["rows_ready"], g + 1)
                    until(pe, s["inv_z_ready"], u - 1)
                    for c in range(DC):
                        last = pe.transpose(s_ps[:, c * P:(c + 1) * P], rows[:, c * P:(c + 1) * P], ident[:, :])
                    last.then_inc(s["rows_turned"], 1)
            steps(pe, step, units, NG, 2, 3)

        @block.scalar
        def _(act):
            def step(at):
                if at(-1):
                    u, n, g = at(-1)
                    act.wait_ge(s["shifted_ready"], u + 1)
                    until(act, s["prob_z_ready"], u)
                    until(act, s["total_ready"], u)
                    act.activation(prob[:, :], shifted[:, :], ACT.Exp).then_inc(s["prob_ready"], 1)
                if at(1):
                    u, n, g = at(1)
                    act.wait_ge(s["qk_done"], u + 1)
                    until(act, s["first_done"], u - 1)
                    act.activation(qk[n % 2][:, :, :, :], qk_ps[:, :].rearrange("p (a j r) -> p a j r", a=2, j=2), ACT.Copy).then_inc(s["qk_ready"], 1)
                    act.wait_ge(s["clipped_ready"], u + 1)
                    until(act, s["ok_done"], u - 1)
                    act.activation(slots[n % 2][:, :], clipped[:, :], ACT.Exp).then_inc(s["slots_ready"], 1)
                if at(-2):
                    u, n, g = at(-2)
                    act.wait_ge(s["head_done"], u + 1)
                    until(act, s["mean_sq_ready"], u)
                    for h in range(GH):
                        last = act.activation(squares[:, h * DV:(h + 1) * DV], head_ps[:, h * DV:(h + 1) * DV], ACT.Square, accum_out=square_sum[:, h:h + 1])
                    last.then_inc(s["squared"], 1)
                if at(0):
                    u, n, g = at(0)
                    act.wait_ge(s["slots_turned"], u + 1)
                    until(act, s["second_done"], u - 1)
                    act.activation(slots_t[n % 2][:, :, :], slot_ps[:, 0:GM].rearrange("p (j r) -> p j r", j=2), ACT.Copy).then_inc(s["slots_t_ready"], 1)
                if at(1):
                    u, n, g = at(1)
                    act.wait_ge(s["v_done"], u + 1)
                    until(act, s["head_done"], u - 3)
                    act.activation(values[n][:, :], vg_ps[:, :], ACT.Copy).then_inc(s["v_ready"], 1)
                if at(-1):
                    u, n, g = at(-1)
                    act.wait_ge(s["prob_turned"], u + 1)
                    until(act, s["second_done"], u)
                    act.activation(prob_t[:, :, :], slot_ps[:, 0:GM].rearrange("p (j r) -> p j r", j=2), ACT.Copy).then_inc(s["prob_t_ready"], 1)
                if at(1):
                    u, n, g = at(1)
                    act.wait_ge(s["g_done"], u + 1)
                    until(act, s["gate_ready"], u)
                    act.activation(tanh[:, :], vg_ps[:, :], ACT.Tanh, scale=0.5).then_inc(s["tanh_ready"], 1)
                if at(-2):
                    u, n, g = at(-2)
                    act.wait_ge(s["heads_turned"], u + 1)
                    until(act, s["projected"], u - 1)
                    act.activation(heads_t[n % 2][:, :, :], qk_ps[:, :].rearrange("p (h r) -> p h r", h=GH), ACT.Copy).then_inc(s["heads_t_ready"], 1)
                if at(2) and at(2)[1] == 0:
                    u, n, g = at(2)
                    act.wait_ge(s["rows_turned"], g + 1)
                    act.activation(rows_t[:, :, :], s_ps[:, 0:D].rearrange("p (c r) -> p c r", c=DC), ACT.Copy).then_inc(s["rows_t_ready"], 1)
            steps(act, step, units, NG, 2, 2)

        @block.vector
        def _(dve):
            dve.tensor_scalar(mask_q[:, :], mask[:, :], float(DK) ** -0.5, None, ALU.mult).then_inc(s["mask_ready"], 1)
            dve.wait_ge(s["wo_loaded"], 32)
            dve.tensor_scalar(wo[:, :, :], wo[:, :, :], norm_w[:, 0:1], 0.5, ALU.mult, ALU.mult).then_inc(s["wo_scaled"], 1)
            dve.wait_ge(s["mask_ready"], 1)

            def step(at):
                if at(-1):
                    u, n, g = at(-1)
                    dve.wait_ge(s["ok_done"], u + 1)
                    dve.wait_ge(s["inv_z_ready"], u + 1)
                    until(dve, s["shifted_ready"], u)
                    dve.tensor_tensor(ok[:, :], slot_ps[:, 256:256 + GM], inv_z[n % 2][:, :], ALU.mult).then_inc(s["ok_ready"], 1)
                    dve.wait_ge(s["ok_ready"], u + 1)
                    dve.tensor_reduce(peak[:, :], by_head(ok[:, :], M), X, ALU.max).then_inc(s["peak_ready"], 1)
                    dve.wait_ge(s["peak_ready"], u + 1)
                    until(dve, s["prob_ready"], u)
                    dve.tensor_tensor(by_head(shifted[:, :], M), by_head(ok[:, :], M), over(peak[:, :], M), ALU.subtract).then_inc(s["shifted_ready"], 1)
                if at(1):
                    u, n, g = at(1)
                    dve.wait_ge(s["s_done"], u + 1)
                    until(dve, s["slots_ready"], u)
                    dve.tensor_scalar(clipped[:, :], s_ps[:, 0:GM], -32.0, 32.0, ALU.max, ALU.min).then_inc(s["clipped_ready"], 1)
                if at(-1):
                    u, n, g = at(-1)
                    dve.wait_ge(s["prob_ready"], u + 1)
                    dve.tensor_reduce(total[n % 2][:, :], by_head(prob[:, :], M), X, ALU.add).then_inc(s["total_ready"], 1)
                if at(-2):
                    u, n, g = at(-2)
                    dve.wait_ge(s["total_ready"], u + 1)
                    dve.scalar_tensor_tensor(eps_sum[:, :], total[n % 2][:, :], EPS, total[n % 2][:, :], ALU.mult, ALU.mult).then_inc(s["eps_ready"], 1)
                    dve.wait_ge(s["squared"], u + 1)
                    dve.wait_ge(s["eps_ready"], u + 1)
                    until(dve, s["root_ready"], u)
                    dve.scalar_tensor_tensor(mean_sq[:, :], square_sum[:, :], 1.0 / DV, eps_sum[:, :], ALU.mult, ALU.add).then_inc(s["mean_sq_ready"], 1)
                if at(0):
                    u, n, g = at(0)
                    dve.wait_ge(s["z_done"], u + 1)
                    until(dve, s["prob_z_ready"], u - 1)
                    dve.reciprocal(inv_z[n % 2][:, :], s_ps[:, 256:256 + GM]).then_inc(s["inv_z_ready"], 1)
                    dve.wait_ge(s["first_done"], u + 1)
                    until(dve, s["ok_done"], u)
                    dve.tensor_tensor(first[:, :, :, :], pair_ps[:, :, 0:2 * P].rearrange("p e (j r) -> p e j r", j=2),
                                      mask_q[:, :].unsqueeze(1).unsqueeze(1).to_broadcast([P, 2, 2, P]), ALU.mult).then_inc(s["first_ready"], 1)
                if at(-2):
                    u, n, g = at(-2)
                    dve.wait_ge(s["root_ready"], u + 1)
                    dve.wait_ge(s["gate_ready"], u + 1)
                    until(dve, s["heads_turned"], u)
                    for h in range(GH):
                        col = slice(h * DV, (h + 1) * DV)
                        last = dve.scalar_tensor_tensor(heads[:, col], head_ps[:, col], root[:, h:h + 1], gate[n][:, col], ALU.mult, ALU.mult)
                    last.then_inc(s["heads_ready"], 1)
                if at(1):
                    u, n, g = at(1)
                    dve.wait_ge(s["tanh_ready"], u + 1)
                    dve.scalar_tensor_tensor(gate[n][:, :], tanh[:, :], 1.0, vg_ps[:, :], ALU.add, ALU.mult).then_inc(s["gate_ready"], 1)
                if at(-1):
                    u, n, g = at(-1)
                    dve.wait_ge(s["second_done"], u + 1)
                    until(dve, s["head_done"], u)
                    dve.tensor_tensor(second[:, :, :, :], pair_ps[:, :, 0:2 * P].rearrange("p e (j r) -> p e j r", j=2),
                                      mask[:, :].unsqueeze(1).unsqueeze(1).to_broadcast([P, 2, 2, P]), ALU.mult).then_inc(s["second_ready"], 1)
                if at(-3) and at(-3)[1] == NG - 1:
                    u, n, g = at(-3)
                    dve.wait_ge(s["projected"], u + 1)
                    dve.tensor_tensor(x_sb[:, g, :], out_ps[:, 0:D], x_sb[:, g, :], ALU.add).then_inc(s["added"], 1)
                if at(3) and at(3)[1] == 0:
                    u, n, g = at(3)
                    until(dve, s["rows_turned"], g)
                    dve.tensor_scalar(rows[:, :], x_sb[:, g, :], mean[:, bass.ds(g, 1)], rstd[:, bass.ds(g, 1)],
                                      ALU.subtract, ALU.mult).then_inc(s["rows_ready"], 1)
            steps(dve, step, units, NG, 3, 3)



def route(nc, sem, w, rows_t, coef, mix, w1, w2, b1, ident, tag="r"):
    groups = NT // TG
    with ExitStack() as ctx:
        def sb(name, shape):
            return ctx.enter_context(nc.sbuf_tensor(f"{tag}_{name}", shape, F32))

        def ps(name, shape):
            return ctx.enter_context(nc.psum_tensor(f"{tag}_{name}", shape, F32))

        router_w, router_b, cost = sb("router_w", [P, DC, NE]), sb("router_b", [P, NE]), sb("cost", [P, NE])
        lower = sb("lower", [P, NE, NE])
        flat = [sb(f"flat{n}", [NE, TG, P]) for n in range(2)]
        logits, prob = sb("logits", [P, NT, NE]), sb("prob", [P, NT, NE])
        peak, total, inverse = (sb(n, [P, NT]) for n in ("peak", "total", "inverse"))
        above, same = sb("above", [P, NT, NE, NE]), sb("same", [P, NT, NE, NE])
        rank, is_first, is_second, picked = (sb(n, [P, NT, NE]) for n in ("rank", "is_first", "is_second", "picked"))
        p_first, p_second, gap, ratio, g_first, g_second = (
            sb(n, [P, NT]) for n in ("p_first", "p_second", "gap", "ratio", "g_first", "g_second"))
        b2 = sb("b2", [NE + 1, FL])
        b2_to = sb("b2_to", [NE + 1, NE + 2])
        gelu_b1 = sb("gelu_b1", [P, NCH])
        spread = sb("spread", [P, NCH, NE + 2])
        flat_ps = [ps(f"flat_ps{n}", [P, 512]) for n in range(2)]
        logit_ps = [ps(f"logit_ps{n}", [P, 512]) for n in range(2)]
        mix_ps = ps("mix_ps", [P, 512])

        names = ("loaded", "w1_loaded", "flat_done", "flat_ready", "logit_done", "logit_ready",
                 "w2_scaled", "chain", "shifted", "exp_done", "gap_ready", "ratio_done", "cleared", "gelu_done",
                 "spread_ready", "mix_done", "mix_ready")
        s = {n: sem(f"{tag}_{n}") for n in names}
        block = ctx.enter_context(nc.Block())
        shape4 = [P, NT, NE, NE]

        @block.sync
        def _(sp):
            sp.dma_start(router_w[:, :, :], w["router_w"].rearrange("(c p) e -> p c e", p=P)).then_inc(s["loaded"], 16)
            for t, n in ((router_b, "router_b"), (cost, "cost")):
                sp.dma_start(t[:, :], w[n].partition_broadcast(P)).then_inc(s["loaded"], 16)
            sp.dma_start(lower[:, :, :], w["lower"].partition_broadcast(P)).then_inc(s["loaded"], 16)
            sp.dma_start(b2[:, :], w["b2"]).then_inc(s["loaded"], 16)
            sp.dma_start(b2_to[:, :], w["b2_to"]).then_inc(s["loaded"], 16)
            sp.dma_start(b1[:, :], w["b1"]).then_inc(s["loaded"], 16)
            sp.dma_start(w2[:, :, :], w["w2"].rearrange("(n p) l -> p n l", p=P)).then_inc(s["loaded"], 16)
            sp.dma_start(w1[:, :, :], w["w1"].rearrange("p (n q) -> p n q", q=P)).then_inc(s["w1_loaded"], 16)
            sp.wait_ge(s["w1_loaded"], 16)

        @block.gpsimd
        def _(pool):
            pool.memset(spread[:, :, :], 0.0).then_inc(s["cleared"], 1)

        @block.tensor
        def _(pe):
            pe.wait_ge(s["loaded"], 16 * 8)

            def step(at):
                if at(0):
                    u, n, g = at(0)
                    until(pe, s["flat_ready"], u - 1)
                    for c in range(DC):
                        last = pe.matmul(flat_ps[n][0:NE, :], router_w[:, c, :], rows_t[:, c, bass.ds(u * TG * P, TG * P)],
                                         start=c == 0, stop=c == DC - 1)
                    last.then_inc(s["flat_done"], 1)
                if at(-1):
                    u, n, g = at(-1)
                    pe.wait_ge(s["flat_ready"], u + 1)
                    until(pe, s["logit_ready"], u - 1)
                    for k in range(TG):
                        last = pe.transpose(logit_ps[n][:, k * NE:(k + 1) * NE], flat[n][:, k, :], ident[0:NE, 0:NE])
                    last.then_inc(s["logit_done"], 1)
            steps(pe, step, groups, 2, 0, 1, loop=False)
            pe.wait_ge(s["spread_ready"], 1)
            pe.matmul(mix_ps[0:NE + 2, 0:FL], b2_to[:, :], b2[:, :], start=True, stop=False)
            for c in range(NCH):
                last = pe.matmul(mix_ps[0:NE + 2, 0:FL], spread[:, c, :], w2[:, c + 1, :], start=False, stop=c == NCH - 1)
            last.then_inc(s["mix_done"], 1)

        @block.scalar
        def _(act):
            def step(at):
                u, n, g = at(0)
                act.wait_ge(s["flat_done"], u + 1)
                until(act, s["logit_done"], u - 1)
                act.activation(flat[n][:, :, :], flat_ps[n][0:NE, :].rearrange("e (k r) -> e k r", k=TG), ACT.Copy).then_inc(s["flat_ready"], 1)
            steps(act, step, groups, 2, 0, 0, loop=False)
            act.wait_ge(s["shifted"], 1)
            act.activation(prob[:, :, :], logits[:, :, :], ACT.Exp).then_inc(s["exp_done"], 1)
            act.wait_ge(s["gap_ready"], 1)
            act.activation(ratio[:, :], gap[:, :], ACT.Exp).then_inc(s["ratio_done"], 1)
            act.activation(gelu_b1[:, :], b1[:, 1:NCH + 1], ACT.Gelu).then_inc(s["gelu_done"], 1)
            act.wait_ge(s["mix_done"], 1)
            act.activation(mix[:, :], mix_ps[0:NE + 2, 0:FL], ACT.Copy).then_inc(s["mix_ready"], 1)

        @block.vector
        def _(dve):
            link = [0]

            def then(ins):
                link[0] += 1
                ins.then_inc(s["chain"], 1)
                dve.wait_ge(s["chain"], link[0])

            dve.wait_ge(s["loaded"], 16 * 8)
            dve.tensor_scalar(w2[:, 0, :], w2[:, 0, :], 0.1, None, ALU.mult).then_inc(s["w2_scaled"], 1)
            then(dve.scalar_tensor_tensor(router_b[:, :], cost[:, :], -COST_LAMBDA, router_b[:, :], ALU.mult, ALU.add))

            def step(at):
                u, n, g = at(0)
                dve.wait_ge(s["logit_done"], u + 1)
                dve.tensor_tensor(logits[:, bass.ds(u * TG, TG), :], logit_ps[n][:, 0:TG * NE].rearrange("p (k e) -> p k e", e=NE),
                                  router_b[:, :].unsqueeze(1).to_broadcast([P, TG, NE]), ALU.add).then_inc(s["logit_ready"], 1)
            steps(dve, step, groups, 2, 0, 0, loop=False)
            dve.wait_ge(s["logit_ready"], groups)

            def each(ap):
                return ap.unsqueeze(2).to_broadcast([P, NT, NE])

            then(dve.tensor_reduce(peak[:, :], logits[:, :, :], X, ALU.max))
            dve.tensor_tensor(logits[:, :, :], logits[:, :, :], each(peak[:, :]), ALU.subtract).then_inc(s["shifted"], 1)
            dve.wait_ge(s["exp_done"], 1)
            then(dve.tensor_reduce(total[:, :], prob[:, :, :], X, ALU.add))
            then(dve.reciprocal(inverse[:, :], total[:, :]))
            then(dve.tensor_tensor(prob[:, :, :], prob[:, :, :], each(inverse[:, :]), ALU.mult))
            mine = prob[:, :, :].unsqueeze(3).to_broadcast(shape4)
            other = prob[:, :, :].unsqueeze(2).to_broadcast(shape4)
            dve.tensor_tensor(above[:, :, :, :], other, mine, ALU.is_gt)
            then(dve.tensor_tensor(same[:, :, :, :], other, mine, ALU.is_equal))
            then(dve.tensor_tensor(same[:, :, :, :], same[:, :, :, :], lower[:, :, :].unsqueeze(1).to_broadcast(shape4), ALU.mult))
            then(dve.tensor_tensor(above[:, :, :, :], above[:, :, :, :], same[:, :, :, :], ALU.add))
            then(dve.tensor_reduce(rank[:, :, :], above[:, :, :, :], X, ALU.add))
            dve.tensor_scalar(is_first[:, :, :], rank[:, :, :], 0.0, None, ALU.is_equal)
            then(dve.tensor_scalar(is_second[:, :, :], rank[:, :, :], 1.0, None, ALU.is_equal))
            then(dve.tensor_tensor(picked[:, :, :], prob[:, :, :], is_first[:, :, :], ALU.mult))
            then(dve.tensor_reduce(p_first[:, :], picked[:, :, :], X, ALU.add))
            then(dve.tensor_tensor(picked[:, :, :], prob[:, :, :], is_second[:, :, :], ALU.mult))
            then(dve.tensor_reduce(p_second[:, :], picked[:, :, :], X, ALU.add))
            dve.tensor_tensor(gap[:, :], p_second[:, :], p_first[:, :], ALU.subtract).then_inc(s["gap_ready"], 1)
            dve.wait_ge(s["ratio_done"], 1)
            then(dve.tensor_scalar(total[:, :], ratio[:, :], 1.0, None, ALU.add))
            then(dve.reciprocal(g_first[:, :], total[:, :]))
            then(dve.tensor_tensor(g_second[:, :], ratio[:, :], g_first[:, :], ALU.mult))
            dve.tensor_tensor(is_first[:, :, :], is_first[:, :, :], each(g_first[:, :]), ALU.mult)
            dve.tensor_tensor(is_second[:, :, :], is_second[:, :, :], each(g_second[:, :]), ALU.mult)
            dve.memset(coef[:, :, NE + 1], 0.1)
            then(dve.tensor_tensor(coef[:, :, NE], g_first[:, :], g_second[:, :], ALU.add))
            then(dve.tensor_tensor(coef[:, :, 0:NE], is_first[:, :, :], is_second[:, :, :], ALU.add))
            dve.wait_ge(s["gelu_done"], 1)
            dve.wait_ge(s["cleared"], 1)
            for c in range(NCH):
                e = CHUNK_EXPERT[c]
                dve.tensor_scalar(spread[:, c, e:e + 1], gelu_b1[:, c:c + 1], -1.0, None, ALU.mult)
            dve.tensor_copy(spread[:, :, NE], gelu_b1[:, :]).then_inc(s["spread_ready"], 1)



def experts(nc, sem, w, out, x_sb, rows_t, coef, mix, w1, w2, b1, ident, tag="e"):
    CH = NCH + 1
    TR = TG * P
    units = NT // TG * CH
    NEX = NE + 1
    owner = [0] + [e + 1 for e in CHUNK_EXPERT]
    opens = [n == 0 or owner[n] != owner[n - 1] for n in range(CH)]
    closes = [n == CH - 1 or owner[n] != owner[n + 1] for n in range(CH)]
    NY = 3
    with ExitStack() as ctx:
        def sb(name, shape):
            return ctx.enter_context(nc.sbuf_tensor(f"{tag}_{name}", shape, F32))

        def ps(name):
            return ctx.enter_context(nc.psum_tensor(f"{tag}_{name}", [P, 512], F32))

        bias, bias2 = sb("bias", [P, D]), sb("bias2", [P, D])
        down_w, down_b = sb("down_w", [P, DC, FL]), sb("down_b", [P, 1])
        core_w, up_w = sb("core_w", [P, DC, D]), sb("up_w", [P, D])
        gelu_h = sb("gelu_h", [P, TR])
        hidden = [sb(f"hidden{k}", [P, TR]) for k in range(3)]
        gelu_x = sb("gelu_x", [P, DC, TR])
        coef_now = sb("coef_now", [P, TG, NE + 2])
        coef_t = sb("coef_t", [NE + 2, TG, P])
        acc, acc_t = sb("acc", [P, TG, FL]), sb("acc_t", [P, TG, P])
        hidden_ps = [ps(f"hidden_ps{k}") for k in range(2)]
        y_ps = [ps(f"y_ps{k}") for k in range(NY)]
        h_ps, turn_ps, out_ps = ps("h_ps"), ps("turn_ps"), ps("out_ps")

        names = ("loaded", "bias_loaded", "bias_ready", "bias_added", "h_done", "gelu_h_ready", "hidden_done", "hidden_ready", "y_chunk", "y_done", "y_added", "gelu_x_ready",
                 "coef_ready", "coef_turned", "coef_t_ready", "acc_turned", "acc_t_ready", "out_done", "x_ready", "stored")
        s = {n: sem(f"{tag}_{n}") for n in names}
        block = ctx.enter_context(nc.Block())
        out_rows = out.rearrange("b s d -> (b s) d").rearrange("(g k p) d -> g p k d", k=TG, p=P)
        assert CH % 3 == 0 and NEX % NY == 0

        @block.sync
        def _(sp):
            sp.dma_start(down_w[:, :, :], w["down_w"].rearrange("(c p) n -> p c n", p=P)).then_inc(s["loaded"], 16)
            sp.dma_start(core_w[:, :, :], w["core_w"].rearrange("(c p) n -> p c n", p=P)).then_inc(s["loaded"], 16)
            sp.dma_start(up_w[:, :], w["up_w"]).then_inc(s["loaded"], 16)
            sp.dma_start(down_b[:, :], w["down_b"].rearrange("(p o) -> p o", o=1)).then_inc(s["loaded"], 16)
            sp.dma_start(bias[:, :], w["core_b"].partition_broadcast(P)).then_inc(s["bias_loaded"], 16)
            sp.dma_start(bias2[:, :], w["up_b"].partition_broadcast(P)).then_inc(s["bias_loaded"], 16)

            def step(at):
                u, n, g = at(0)
                sp.wait_ge(s["x_ready"], 2 * (u + 1))
                sp.dma_start(out_rows[u], x_sb[:, bass.ds(u * TG, TG), :]).then_inc(s["stored"], 16)
            steps(sp, step, NT // TG, 2, 0, 0)
            sp.wait_ge(s["stored"], 16 * NT // TG)

        @block.gpsimd
        def _(pool):
            pool.wait_ge(s["bias_loaded"], 32)
            pool.tensor_tensor(bias[:, :], bias[:, :], bias2[:, :], ALU.add).then_inc(s["bias_ready"], 1)
            pool.wait_ge(s["bias_ready"], 1)
            pool.tensor_tensor(x_sb[:, :, :], x_sb[:, :, :], bias[:, :].unsqueeze(1).to_broadcast([P, NT, D]), ALU.add).then_inc(s["bias_added"], 1)

        @block.tensor
        def _(pe):
            pe.wait_ge(s["loaded"], 64)

            def step(at):
                if at(0):
                    u, n, g = at(0)
                    e = owner[n]
                    y = y_ps[e % NY]
                    pe.wait_ge(s["hidden_ready"], u + 1)
                    if opens[n]:
                        until(pe, s["y_added"], g * NEX + e - NY + 1)
                    if n == 0:
                        pe.wait_ge(s["coef_t_ready"], g + 1)
                    for k in range(TG):
                        last = pe.matmul(y[:, k * FL:(k + 1) * FL], hidden[n % 3][:, k * P:(k + 1) * P], w2[:, n, :],
                                         start=opens[n] and k == 0, stop=closes[n] and n > 0, skip_group_check=True)
                    if n == 0:
                        for k in range(TG):
                            last = pe.matmul(y[:, k * FL:(k + 1) * FL], coef_t[:, k, :], mix[:, :], start=False, stop=True,
                                             skip_group_check=True)
                    last.then_inc(s["y_chunk"], 1)
                if at(-1) and at(-1)[1] == CH - 1:
                    u, n, g = at(-1)
                    pe.wait_ge(s["y_added"], (g + 1) * NEX)
                    until(pe, s["coef_t_ready"], min(g + 2, NT // TG) if isinstance(g, int) else g + 2)
                    for k in range(TG):
                        last = pe.transpose(turn_ps[:, k * P:(k + 1) * P], acc[:, k, :], ident[:, :])
                    last.then_inc(s["acc_turned"], 1)
                if at(2):
                    u, n, g = at(2)
                    if n == 0:
                        pe.wait_ge(s["gelu_h_ready"], g + 1)
                    until(pe, s["hidden_ready"], u - 1 if n else u)
                    pe.matmul(hidden_ps[n % 2][:, :], w1[:, n, :], gelu_h[:, :], start=True, stop=True).then_inc(s["hidden_done"], 1)
                if at(-2) and at(-2)[1] == CH - 1:
                    u, n, g = at(-2)
                    pe.wait_ge(s["acc_t_ready"], g + 1)
                    pe.wait_ge(s["gelu_x_ready"], g + 1)
                    for r in range(2):
                        until(pe, s["x_ready"], 2 * g + r)
                        for q in range(2):
                            k = 2 * r + q
                            for c in range(DC):
                                pe.matmul(out_ps[:, q * D:(q + 1) * D], gelu_x[:, c, k * P:(k + 1) * P], core_w[:, c, :],
                                          start=c == 0, stop=False)
                            last = pe.matmul(out_ps[:, q * D:(q + 1) * D], acc_t[:, k, :], up_w[:, :], start=False, stop=True)
                        last.then_inc(s["out_done"], 1)
                if at(4) and at(4)[1] == 0:
                    u, n, g = at(4)
                    until(pe, s["gelu_h_ready"], g)
                    for c in range(DC):
                        last = pe.matmul(h_ps[:, :], down_w[:, c, :], rows_t[:, c, bass.ds(g * TR, TR)], start=c == 0, stop=c == DC - 1)
                    last.then_inc(s["h_done"], 1)
                if at(6) and at(6)[1] == 0:
                    u, n, g = at(6)
                    pe.wait_ge(s["coef_ready"], g + 1)
                    until(pe, s["acc_t_ready"], g - 1)
                    until(pe, s["coef_t_ready"], g)
                    for k in range(TG):
                        last = pe.transpose(turn_ps[0:NE + 2, k * P:(k + 1) * P], coef_now[:, k, :], ident[:, :])
                    last.then_inc(s["coef_turned"], 1)

            steps(pe, step, units, CH, 6, 2)

        @block.scalar
        def _(act):
            act.wait_ge(s["loaded"], 64)

            def step(at):
                if at(3) and at(3)[1] == 0:
                    u, n, g = at(3)
                    act.wait_ge(s["h_done"], g + 1)
                    until(act, s["hidden_done"], u)
                    act.activation(gelu_h[:, :], h_ps[:, :], ACT.Gelu, bias=down_b[:, 0:1]).then_inc(s["gelu_h_ready"], 1)
                if at(2):
                    u, n, g = at(2)
                    act.wait_ge(s["hidden_done"], u + 1)
                    until(act, s["y_chunk"], u - 2)
                    act.activation(hidden[n % 3][:, :], hidden_ps[n % 2][:, :], ACT.Gelu, bias=b1[:, n:n + 1]).then_inc(s["hidden_ready"], 1)
                if at(0) and at(0)[1] == 6:
                    u, n, g = at(0)
                    until(act, s["out_done"], 2 * g)
                    for c in range(DC):
                        last = act.activation(gelu_x[:, c, :], rows_t[:, c, bass.ds(g * TR, TR)], ACT.Gelu)
                    last.then_inc(s["gelu_x_ready"], 1)
            steps(act, step, units, CH, 3, 0)

        @block.vector
        def _(dve):
            dve.wait_ge(s["bias_added"], 1)

            def step(at):
                if at(0) and closes[at(0)[1]]:
                    u, n, g = at(0)
                    e = owner[n]
                    y = y_ps[e % NY][:, :].rearrange("p (k l) -> p k l", k=TG)
                    dve.wait_ge(s["y_chunk"], u + 1)
                    if e == 0:
                        until(dve, s["acc_turned"], g)
                        dve.tensor_copy(acc[:, :, :], y).then_inc(s["y_added"], 1)
                    else:
                        dve.wait_ge(s["y_added"], g * NEX + e)
                        for k in range(TG):
                            last = dve.scalar_tensor_tensor(acc[:, k, :], y[:, k, :], coef[:, g * TG + k, e - 1:e], acc[:, k, :],
                                                            ALU.mult, ALU.add)
                        last.then_inc(s["y_added"], 1)
                if at(-1) and at(-1)[1] == CH - 1:
                    u, n, g = at(-1)
                    dve.wait_ge(s["acc_turned"], g + 1)
                    until(dve, s["out_done"], 2 * g)
                    dve.tensor_copy(acc_t[:, :, :], turn_ps[:, :].rearrange("p (k r) -> p k r", k=TG)).then_inc(s["acc_t_ready"], 1)
                if at(-2) and at(-2)[1] == CH - 1:
                    u, n, g = at(-2)
                    for r in range(2):
                        dve.wait_ge(s["out_done"], 2 * g + r + 1)
                        rows = x_sb[:, bass.ds(g * TG + 2 * r, 2), :]
                        dve.tensor_tensor(rows, out_ps[:, :].rearrange("p (k d) -> p k d", k=2), rows, ALU.add).then_inc(s["x_ready"], 1)
                if at(8) and at(8)[1] == 0:
                    u, n, g = at(8)
                    until(dve, s["coef_turned"], g)
                    dve.tensor_scalar(coef_now[:, :, :], coef[:, bass.ds(g * TG, TG), :], 1.0, None, ALU.mult).then_inc(s["coef_ready"], 1)
                if at(5) and at(5)[1] == 0:
                    u, n, g = at(5)
                    dve.wait_ge(s["coef_turned"], g + 1)
                    until(dve, s["y_chunk"], g * CH - CH + 1)
                    dve.tensor_copy(coef_t[:, :, :], turn_ps[0:NE + 2, :].rearrange("p (k r) -> p k r", k=TG)).then_inc(s["coef_t_ready"], 1)
            steps(dve, step, units, CH, 8, 2)



CONSTANTS = {
    "ident": [P, P], "mask": [P, P], "minus_half": [P, NT],
    "cos_k": [LN, LC, CD], "sin_k": [LN, LC, CD], "cos_q": [QC, 2, S], "sin_q": [QC, 2, S],
}


def perceiver_block(nc, w, out):
    with ExitStack() as ctx:
        taken = []

        def sem(name):
            taken.append(nc.alloc_semaphore(name))
            return taken[-1]

        def semaphores_end():
            nc.clear_and_free_semaphores(taken)
            nc.all_engine_barrier()
            taken.clear()

        x_sb = ctx.enter_context(nc.sbuf_tensor("x_sb", [P, NT, D], F32))
        mean = ctx.enter_context(nc.sbuf_tensor("mean", [P, NT], F32))
        rstd = ctx.enter_context(nc.sbuf_tensor("rstd", [P, NT], F32))
        const = {n: ctx.enter_context(nc.sbuf_tensor(n, shape, F32)) for n, shape in CONSTANTS.items()}
        ident, minus_half = const["ident"], const["minus_half"]

        x_loaded, const_loaded = sem("x_loaded"), sem("const_loaded")
        with nc.Block() as block:
            @block.sync
            def _(sp):
                rows = w["x"].rearrange("b s d -> (b s) d").rearrange("(i p) d -> p i d", p=P)
                for j in range(4):
                    q = NT // 4
                    sp.dma_start(x_sb[:, j * q:(j + 1) * q, :], rows[:, j * q:(j + 1) * q, :]).then_inc(x_loaded, 16)
                sp.wait_ge(x_loaded, 64)

            @block.scalar
            def _(act):
                for n, shape in CONSTANTS.items():
                    act.dma_start(const[n][:], w[n]).then_inc(const_loaded, 16)
                act.wait_ge(const_loaded, 16 * len(CONSTANTS))

        row_statistics(nc, sem, x_sb, mean, rstd, minus_half, "n1")
        with ExitStack() as one:
            def sb(name, shape):
                return one.enter_context(nc.sbuf_tensor(name, shape, F32))

            xnt = sb("xnt", [P, DC, S, B])
            queries = sb("queries", [P, NP, S, B])
            qmap, gmap, omap = sb("qmap", [QC, 2, HH, D]), sb("gmap", [QC, 2, HH, CD]), sb("omap", [P, NP, D])
            transposed_rows(nc, sem, x_sb, mean, rstd, ident,
                            lambda i: xnt[:, :, :, bass.ds(i * BT, BT)].rearrange("p c s b -> p c b s"), "t1")
            for hh in range(2):
                fold_weights(nc, sem, w, hh, qmap, gmap, omap, f"f{hh}")
                make_queries(nc, sem, qmap, gmap, const["cos_q"], const["sin_q"], xnt, queries, f"q{hh}")
                attend(nc, sem, w, x_sb, queries, omap, const["cos_k"], const["sin_k"], ident, f"a{hh}")

        semaphores_end()
        row_statistics(nc, sem, x_sb, mean, rstd, minus_half, "n2")
        slot_attention(nc, sem, w, x_sb, mean, rstd, ident, const["mask"])

        semaphores_end()
        row_statistics(nc, sem, x_sb, mean, rstd, minus_half, "n3")
        with ExitStack() as three:
            def sb(name, shape):
                return three.enter_context(nc.sbuf_tensor(name, shape, F32))

            rows_t = sb("rows_t", [P, DC, ROWS])
            coef, mix = sb("coef", [P, NT, NE + 2]), sb("mix", [NE + 2, FL])
            w1, w2, b1 = sb("w1", [P, NCH + 1, P]), sb("w2", [P, NCH + 1, FL]), sb("b1", [P, NCH + 1])
            transposed_rows(nc, sem, x_sb, mean, rstd, ident,
                            lambda i: rows_t[:, :, bass.ds(i * P, P)].rearrange("p c (b s) -> p c b s", b=BT), "t3")
            route(nc, sem, w, rows_t, coef, mix, w1, w2, b1, ident)
            experts(nc, sem, w, out, x_sb, rows_t, coef, mix, w1, w2, b1, ident)



def constants():
    f32 = np.float32

    def tables(length, dim):
        inv = f32(1.0) / np.power(f32(10000.0), np.arange(0, dim, 2, dtype=f32) / f32(dim))
        f = np.arange(length, dtype=f32)[:, None] * inv[None, :].astype(f32)
        return np.repeat(np.sin(f), 2, axis=-1), np.repeat(np.cos(f), 2, axis=-1)

    row = np.arange(P)
    sin_k, cos_k = (np.concatenate([a[:L], np.zeros((LC * LN - L, CD), f32)]).reshape(LC, LN, CD).transpose(1, 0, 2)
                    for a in tables(L, CD))
    sign = np.where(np.arange(CD) < CD // 2, f32(-1), f32(1))
    sin_q, cos_q = (a.reshape(S, 2, QC).transpose(2, 1, 0) for a in tables(S, CQ))
    out = {
        "ident": np.eye(P), "minus_half": np.full((P, NT), -0.5),
        "mask": (row[:, None] // S == row[None, :] // S) & (row[:, None] <= row[None, :]),
        "cos_k": cos_k, "sin_k": sin_k * sign, "cos_q": cos_q,
        "cost": [2 * FL * h for h in HID],
        "lower": np.tril(np.ones((NE, NE)), -1),
        "b2_to": [[float(k == NE + (e == NE)) for k in range(NE + 2)] for e in range(NE + 1)],
        "sin_q": np.stack([sin_q[:, 1], -sin_q[:, 0]], axis=1),
    }
    return {n: np.ascontiguousarray(a, dtype=f32) for n, a in out.items()}


def lay_out(i):
    names = ["shared"] + [f"e{e}" for e in range(NE)]
    return {
        "x": i["x"], "ctx": i["ctx_512"],
        "wq": i["L0_xattn_Wq"], "wkq": i["L0_xattn_w_kc_q"], "wkv": i["L0_xattn_w_kc_kv"],
        "wqr_t": i["L0_xattn_W_qr"].transpose(0, 2, 1), "wkr_t": i["L0_xattn_W_kr"].transpose(0, 2, 1),
        "xwo_t": i["L0_xattn_Wo"].T,
        "awq": i["L0_attn_Wq"], "awk": i["L0_attn_Wk"], "aws": i["L0_attn_Ws"], "awv": i["L0_attn_Wv"],
        "awg": i["L0_attn_Wg"], "awo": i["L0_attn_Wo"], "norm_w": i["L0_attn_g_norm_weight"],
        **{n: i[f"L0_ffn_{n}"] for n in ("router_w", "router_b", "down_w", "down_b", "core_w", "core_b", "up_w", "up_b")},
        "w1": np.concatenate([i[f"L0_ffn_{e}_w1"] for e in names], axis=1),
        "b1": np.concatenate([i[f"L0_ffn_{e}_b1"] for e in names]).reshape(-1, P).T,
        "w2": np.concatenate([i[f"L0_ffn_{e}_w2"] for e in names]),
        "b2": np.stack([i[f"L0_ffn_{e}_b2"] for e in names[1:] + names[:1]]),
    }


def kernel(**inputs):
    import concourse.bacc as bacc
    from concourse.bass_utils import run_bass_kernel_spmd

    nc = bacc.Bacc("TRN2", target_bir_lowering=False, num_devices=1)
    inputs = {n: np.asarray(a) for n, a in inputs.items()}
    arrays, w = {}, {}
    for name, a in {**lay_out(inputs), **constants()}.items():
        arrays[f"in_{name}"] = np.ascontiguousarray(a)
        w[name] = nc.dram_tensor(f"in_{name}", a.shape, F32, kind="ExternalInput").ap()
    out = nc.dram_tensor("out", [B, S, D], F32, kind="ExternalOutput").ap()
    perceiver_block(nc, w, out)
    r = run_bass_kernel_spmd(nc, [arrays], core_ids=[0])
    return r.results[0]["out"]
```

```python
from contextlib import ExitStack

import numpy as np

import concourse.bass as bass
from concourse import mybir

F32 = mybir.dt.float32
F32R = mybir.dt.float32r
ALU = mybir.AluOpType
ACT = mybir.ActivationFunctionType
X = mybir.AxisListType.X

P = 128
B, S, D = 128, 32, 256
ROWS = B * S
NT = ROWS // P
BT = P // S
DC = D // P
EPS = 1e-5

L, H, HK, CD, CQ, R = 257, 16, 128, 64, 192, 64
QC = CQ // 2
HH = H // 2
NP = HH // 2
LC, LN = 3, 86
SG = 4

AH, DK, DV, M = 16, 64, 128, 64
GH = 4
NG = AH // GH

HID = [128, 256, 384, 512, 128, 256, 384, 512]
NE = len(HID)
FL = 128
NCH = sum(HID) // P
CHUNK_EXPERT = [e for e, h in enumerate(HID) for _ in range(h // P)]
TG = 4
COST_LAMBDA = 1e-07


def until(eng, sem, count):
    if not (isinstance(count, int) and count <= 0):
        eng.wait_ge(sem, count)


def steps(eng, step, units, group, lead, lag, loop=True):
    assert lead <= group and lag <= group and units % group == 0

    def offset(t, b, i):
        def at(o):
            u = t + o
            if isinstance(u, int) and not 0 <= u < units:
                return None
            return u, (b + o) % group, i + (b + o) // group
        return at

    if not loop:
        for t in range(-lead, units + lag):
            step(offset(t, t % group, t // group))
        return
    for t in range(-lead, group):
        step(offset(t, t % group, t // group))
    with eng.Fori(1, units // group - 1) as i:
        for b in range(group):
            step(offset(i * group + b, b, i))
    for t in range(units - group, units + lag):
        step(offset(t, t % group, t // group))



def row_statistics(sem, block, ctx, nc, stats, mean, rstd, half, tag, x_sb=None, x_loaded=()):
    diff = ctx.enter_context(nc.sbuf_tensor(f"{tag}_diff", [P, NT], F32))
    var = ctx.enter_context(nc.sbuf_tensor(f"{tag}_var", [P, NT], F32))
    stats_done, step_done, var_done, rstd_done = (
        sem(f"{tag}_stats_done"), sem(f"{tag}_step_done"), sem(f"{tag}_var_done"), sem(f"{tag}_rstd_done"))

    @block.vector
    def _(dve):
        if x_sb is not None:
            part = NT // len(x_loaded)
            for i in range(NT):
                if i % part == 0:
                    dve.wait_ge(x_loaded[i // part], 16)
                dve.bn_stats(stats[:, i, :], x_sb[:, i, :]).then_inc(stats_done, 1)
            dve.wait_ge(stats_done, NT)
        dve.tensor_tensor(mean[:, :], stats[:, :, 1], stats[:, :, 4], ALU.add).then_inc(step_done, 1)
        dve.tensor_tensor(diff[:, :], stats[:, :, 1], stats[:, :, 4], ALU.subtract).then_inc(step_done, 1)
        dve.tensor_tensor(var[:, :], stats[:, :, 2], stats[:, :, 5], ALU.add).then_inc(step_done, 1)
        dve.wait_ge(step_done, 3)
        dve.tensor_scalar(mean[:, :], mean[:, :], 0.5, None, ALU.mult).then_inc(step_done, 1)
        dve.scalar_tensor_tensor(diff[:, :], diff[:, :], 0.25, diff[:, :], ALU.mult, ALU.mult).then_inc(step_done, 1)
        dve.tensor_scalar(var[:, :], var[:, :], 1.0 / D, EPS, ALU.mult, ALU.add).then_inc(step_done, 1)
        dve.wait_ge(step_done, 6)
        dve.tensor_tensor(var[:, :], var[:, :], diff[:, :], ALU.add).then_inc(var_done, 1)

    @block.gpsimd
    def _(pool):
        pool.wait_ge(var_done, 1)
        pool.tensor_tensor(rstd[:, :], var[:, :], half[:, 0:NT], ALU.pow).then_inc(rstd_done, 1)


def transposed_rows(nc, sem, x_sb, mean, rstd, ident, place, tag):
    RING = 4
    with ExitStack() as ctx:
        xn = ctx.enter_context(nc.sbuf_tensor(f"{tag}_xn", [P, RING, D], F32))
        turned = ctx.enter_context(nc.psum_tensor(f"{tag}_turned", [P, RING, 512], F32))
        xn_ready, turn_done, place_done = sem(f"{tag}_xn_ready"), sem(f"{tag}_turn_done"), sem(f"{tag}_place_done")
        block = ctx.enter_context(nc.Block())

        @block.vector
        def _(dve):
            def step(at):
                i, b, _ = at(0)
                until(dve, turn_done, i - RING + 1)
                dve.tensor_scalar(xn[:, b, :], x_sb[:, i, :], mean[:, bass.ds(i, 1)], rstd[:, bass.ds(i, 1)],
                                  ALU.subtract, ALU.mult).then_inc(xn_ready, 1)
            steps(dve, step, NT, RING, 0, 0)

        @block.tensor
        def _(pe):
            def step(at):
                i, b, _ = at(0)
                until(pe, xn_ready, i + 1)
                until(pe, place_done, i - RING + 1)
                for c in range(DC):
                    last = pe.transpose(turned[:, b, c * P:(c + 1) * P], xn[:, b, c * P:(c + 1) * P], ident[:, :])
                last.then_inc(turn_done, 1)
            steps(pe, step, NT, RING, 0, 0)

        @block.scalar
        def _(act):
            def step(at):
                i, b, _ = at(0)
                until(act, turn_done, i + 1)
                act.activation(place(i), turned[:, b, 0:D].rearrange("p (c b s) -> p c b s", c=DC, b=BT),
                               ACT.Copy).then_inc(place_done, 1)
            steps(act, step, NT, RING, 0, 0)



def fold_weights(nc, sem, w, hh, qmap, gmap, omap, tag, beside=None):
    with ExitStack() as ctx:
        def sb(name, shape):
            return ctx.enter_context(nc.sbuf_tensor(f"{tag}_{name}", shape, F32))

        def banks(name):
            return [ctx.enter_context(nc.psum_tensor(f"{tag}_{name}{k}", [P, 512], F32)) for k in range(2)]

        wq, wkq, wkv, wo = sb("wq", [P, HH, D]), sb("wkq", [P, HH, CQ]), sb("wkv", [P, HH, CD]), sb("wo", [P, HH, D])
        wqr, wkr = sb("wqr", [R, HH, CQ]), sb("wkr", [R, HH, CD])
        q_ps, g_ps, o_ps = banks("q_ps"), banks("g_ps"), banks("o_ps")
        loaded = [sem(f"{tag}_{n}_loaded") for n in ("q", "g", "o")]
        product_done, q_copied, g_copied, o_copied = (
            sem(f"{tag}_product_done"), sem(f"{tag}_q_copied"), sem(f"{tag}_g_copied"), sem(f"{tag}_o_copied"))
        block = ctx.enter_context(nc.Block())
        h0 = hh * HH

        @block.sync
        def _(sp):
            sp.dma_start(wq[:, :, :], w["wq"][h0 * HK:(h0 + HH) * HK, :].rearrange("(h k) d -> k h d", k=HK)).then_inc(loaded[0], 16)
            sp.dma_start(wkq[:, :, :], w["wkq"][h0:h0 + HH].rearrange("h k q -> k h q")).then_inc(loaded[0], 16)
            sp.dma_start(wqr[:, :, :], w["wqr_t"][h0:h0 + HH].rearrange("h r q -> r h q")).then_inc(loaded[1], 16)
            sp.dma_start(wkr[:, :, :], w["wkr_t"][h0:h0 + HH].rearrange("h r d -> r h d")).then_inc(loaded[1], 16)
            sp.dma_start(wkv[:, :, :], w["wkv"][h0:h0 + HH].rearrange("h k d -> k h d")).then_inc(loaded[2], 16)
            sp.dma_start(wo[:, :, :], w["xwo_t"][h0 * HK:(h0 + HH) * HK, :].rearrange("(h k) d -> k h d", k=HK)).then_inc(loaded[2], 16)

        @block.tensor
        def _(pe):
            pe.wait_ge(loaded[0], 32)
            for h in range(HH):
                n = h % 2
                until(pe, q_copied, h - 1)
                for c in range(2):
                    last = pe.matmul(q_ps[n][0:QC, c * D:(c + 1) * D], wkq[:, h, c * QC:(c + 1) * QC], wq[:, h, :],
                                     start=True, stop=True)
                last.then_inc(product_done, 1)
                if h == 0:
                    pe.wait_ge(loaded[1], 32)
                    pe.wait_ge(loaded[2], 32)
                until(pe, g_copied, h - 1)
                for c in range(2):
                    last = pe.matmul(g_ps[n][0:QC, c * CD:(c + 1) * CD], wqr[:, h, c * QC:(c + 1) * QC], wkr[:, h, :],
                                     start=True, stop=True)
                last.then_inc(product_done, 1)
                e = h % 2 * CD
                until(pe, o_copied, h - 1)
                pe.matmul(o_ps[n][e:e + CD, 0:D], wkv[:, h, :], wo[:, h, :], start=True, stop=True).then_inc(product_done, 1)

        @block.scalar
        def _(act):
            for h in range(HH):
                n, e = h % 2, h % 2 * CD
                act.wait_ge(product_done, 3 * h + 1)
                act.activation(qmap[:, :, h, :], q_ps[n][0:QC, :].rearrange("p (c d) -> p c d", c=2), ACT.Copy).then_inc(q_copied, 1)
                act.wait_ge(product_done, 3 * h + 2)
                act.activation(gmap[:, :, h, :], g_ps[n][0:QC, 0:2 * CD].rearrange("p (c d) -> p c d", c=2), ACT.Copy).then_inc(g_copied, 1)
                act.wait_ge(product_done, 3 * h + 3)
                act.activation(omap[e:e + CD, h // 2, :], o_ps[n][e:e + CD, 0:D], ACT.Copy).then_inc(o_copied, 1)

        if beside:
            beside(block, ctx)


def make_queries(nc, sem, qmap, gmap, cos_q, sin_q, xnt, queries, tag):
    units = S // SG * NP
    with ExitStack() as ctx:
        def sb(name, shape):
            return ctx.enter_context(nc.sbuf_tensor(f"{tag}_{name}", shape, F32))

        turned = [sb(f"turned{n}", [QC, 2, 2, SG, CD]) for n in range(2)]
        maps = [sb(f"maps{n}", [P, DC, SG, 2, CD]) for n in range(2)]
        map_ps = [ctx.enter_context(nc.psum_tensor(f"{tag}_map_ps{n}", [P, DC, SG, CD], F32)) for n in range(2)]
        query_ps = [ctx.enter_context(nc.psum_tensor(f"{tag}_query_ps{n}", [P, SG, B], F32)) for n in range(2)]
        cos_done, turned_ready = sem(f"{tag}_cos_done"), sem(f"{tag}_turned_ready")
        map_done = [sem(f"{tag}_map_done{n}") for n in range(2)]
        map_copied = [sem(f"{tag}_map_copied{n}") for n in range(2)]
        query_done, query_copied = sem(f"{tag}_query_done"), sem(f"{tag}_query_copied")
        block = ctx.enter_context(nc.Block())

        @block.scalar
        def _(act):
            def step(at):
                if at(2):
                    u, n, g = at(2)
                    for k in range(2):
                        for s in range(SG):
                            s_at = g * SG + s
                            last = act.activation(turned[n % 2][:, k, :, s, :], gmap[:, k, 2 * n:2 * n + 2, :], ACT.Copy,
                                                  scale=cos_q[:, k, bass.ds(s_at, 1)])
                    last.then_inc(cos_done, 1)
                if at(1):
                    u, n, g = at(1)
                    act.wait_ge(map_done[1], u + 1)
                    until(act, query_done, u - 1)
                    act.activation(maps[n % 2][:, :, :, 0, :], map_ps[0][:, :, :, :], ACT.Copy).then_inc(map_copied[0], 1)
            steps(act, step, units, NP, 2, 0)

        @block.vector
        def _(dve):
            def step(at):
                if at(2):
                    u, n, g = at(2)
                    dve.wait_ge(cos_done, u + 1)
                    for k in range(2):
                        for s in range(SG):
                            s_at = g * SG + s
                            out = turned[n % 2][:, k, :, s, :]
                            last = dve.scalar_tensor_tensor(out, gmap[:, 1 - k, 2 * n:2 * n + 2, :], sin_q[:, k, bass.ds(s_at, 1)],
                                                            out, ALU.mult, ALU.add)
                    last.then_inc(turned_ready, 1)
                if at(1):
                    u, n, g = at(1)
                    dve.wait_ge(map_done[1], u + 1)
                    until(dve, query_done, u - 1)
                    dve.tensor_copy(maps[n % 2][:, :, :, 1, :], map_ps[1][:, :, :, :]).then_inc(map_copied[1], 1)
                if at(0):
                    u, n, g = at(0)
                    dve.wait_ge(query_done, u + 1)
                    s_at = g * SG
                    dve.tensor_copy(queries[:, n, bass.ds(s_at, SG), :], query_ps[n % 2][:, :, :]).then_inc(query_copied, 1)
            steps(dve, step, units, NP, 2, 0)

        @block.tensor
        def _(pe):
            def step(at):
                if at(1):
                    u, n, g = at(1)
                    pe.wait_ge(turned_ready, u + 1)
                    for e in range(2):
                        until(pe, map_copied[e], u)
                        for m in range(DC):
                            for k in range(2):
                                last = pe.matmul(map_ps[e][:, m, :, :], qmap[:, k, 2 * n + e, m * P:(m + 1) * P],
                                                 turned[n % 2][:, k, e, :, :], start=k == 0, stop=k == 1)
                        last.then_inc(map_done[e], 1)
                if at(0):
                    u, n, g = at(0)
                    for e in range(2):
                        pe.wait_ge(map_copied[e], u + 1)
                    until(pe, query_copied, u - 1)
                    for s in range(SG):
                        s_at = g * SG + s
                        for m in range(DC):
                            last = pe.matmul(query_ps[n % 2][:, s, :], maps[n % 2][:, m, s, :, :],
                                             xnt[:, m, bass.ds(s_at, 1), :], start=m == 0, stop=m == DC - 1)
                    last.then_inc(query_done, 1)
            steps(pe, step, units, NP, 1, 0)


def attend(nc, sem, w, x_sb, queries, omap, cos_k, sin_k, ident, tag, stats=None, ahead=()):
    with ExitStack() as ctx:
        def sb(name, shape):
            return ctx.enter_context(nc.sbuf_tensor(f"{tag}_{name}", shape, F32))

        def ps(name, shape):
            return ctx.enter_context(nc.psum_tensor(f"{tag}_{name}", shape, F32))

        raw = [sb(f"raw{n}", [LN, LC, CD]) for n in range(4)]
        swap = sb("swap", [LN, LC, CD])
        direct = sb("direct", [LN, LC, CD])
        keys = [sb(f"keys{n}", [P, LC, 2, CD]) for n in range(4)]
        keys_t = [sb(f"keys_t{n}", [P, LC * LN]) for n in range(2)]
        query = [sb(f"query{n}", [P, 2, NP * S]) for n in range(2)]
        peak = sb("peak", [P, 2, 2])
        total = sb("total", [P, 2, 2])
        inverse = sb("inverse", [P, 2, 2])
        weights = [sb(f"weights{n}", [P, 2, LC * LN]) for n in range(2)]
        weights_t = [sb(f"weights_t{n}", [P, 2, LC, P]) for n in range(2)]
        context = [sb(f"context{n}", [P, 2, CD]) for n in range(2)]
        context_t = sb("context_t", [P, NP, BT, S])

        turn_ps = ps("turn_ps", [P, 512])
        score_ps = [ps(f"score_ps{n}", [P, 2, 512]) for n in range(2)]
        project_ps = score_ps[1][:, :, 512 - P:512]
        weight_ps = ps("weight_ps", [P, 2, 512])
        sum_ps = ps("sum_ps", [P, 512])

        raw_loaded = [sem(f"{tag}_raw_loaded{n}") for n in range(4)]
        names = ("cleared", "rows_cleared", "query1_ready", "product", "swapped", "keys_ready", "query_ready", "keys_turned", "keys_t_ready", "scored", "peak_ready",
                 "padded", "weighed", "weights_turned", "weights_t0", "weights_t1", "summed", "inverted", "context_ready",
                 "context_turned", "context_t_ready", "projected", "added", "stats_done", "ahead_loaded")
        s = {n: sem(f"{tag}_{n}") for n in names}
        block = ctx.enter_context(nc.Block())

        @block.sync
        def _(sp):
            sp.wait_ge(s["cleared"], 1)
            def step(at):
                if at(4):
                    u, n, g = at(4)
                    until(sp, s["product"], u - 3)
                    until(sp, s["swapped"], u - 3)
                    full = (LC - 1) * LN
                    kv = w["ctx"][bass.ds(u, 1), :, :]
                    sp.dma_start(raw[n][:, 0:LC - 1, :], kv[:, 0:full, :].rearrange("o (c p) d -> p (o c) d", p=LN)).then_inc(raw_loaded[n], 16)
                    sp.dma_start(raw[n][0:L - full, LC - 1, :], kv[:, full:L, :].rearrange("o p d -> p (o d)")).then_inc(raw_loaded[n], 16)
            for to, source in ahead:
                sp.dma_start(to, source).then_inc(s["ahead_loaded"], 16)
            steps(sp, step, B, 4, 4, 0)
            until(sp, s["ahead_loaded"], 16 * len(ahead))

        @block.gpsimd
        def _(pool):
            for n in range(4):
                last = pool.memset(raw[n][:, LC - 1, :], 0.0)
            last.then_inc(s["cleared"], 1)
            for t in keys + query:
                last = pool.memset(t[:, :, :, :] if t in keys else t[:, :, :], 0.0)
            last.then_inc(s["rows_cleared"], 1)
            pool.wait_ge(s["rows_cleared"], 1)

            def step(at):
                if at(3):
                    u, n, g = at(3)
                    pool.wait_ge(raw_loaded[n], g * 32 + 32)
                    until(pool, s["keys_ready"], u)
                    h = CD // 2
                    pool.tensor_tensor(direct[:, :, :], raw[n][:, :, :], cos_k[:, :, :], ALU.mult).then_inc(s["product"], 1)
                    pool.tensor_tensor(swap[:, :, 0:h], raw[n][:, :, h:CD], sin_k[:, :, 0:h], ALU.mult)
                    pool.tensor_tensor(swap[:, :, h:CD], raw[n][:, :, 0:h], sin_k[:, :, h:CD], ALU.mult).then_inc(s["swapped"], 1)
                if at(2):
                    u, n, g = at(2)
                    until(pool, s["scored"], u - 1)
                    pool.tensor_copy(query[n % 2][0:CD, 0, :].rearrange("p (a s) -> p a s", a=NP),
                                     queries[0:CD, :, :, bass.ds(u, 1)].rearrange("p a s o -> p a (s o)")).then_inc(s["query_ready"], 1)
                if at(3):
                    u, n, g = at(3)
                    pool.wait_ge(s["product"], u + 1)
                    pool.wait_ge(s["swapped"], u + 1)
                    until(pool, s["summed"], u - 3)
                    for e in range(2):
                        last = pool.tensor_tensor(keys[n][0:LN, :, e, :], direct[:, :, :], swap[:, :, :], ALU.add)
                    last.then_inc(s["keys_ready"], 1)
            steps(pool, step, B, 4, 3, 0)

        @block.tensor
        def _(pe):
            def step(at):
                if at(1):
                    u, n, g = at(1)
                    pe.wait_ge(s["keys_t_ready"], u + 1)
                    pe.wait_ge(s["query_ready"], u + 1)
                    pe.wait_ge(s["query1_ready"], u + 1)
                    until(pe, s["weighed"], u - 1)
                    if n == BT - 1:
                        until(pe, s["added"], g)
                    for e in range(2):
                        last = pe.matmul(score_ps[n % 2][:, e, 0:L], query[n % 2][:, e, :], keys_t[n % 2][:, 0:L],
                                         start=True, stop=True)
                    last.then_inc(s["scored"], 1)
                if at(-2):
                    u, n, g = at(-2)
                    pe.wait_ge(s["context_ready"], u + 1)
                    pe.wait_ge(s["keys_t_ready"], min(u + 4, B) if isinstance(u, int) else u + 4)
                    until(pe, s["context_t_ready"], u)
                    pe.transpose(turn_ps[:, 0:P], context[n % 2][:, :, :].rearrange("p e d -> p (e d)"), ident[:, :]).then_inc(s["context_turned"], 1)
                if at(0):
                    u, n, g = at(0)
                    pe.wait_ge(s["weighed"], u + 1)
                    until(pe, s["weights_t0"], u)
                    until(pe, s["weights_t1"], u)
                    for e in range(2):
                        for c in range(LC):
                            last = pe.transpose(weight_ps[0:LN, e, c * P:(c + 1) * P], weights[n % 2][:, e, c * LN:(c + 1) * LN], ident[:, :])
                    last.then_inc(s["weights_turned"], 1)
                if at(2):
                    u, n, g = at(2)
                    pe.wait_ge(s["keys_ready"], u + 1)
                    until(pe, s["keys_t_ready"], u)
                    until(pe, s["context_t_ready"], u - 3)
                    for c in range(LC):
                        last = pe.transpose(turn_ps[:, c * LN:(c + 1) * LN], keys[n][0:LN, c, :, :].rearrange("p e d -> p (e d)"),
                                            ident[0:LN, 0:LN])
                    last.then_inc(s["keys_turned"], 1)
                if at(-2) and at(-2)[1] == BT - 1:
                    u, n, g = at(-2)
                    pe.wait_ge(s["context_t_ready"], u + 1)
                    pe.wait_ge(s["weighed"], min(u + 3, B) if isinstance(u, int) else u + 3)
                    for c in range(DC):
                        for a in range(NP):
                            last = pe.matmul(project_ps[:, c, :], context_t[:, a, :, :], omap[:, a, c * P:(c + 1) * P],
                                             start=a == 0, stop=a == NP - 1)
                    last.then_inc(s["projected"], 1)
                if at(-1):
                    u, n, g = at(-1)
                    pe.wait_ge(s["weights_t0"], u + 1)
                    pe.wait_ge(s["weights_t1"], u + 1)
                    until(pe, s["context_ready"], u)
                    for e in range(2):
                        for c in range(LC):
                            last = pe.matmul(sum_ps[:, e * CD:(e + 1) * CD], weights_t[n % 2][:, e, c, :], keys[n][:, c, 0, :],
                                             start=c == 0, stop=c == LC - 1)
                    last.then_inc(s["summed"], 1)
            pe.wait_ge(s["padded"], 1)
            pe.wait_ge(s["rows_cleared"], 1)
            steps(pe, step, B, 4, 2, 2)

        @block.scalar
        def _(act):
            act.wait_ge(s["padded"], 1)

            def step(at):
                if at(-2):
                    u, n, g = at(-2)
                    act.wait_ge(s["context_turned"], u + 1)
                    if n == 0:
                        until(act, s["projected"], g)
                    act.activation(context_t[:, :, n, :], turn_ps[:, 0:P].rearrange("p (a s) -> p a s", a=NP), ACT.Copy).then_inc(s["context_t_ready"], 1)
                if at(0):
                    u, n, g = at(0)
                    act.wait_ge(s["weights_turned"], u + 1)
                    until(act, s["summed"], u - 1)
                    act.activation(weights_t[n % 2][0:LN, 0, :, :], weight_ps[0:LN, 0, 0:LC * P].rearrange("p (c q) -> p c q", c=LC), ACT.Copy).then_inc(s["weights_t0"], 1)
                if at(2):
                    u, n, g = at(2)
                    act.wait_ge(s["keys_turned"], u + 1)
                    until(act, s["scored"], u - 1)
                    act.activation(keys_t[n % 2][:, :], turn_ps[:, 0:LC * LN], ACT.Copy).then_inc(s["keys_t_ready"], 1)
                if at(1):
                    u, n, g = at(1)
                    act.wait_ge(s["peak_ready"], u + 1)
                    until(act, s["weights_turned"], u - 1)
                    until(act, s["inverted"], u - 1)
                    for e in range(2):
                        last = act.activation(weights[n % 2][:, e, 0:L], score_ps[n % 2][:, e, 0:L], ACT.Exp, bias=peak[:, n % 2, e:e + 1],
                                              accum_out=total[:, n % 2, e:e + 1])
                    last.then_inc(s["weighed"], 1)
            steps(act, step, B, 4, 2, 2)

        @block.vector
        def _(dve):
            for n in range(2):
                dve.memset(weights_t[n][:, :, :, :], 0.0)
                last = dve.memset(weights[n][:, :, L:LC * LN], 0.0)
            last.then_inc(s["padded"], 1)
            dve.wait_ge(s["padded"], 1)
            dve.wait_ge(s["rows_cleared"], 1)

            def step(at):
                if at(1):
                    u, n, g = at(1)
                    dve.wait_ge(s["scored"], u + 1)
                    until(dve, s["weighed"], u - 1)
                    dve.tensor_reduce(peak[:, n % 2, :], score_ps[n % 2][:, :, 0:L], X, ALU.max, negate=True).then_inc(s["peak_ready"], 1)
                if at(0):
                    u, n, g = at(0)
                    dve.wait_ge(s["weights_turned"], u + 1)
                    until(dve, s["summed"], u - 1)
                    dve.tensor_copy(weights_t[n % 2][0:LN, 1, :, :], weight_ps[0:LN, 1, 0:LC * P].rearrange("p (c q) -> p c q", c=LC)).then_inc(s["weights_t1"], 1)
                if at(2):
                    u, n, g = at(2)
                    until(dve, s["scored"], u - 1)
                    dve.tensor_scalar(query[n % 2][CD:P, 1, :].rearrange("p (a s) -> p a s", a=NP),
                                      queries[CD:P, :, :, bass.ds(u, 1)].rearrange("p a s o -> p a (s o)"),
                                      1.0, None, ALU.mult).then_inc(s["query1_ready"], 1)
                if at(-1):
                    u, n, g = at(-1)
                    dve.wait_ge(s["weighed"], u + 1)
                    dve.reciprocal(inverse[:, n % 2, :], total[:, n % 2, :]).then_inc(s["inverted"], 1)
                if at(-2) and at(-2)[1] == BT - 1:
                    u, n, g = at(-2)
                    dve.wait_ge(s["projected"], g + 1)
                    rows = x_sb[:, g, :].rearrange("p (c d) -> p c d", c=DC)
                    dve.tensor_tensor(rows, project_ps, rows, ALU.add).then_inc(s["added"], 1)
                    if stats is not None:
                        dve.wait_ge(s["added"], g + 1)
                if at(-1):
                    u, n, g = at(-1)
                    dve.wait_ge(s["summed"], u + 1)
                    dve.wait_ge(s["inverted"], u + 1)
                    until(dve, s["context_turned"], u - 1)
                    dve.tensor_tensor(context[n % 2][:, :, :], sum_ps[:, 0:2 * CD].rearrange("p (e d) -> p e d", e=2),
                                      inverse[:, n % 2, :].unsqueeze(2).to_broadcast([P, 2, CD]), ALU.mult).then_inc(s["context_ready"], 1)
                if stats is not None and at(-2) and at(-2)[1] == BT - 1:
                    u, n, g = at(-2)
                    dve.bn_stats(stats[:, g, :], x_sb[:, g, :]).then_inc(s["stats_done"], 1)
            steps(dve, step, B, 4, 2, 2)



def split_weights(sem, block, ctx, nc, w, raw, wo_split, norm_w, tag):
    wo = ctx.enter_context(nc.sbuf_tensor(f"{tag}_wo", [DV, AH, D], F32))
    scaled = ctx.enter_context(nc.sbuf_tensor(f"{tag}_norm_w", [DV, 1], F32))
    wo_loaded, wo_scaled = sem(f"{tag}_wo_loaded"), sem(f"{tag}_wo_scaled")
    high_ready, low_ready = sem(f"{tag}_high_ready"), sem(f"{tag}_low_ready")
    parts = raw + [(wo, wo_split)]

    @block.sync
    def _(sp):
        sp.dma_start(wo[:, :, :], w["awo"].rearrange("(h v) n -> v h n", v=DV)).then_inc(wo_loaded, 16)
        sp.dma_start(scaled[:, :], norm_w.rearrange("(v o) -> v o", o=1)).then_inc(wo_loaded, 16)

    @block.gpsimd
    def _(pool):
        pool.wait_ge(wo_loaded, 32)
        pool.tensor_scalar(wo[:, :, :], wo[:, :, :], scaled[:, 0:1], 0.5, ALU.mult, ALU.mult).then_inc(wo_scaled, 1)

    @block.scalar
    def _(act):
        for k, (full, (high, low)) in enumerate(parts):
            if k == len(raw):
                act.wait_ge(wo_scaled, 1)
            act.activation(high[:, :, :], full[:, :, :], ACT.Copy).then_inc(high_ready, 1)

    @block.vector
    def _(dve):
        for k, (full, (high, low)) in enumerate(parts):
            dve.wait_ge(high_ready, k + 1)
            dve.tensor_tensor(low[:, :, :], full[:, :, :], high[:, :, :].bitcast(F32), ALU.subtract).then_inc(low_ready, 1)


def slot_attention(nc, sem, w, x_sb, mean, rstd, ident, mask, weights, wide, stats, tag="s"):
    units = NT * NG
    with ExitStack() as ctx:
        def sb(name, shape):
            return ctx.enter_context(nc.sbuf_tensor(f"{tag}_{name}", shape, F32))

        def ring(name, n, shape):
            return [sb(f"{name}{k}", shape) for k in range(n)]

        def ps(name, shape):
            return ctx.enter_context(nc.psum_tensor(f"{tag}_{name}", shape, F32))

        GK, GM, GV = GH * DK, GH * M, GH * DV
        wq, wk, ws, wv, wg, wo = weights
        mask_q = sb("mask_q", [P, P])

        used = [0]

        def carve(count):
            used[0] += count
            return [wide[:, k * GV:(k + 1) * GV] for k in range(used[0] - count, used[0])]

        values, gate = carve(4), carve(4)
        qk = [t.rearrange("p (a j r) -> p a j r", a=2, j=2) for t in carve(2)]
        tanh, squares, heads = carve(3)
        first, second = (t.rearrange("p (e j r) -> p e j r", e=2, j=2) for t in carve(2))

        rows = sb("rows", [P, D])
        rows_t = sb("rows_t", [P, DC, P])
        rows_high, rows_low = (ctx.enter_context(nc.sbuf_tensor(f"{tag}_rows_{n}", [P, DC, P], F32R)) for n in ("high", "low"))
        slots = ring("slots", 2, [P, GM])
        slots_t = ring("slots_t", 2, [P, 2, P])
        inv_z = ring("inv_z", 2, [P, GM])
        ok = sb("ok", [P, GM])
        peak = sb("peak", [P, GH])
        prob = sb("prob", [P, GM])
        total = ring("total", 2, [P, GH])
        prob_z = sb("prob_z", [P, GM])
        prob_t = sb("prob_t", [P, 2, P])
        square_sum, eps_sum, mean_sq, root = (sb(n, [P, GH]) for n in ("square_sum", "eps_sum", "mean_sq", "root"))
        minus_half = sb("power", [P, GH])
        heads_high, heads_low = (ctx.enter_context(nc.sbuf_tensor(f"{tag}_heads_{n}", [P, GH, P], F32R)) for n in ("high", "low"))

        s_ps, qk_ps, vg_ps, out_ps = ps("s_ps", [P, 512]), ps("qk_ps", [P, 512]), ps("vg_ps", [P, 512]), ps("out_ps", [P, 512])
        pair_ps = ps("pair_ps", [P, 2, 512])
        slot_ps = ps("slot_ps", [P, 512])
        head_ps = ps("head_ps", [P, 512])

        names = ("stats_done", "rows_high_ready", "rows_low_ready", "heads_high_ready", "heads_low_ready", "mask_ready", "power_ready",
                 "rows_ready", "rows_turned", "rows_t_ready", "s_done", "clipped_ready", "slots_ready",
                 "qk_done", "qk_ready", "v_done", "v_ready", "g_done", "tanh_ready", "gate_ready",
                 "z_done", "inv_z_ready", "first_done", "first_ready", "slots_turned", "slots_t_ready",
                 "ok_done", "ok_ready", "peak_ready", "shifted_ready", "prob_ready", "total_ready", "prob_z_ready",
                 "prob_turned", "prob_t_ready", "second_done", "second_ready", "head_done", "squared", "eps_ready",
                 "mean_sq_ready", "root_ready", "heads_ready", "heads_turned", "heads_t_ready", "projected", "added")
        s = {n: sem(f"{tag}_{n}") for n in names}
        block = ctx.enter_context(nc.Block())

        def upto(n):
            return min(n, units) if isinstance(n, int) else n

        def by_head(ap, width):
            return ap.rearrange("p (h k) -> p h k", k=width)

        def over(ap, width):
            return ap.unsqueeze(2).to_broadcast([P, GH, width])

        def split_product(pe, out, stationary, moving, start, stop):
            (high, low), (moving_high, moving_low) = stationary, moving
            pe.matmul(out, high, moving_low, start=start, stop=False)
            pe.matmul(out, low, moving_high, start=False, stop=False)
            return pe.matmul(out, high, moving_high, start=False, stop=stop)

        @block.gpsimd
        def _(pool):
            pool.memset(minus_half[:, :], -0.5).then_inc(s["power_ready"], 1)
            pool.wait_ge(s["power_ready"], 1)

            def step(at):
                if at(-1):
                    u, n, g = at(-1)
                    pool.wait_ge(s["prob_ready"], u + 1)
                    until(pool, s["prob_turned"], u)
                    pool.tensor_tensor(prob_z[:, :], prob[:, :], inv_z[n % 2][:, :], ALU.mult).then_inc(s["prob_z_ready"], 1)
                if at(-2):
                    u, n, g = at(-2)
                    pool.wait_ge(s["mean_sq_ready"], u + 1)
                    until(pool, s["heads_ready"], u)
                    pool.tensor_tensor(root[:, :], mean_sq[:, :], minus_half[:, :], ALU.pow).then_inc(s["root_ready"], 1)
                if at(2) and at(2)[1] == 0:
                    u, n, g = at(2)
                    pool.wait_ge(s["rows_t_ready"], g + 1)
                    pool.wait_ge(s["rows_high_ready"], g + 1)
                    pool.tensor_tensor(rows_low[:, :, :], rows_t[:, :, :], rows_high[:, :, :].bitcast(F32), ALU.subtract).then_inc(s["rows_low_ready"], 1)
            steps(pool, step, units, NG, 2, 2)

        @block.tensor
        def _(pe):
            def step(at):
                if at(1):
                    u, n, g = at(1)
                    pe.wait_ge(s["rows_t_ready"], g + 1)
                    pe.wait_ge(s["rows_high_ready"], g + 1)
                    until(pe, s["inv_z_ready"], u - 1)
                    until(pe, s["clipped_ready"], u)
                    for c in range(DC):
                        last = pe.matmul(s_ps[:, 0:GM], rows_t[:, c, :], ws[:, c, n * GM:(n + 1) * GM], start=c == 0, stop=c == DC - 1)
                    last.then_inc(s["s_done"], 1)
                    until(pe, s["qk_ready"], u)
                    until(pe, s["heads_high_ready"], u - 3)
                    until(pe, s["heads_low_ready"], u - 3)
                    for a, weight in enumerate((wq, wk)):
                        for j in range(2):
                            for c in range(DC):
                                last = pe.matmul(qk_ps[:, (2 * a + j) * P:(2 * a + j + 1) * P],
                                                 weight[:, c, n * GK + j * P:n * GK + (j + 1) * P], rows_t[:, c, :],
                                                 start=c == 0, stop=c == DC - 1)
                    last.then_inc(s["qk_done"], 1)
                if at(-2):
                    u, n, g = at(-2)
                    pe.wait_ge(s["second_ready"], u + 1)
                    pe.wait_ge(s["v_ready"], u + 1)
                    until(pe, s["heads_ready"], u)
                    for h in range(GH):
                        last = pe.matmul(head_ps[:, h * DV:(h + 1) * DV], second[:, h % 2, h // 2, :],
                                         values[n][:, h * DV:(h + 1) * DV], start=True, stop=True)
                    last.then_inc(s["head_done"], 1)
                if at(0):
                    u, n, g = at(0)
                    pe.wait_ge(s["slots_ready"], u + 1)
                    pe.wait_ge(s["clipped_ready"], upto(u + 2))
                    until(pe, s["inv_z_ready"], u)
                    pe.matmul(s_ps[:, 256:256 + GM], mask[:, :], slots[n % 2][:, :], start=True, stop=True).then_inc(s["z_done"], 1)
                    pe.wait_ge(s["qk_ready"], u + 1)
                    until(pe, s["second_ready"], u - 1)
                    until(pe, s["first_ready"], u)
                    for j in range(2):
                        for e in range(2):
                            a = e * DK
                            last = pe.matmul(pair_ps[:, e, j * P:(j + 1) * P], qk[n % 2][a:a + DK, 1, j, :], qk[n % 2][a:a + DK, 0, j, :],
                                             start=True, stop=True)
                    last.then_inc(s["first_done"], 1)
                    until(pe, s["ok_ready"], u)
                    for j in range(2):
                        last = pe.transpose(slot_ps[:, j * P:(j + 1) * P], slots[n % 2][:, j * P:(j + 1) * P], ident[:, :])
                    last.then_inc(s["slots_turned"], 1)
                if at(1):
                    u, n, g = at(1)
                    until(pe, s["gate_ready"], u)
                    pe.wait_ge(s["rows_low_ready"], g + 1)
                    for c in range(DC):
                        last = split_product(pe, vg_ps[:, :], (rows_high[:, c, :], rows_low[:, c, :]),
                                             [half[:, c, n * GV:(n + 1) * GV] for half in wv], c == 0, c == DC - 1)
                    last.then_inc(s["v_done"], 1)
                if at(-1):
                    u, n, g = at(-1)
                    pe.wait_ge(s["prob_z_ready"], u + 1)
                    pe.wait_ge(s["slots_t_ready"], upto(u + 2))
                    for j in range(2):
                        last = pe.transpose(slot_ps[:, j * P:(j + 1) * P], prob_z[:, j * P:(j + 1) * P], ident[:, :])
                    last.then_inc(s["prob_turned"], 1)
                if at(-3):
                    u, n, g = at(-3)
                    pe.wait_ge(s["heads_high_ready"], u + 1)
                    pe.wait_ge(s["heads_low_ready"], u + 1)
                    if n == 0:
                        until(pe, s["added"], g)
                    for h in range(GH):
                        last = split_product(pe, out_ps[:, 0:D], (heads_high[:, h, :], heads_low[:, h, :]),
                                             [half[:, n * GH + h, :] for half in wo], n == 0 and h == 0, n == NG - 1 and h == GH - 1)
                    last.then_inc(s["projected"], 1)
                if at(0):
                    u, n, g = at(0)
                    pe.wait_ge(s["first_ready"], u + 1)
                    pe.wait_ge(s["slots_t_ready"], u + 1)
                    until(pe, s["prob_t_ready"], u)
                    for h in range(GH):
                        last = pe.matmul(slot_ps[:, 256 + h * M:256 + (h + 1) * M], first[:, h % 2, h // 2, :],
                                         slots[n % 2][:, h * M:(h + 1) * M], start=True, stop=True)
                    last.then_inc(s["ok_done"], 1)
                if at(1):
                    u, n, g = at(1)
                    pe.wait_ge(s["v_ready"], u + 1)
                    for c in range(DC):
                        last = split_product(pe, vg_ps[:, :], (rows_high[:, c, :], rows_low[:, c, :]),
                                             [half[:, c, n * GV:(n + 1) * GV] for half in wg], c == 0, c == DC - 1)
                    last.then_inc(s["g_done"], 1)
                if at(2) and at(2)[1] == 0:
                    u, n, g = at(2)
                    pe.wait_ge(s["rows_ready"], g + 1)
                    until(pe, s["inv_z_ready"], u - 1)
                    for c in range(DC):
                        last = pe.transpose(s_ps[:, c * P:(c + 1) * P], rows[:, c * P:(c + 1) * P], ident[:, :])
                    last.then_inc(s["rows_turned"], 1)
                if at(-2):
                    u, n, g = at(-2)
                    pe.wait_ge(s["heads_ready"], u + 1)
                    pe.wait_ge(s["qk_ready"], upto(u + 4))
                    until(pe, s["heads_high_ready"], u)
                    until(pe, s["heads_low_ready"], u)
                    for h in range(GH):
                        last = pe.transpose(qk_ps[:, h * P:(h + 1) * P], heads[:, h * DV:(h + 1) * DV], ident[:, :])
                    last.then_inc(s["heads_turned"], 1)
                if at(-1):
                    u, n, g = at(-1)
                    pe.wait_ge(s["prob_t_ready"], u + 1)
                    pe.wait_ge(s["first_ready"], upto(u + 2))
                    until(pe, s["second_ready"], u)
                    for j in range(2):
                        for e in range(2):
                            a = e * M
                            last = pe.matmul(pair_ps[:, e, j * P:(j + 1) * P], slots_t[n % 2][a:a + M, j, :], prob_t[a:a + M, j, :],
                                             start=True, stop=True)
                    last.then_inc(s["second_done"], 1)
            steps(pe, step, units, NG, 2, 3)

        @block.scalar
        def _(act):
            def step(at):
                if at(-1):
                    u, n, g = at(-1)
                    act.wait_ge(s["shifted_ready"], u + 1)
                    until(act, s["prob_z_ready"], u)
                    until(act, s["total_ready"], u)
                    act.activation(prob[:, :], ok[:, :], ACT.Exp).then_inc(s["prob_ready"], 1)
                if at(1):
                    u, n, g = at(1)
                    act.wait_ge(s["qk_done"], u + 1)
                    until(act, s["first_done"], u - 1)
                    act.activation(qk[n % 2][:, :, :, :], qk_ps[:, :].rearrange("p (a j r) -> p a j r", a=2, j=2), ACT.Copy).then_inc(s["qk_ready"], 1)
                    act.wait_ge(s["clipped_ready"], u + 1)
                    act.activation(slots[n % 2][:, :], slots[n % 2][:, :], ACT.Exp).then_inc(s["slots_ready"], 1)
                if at(-2):
                    u, n, g = at(-2)
                    act.wait_ge(s["head_done"], u + 1)
                    until(act, s["mean_sq_ready"], u)
                    for h in range(GH):
                        last = act.activation(squares[:, h * DV:(h + 1) * DV], head_ps[:, h * DV:(h + 1) * DV], ACT.Square, accum_out=square_sum[:, h:h + 1])
                    last.then_inc(s["squared"], 1)
                if at(0):
                    u, n, g = at(0)
                    act.wait_ge(s["slots_turned"], u + 1)
                    until(act, s["second_done"], u - 1)
                    act.activation(slots_t[n % 2][:, :, :], slot_ps[:, 0:GM].rearrange("p (j r) -> p j r", j=2), ACT.Copy).then_inc(s["slots_t_ready"], 1)
                if at(1):
                    u, n, g = at(1)
                    act.wait_ge(s["v_done"], u + 1)
                    until(act, s["head_done"], u - 3)
                    act.activation(values[n][:, :], vg_ps[:, :], ACT.Copy).then_inc(s["v_ready"], 1)
                if at(-1):
                    u, n, g = at(-1)
                    act.wait_ge(s["prob_turned"], u + 1)
                    until(act, s["second_done"], u)
                    act.activation(prob_t[:, :, :], slot_ps[:, 0:GM].rearrange("p (j r) -> p j r", j=2), ACT.Copy).then_inc(s["prob_t_ready"], 1)
                if at(1):
                    u, n, g = at(1)
                    act.wait_ge(s["g_done"], u + 1)
                    until(act, s["gate_ready"], u)
                    act.activation(tanh[:, :], vg_ps[:, :], ACT.Tanh, scale=0.5).then_inc(s["tanh_ready"], 1)
                if at(2) and at(2)[1] == 0:
                    u, n, g = at(2)
                    act.wait_ge(s["rows_turned"], g + 1)
                    act.activation(rows_high[:, :, :], s_ps[:, 0:D].rearrange("p (c r) -> p c r", c=DC), ACT.Copy).then_inc(s["rows_high_ready"], 1)
                    act.activation(rows_t[:, :, :], s_ps[:, 0:D].rearrange("p (c r) -> p c r", c=DC), ACT.Copy).then_inc(s["rows_t_ready"], 1)
                if at(-2):
                    u, n, g = at(-2)
                    act.wait_ge(s["heads_turned"], u + 1)
                    until(act, s["projected"], u)
                    until(act, s["heads_low_ready"], u)
                    act.activation(heads_high[:, :, :], qk_ps[:, :].rearrange("p (h r) -> p h r", h=GH), ACT.Copy).then_inc(s["heads_high_ready"], 1)
            steps(act, step, units, NG, 2, 2)

        @block.vector
        def _(dve):
            dve.tensor_scalar(mask_q[:, :], mask[:, :], float(DK) ** -0.5, None, ALU.mult).then_inc(s["mask_ready"], 1)
            dve.wait_ge(s["mask_ready"], 1)

            def step(at):
                if at(-4) and at(-4)[1] == NG - 1:
                    dve.wait_ge(s["added"], at(-4)[2] + 1)
                if at(-1):
                    u, n, g = at(-1)
                    dve.wait_ge(s["ok_done"], u + 1)
                    dve.wait_ge(s["inv_z_ready"], u + 1)
                    until(dve, s["prob_ready"], u)
                    dve.tensor_tensor(ok[:, :], slot_ps[:, 256:256 + GM], inv_z[n % 2][:, :], ALU.mult).then_inc(s["ok_ready"], 1)
                    dve.wait_ge(s["ok_ready"], u + 1)
                    dve.tensor_reduce(peak[:, :], by_head(ok[:, :], M), X, ALU.max).then_inc(s["peak_ready"], 1)
                    dve.wait_ge(s["peak_ready"], u + 1)
                    dve.tensor_tensor(by_head(ok[:, :], M), by_head(ok[:, :], M), over(peak[:, :], M), ALU.subtract).then_inc(s["shifted_ready"], 1)
                if at(-4) and at(-4)[1] == NG - 1:
                    u, n, g = at(-4)
                    dve.bn_stats(stats[:, g, :], x_sb[:, g, :]).then_inc(s["stats_done"], 1)
                if at(1):
                    u, n, g = at(1)
                    dve.wait_ge(s["s_done"], u + 1)
                    until(dve, s["ok_done"], u - 1)
                    dve.tensor_scalar(slots[n % 2][:, :], s_ps[:, 0:GM], -32.0, 32.0, ALU.max, ALU.min).then_inc(s["clipped_ready"], 1)
                if at(-1):
                    u, n, g = at(-1)
                    dve.wait_ge(s["prob_ready"], u + 1)
                    dve.tensor_reduce(total[n % 2][:, :], by_head(prob[:, :], M), X, ALU.add).then_inc(s["total_ready"], 1)
                if at(-2):
                    u, n, g = at(-2)
                    dve.wait_ge(s["total_ready"], u + 1)
                    dve.scalar_tensor_tensor(eps_sum[:, :], total[n % 2][:, :], EPS, total[n % 2][:, :], ALU.mult, ALU.mult).then_inc(s["eps_ready"], 1)
                    dve.wait_ge(s["squared"], u + 1)
                    dve.wait_ge(s["eps_ready"], u + 1)
                    until(dve, s["root_ready"], u)
                    dve.scalar_tensor_tensor(mean_sq[:, :], square_sum[:, :], 1.0 / DV, eps_sum[:, :], ALU.mult, ALU.add).then_inc(s["mean_sq_ready"], 1)
                if at(0):
                    u, n, g = at(0)
                    dve.wait_ge(s["first_done"], u + 1)
                    until(dve, s["ok_done"], u)
                    dve.tensor_tensor(first[:, :, :, :], pair_ps[:, :, 0:2 * P].rearrange("p e (j r) -> p e j r", j=2),
                                      mask_q[:, :].unsqueeze(1).unsqueeze(1).to_broadcast([P, 2, 2, P]), ALU.mult).then_inc(s["first_ready"], 1)
                    dve.wait_ge(s["z_done"], u + 1)
                    until(dve, s["prob_z_ready"], u - 1)
                    dve.reciprocal(inv_z[n % 2][:, :], s_ps[:, 256:256 + GM]).then_inc(s["inv_z_ready"], 1)
                if at(-2):
                    u, n, g = at(-2)
                    dve.wait_ge(s["root_ready"], u + 1)
                    dve.wait_ge(s["gate_ready"], u + 1)
                    until(dve, s["heads_turned"], u)
                    for h in range(GH):
                        col = slice(h * DV, (h + 1) * DV)
                        last = dve.scalar_tensor_tensor(heads[:, col], head_ps[:, col], root[:, h:h + 1], gate[n][:, col], ALU.mult, ALU.mult)
                    last.then_inc(s["heads_ready"], 1)
                if at(1):
                    u, n, g = at(1)
                    dve.wait_ge(s["tanh_ready"], u + 1)
                    dve.scalar_tensor_tensor(gate[n][:, :], tanh[:, :], 1.0, vg_ps[:, :], ALU.add, ALU.mult).then_inc(s["gate_ready"], 1)
                if at(-2):
                    u, n, g = at(-2)
                    dve.wait_ge(s["heads_high_ready"], u + 1)
                    dve.tensor_tensor(heads_low[:, :, :], qk_ps[:, :].rearrange("p (h r) -> p h r", h=GH),
                                      heads_high[:, :, :].bitcast(F32), ALU.subtract).then_inc(s["heads_low_ready"], 1)
                if at(-1):
                    u, n, g = at(-1)
                    dve.wait_ge(s["second_done"], u + 1)
                    until(dve, s["head_done"], u)
                    dve.tensor_tensor(second[:, :, :, :], pair_ps[:, :, 0:2 * P].rearrange("p e (j r) -> p e j r", j=2),
                                      mask[:, :].unsqueeze(1).unsqueeze(1).to_broadcast([P, 2, 2, P]), ALU.mult).then_inc(s["second_ready"], 1)
                if at(-3) and at(-3)[1] == NG - 1:
                    u, n, g = at(-3)
                    dve.wait_ge(s["projected"], u + 1)
                    dve.tensor_tensor(x_sb[:, g, :], out_ps[:, 0:D], x_sb[:, g, :], ALU.add).then_inc(s["added"], 1)
                if at(3) and at(3)[1] == 0:
                    u, n, g = at(3)
                    until(dve, s["rows_turned"], g)
                    dve.tensor_scalar(rows[:, :], x_sb[:, g, :], mean[:, bass.ds(g, 1)], rstd[:, bass.ds(g, 1)],
                                      ALU.subtract, ALU.mult).then_inc(s["rows_ready"], 1)
            steps(dve, step, units, NG, 3, 4)



def route(nc, sem, w, rows_t, coef, mix, w2, b1, ident, experts_loaded, tag="r"):
    groups = NT // TG
    with ExitStack() as ctx:
        def sb(name, shape):
            return ctx.enter_context(nc.sbuf_tensor(f"{tag}_{name}", shape, F32))

        def ps(name, shape):
            return ctx.enter_context(nc.psum_tensor(f"{tag}_{name}", shape, F32))

        router_w, router_b, cost = sb("router_w", [P, DC, NE]), sb("router_b", [P, NE]), sb("cost", [P, NE])
        lower = sb("lower", [P, NE, NE])
        flat = [sb(f"flat{n}", [NE, TG, P]) for n in range(2)]
        logits, prob = sb("logits", [P, NT, NE]), sb("prob", [P, NT, NE])
        peak, total, inverse = (sb(n, [P, NT]) for n in ("peak", "total", "inverse"))
        above, same = sb("above", [P, NT, NE, NE]), sb("same", [P, NT, NE, NE])
        rank, is_first, is_second, picked = (sb(n, [P, NT, NE]) for n in ("rank", "is_first", "is_second", "picked"))
        p_first, p_second, gap, ratio, g_first, g_second = (
            sb(n, [P, NT]) for n in ("p_first", "p_second", "gap", "ratio", "g_first", "g_second"))
        b2 = sb("b2", [NE + 1, FL])
        b2_to = sb("b2_to", [NE + 1, NE + 2])
        gelu_b1 = sb("gelu_b1", [P, NCH])
        spread = sb("spread", [P, NCH, NE + 2])
        flat_ps = [ps(f"flat_ps{n}", [P, 512]) for n in range(2)]
        logit_ps = [ps(f"logit_ps{n}", [P, 512]) for n in range(2)]
        mix_ps = ps("mix_ps", [P, 512])

        names = ("loaded", "flat_done", "flat_ready", "logit_done", "logit_ready",
                 "w2_scaled", "chain", "shifted", "exp_done", "gap_ready", "ratio_done", "cleared", "gelu_done",
                 "spread_ready", "mix_done", "mix_ready")
        s = {n: sem(f"{tag}_{n}") for n in names}
        block = ctx.enter_context(nc.Block())
        shape4 = [P, NT, NE, NE]

        @block.sync
        def _(sp):
            sp.dma_start(router_w[:, :, :], w["router_w"].rearrange("(c p) e -> p c e", p=P)).then_inc(s["loaded"], 16)
            for t, n in ((router_b, "router_b"), (cost, "cost")):
                sp.dma_start(t[:, :], w[n].partition_broadcast(P)).then_inc(s["loaded"], 16)
            sp.dma_start(lower[:, :, :], w["lower"].partition_broadcast(P)).then_inc(s["loaded"], 16)
            sp.dma_start(b2[:, :], w["b2"]).then_inc(s["loaded"], 16)
            sp.dma_start(b2_to[:, :], w["b2_to"]).then_inc(s["loaded"], 16)

        @block.gpsimd
        def _(pool):
            pool.memset(spread[:, :, :], 0.0).then_inc(s["cleared"], 1)

        @block.tensor
        def _(pe):
            pe.wait_ge(s["loaded"], 16 * 6)

            def step(at):
                if at(0):
                    u, n, g = at(0)
                    until(pe, s["flat_ready"], u - 1)
                    for c in range(DC):
                        last = pe.matmul(flat_ps[n][0:NE, :], router_w[:, c, :], rows_t[:, c, bass.ds(u * TG * P, TG * P)],
                                         start=c == 0, stop=c == DC - 1)
                    last.then_inc(s["flat_done"], 1)
                if at(-1):
                    u, n, g = at(-1)
                    pe.wait_ge(s["flat_ready"], u + 1)
                    until(pe, s["logit_ready"], u - 1)
                    for k in range(TG):
                        last = pe.transpose(logit_ps[n][:, k * NE:(k + 1) * NE], flat[n][:, k, :], ident[0:NE, 0:NE])
                    last.then_inc(s["logit_done"], 1)
            steps(pe, step, groups, 2, 0, 1, loop=False)
            pe.wait_ge(s["spread_ready"], 1)
            pe.matmul(mix_ps[0:NE + 2, 0:FL], b2_to[:, :], b2[:, :], start=True, stop=False)
            for c in range(NCH):
                last = pe.matmul(mix_ps[0:NE + 2, 0:FL], spread[:, c, :], w2[:, c + 1, :], start=False, stop=c == NCH - 1)
            last.then_inc(s["mix_done"], 1)

        @block.scalar
        def _(act):
            def step(at):
                u, n, g = at(0)
                act.wait_ge(s["flat_done"], u + 1)
                until(act, s["logit_done"], u - 1)
                act.activation(flat[n][:, :, :], flat_ps[n][0:NE, :].rearrange("e (k r) -> e k r", k=TG), ACT.Copy).then_inc(s["flat_ready"], 1)
            steps(act, step, groups, 2, 0, 0, loop=False)
            act.wait_ge(s["shifted"], 1)
            act.activation(prob[:, :, :], logits[:, :, :], ACT.Exp).then_inc(s["exp_done"], 1)
            act.wait_ge(s["gap_ready"], 1)
            act.wait_ge(experts_loaded, 48)
            act.activation(ratio[:, :], gap[:, :], ACT.Exp).then_inc(s["ratio_done"], 1)
            act.activation(gelu_b1[:, :], b1[:, 1:NCH + 1], ACT.Gelu).then_inc(s["gelu_done"], 1)
            act.wait_ge(s["mix_done"], 1)
            act.activation(mix[:, :], mix_ps[0:NE + 2, 0:FL], ACT.Copy).then_inc(s["mix_ready"], 1)

        @block.vector
        def _(dve):
            link = [0]

            def then(ins):
                link[0] += 1
                ins.then_inc(s["chain"], 1)
                dve.wait_ge(s["chain"], link[0])

            dve.wait_ge(s["loaded"], 16 * 6)
            dve.wait_ge(experts_loaded, 48)
            dve.tensor_scalar(w2[:, 0, :], w2[:, 0, :], 0.1, None, ALU.mult).then_inc(s["w2_scaled"], 1)
            then(dve.scalar_tensor_tensor(router_b[:, :], cost[:, :], -COST_LAMBDA, router_b[:, :], ALU.mult, ALU.add))

            def step(at):
                u, n, g = at(0)
                dve.wait_ge(s["logit_done"], u + 1)
                dve.tensor_tensor(logits[:, bass.ds(u * TG, TG), :], logit_ps[n][:, 0:TG * NE].rearrange("p (k e) -> p k e", e=NE),
                                  router_b[:, :].unsqueeze(1).to_broadcast([P, TG, NE]), ALU.add).then_inc(s["logit_ready"], 1)
            steps(dve, step, groups, 2, 0, 0, loop=False)
            dve.wait_ge(s["logit_ready"], groups)

            def each(ap):
                return ap.unsqueeze(2).to_broadcast([P, NT, NE])

            then(dve.tensor_reduce(peak[:, :], logits[:, :, :], X, ALU.max))
            dve.tensor_tensor(logits[:, :, :], logits[:, :, :], each(peak[:, :]), ALU.subtract).then_inc(s["shifted"], 1)
            dve.wait_ge(s["exp_done"], 1)
            then(dve.tensor_reduce(total[:, :], prob[:, :, :], X, ALU.add))
            then(dve.reciprocal(inverse[:, :], total[:, :]))
            then(dve.tensor_tensor(prob[:, :, :], prob[:, :, :], each(inverse[:, :]), ALU.mult))
            mine = prob[:, :, :].unsqueeze(3).to_broadcast(shape4)
            other = prob[:, :, :].unsqueeze(2).to_broadcast(shape4)
            dve.tensor_tensor(above[:, :, :, :], other, mine, ALU.is_gt)
            then(dve.tensor_tensor(same[:, :, :, :], other, mine, ALU.is_equal))
            then(dve.tensor_tensor(same[:, :, :, :], same[:, :, :, :], lower[:, :, :].unsqueeze(1).to_broadcast(shape4), ALU.mult))
            then(dve.tensor_tensor(above[:, :, :, :], above[:, :, :, :], same[:, :, :, :], ALU.add))
            then(dve.tensor_reduce(rank[:, :, :], above[:, :, :, :], X, ALU.add))
            dve.tensor_scalar(is_first[:, :, :], rank[:, :, :], 0.0, None, ALU.is_equal)
            then(dve.tensor_scalar(is_second[:, :, :], rank[:, :, :], 1.0, None, ALU.is_equal))
            then(dve.tensor_tensor(picked[:, :, :], prob[:, :, :], is_first[:, :, :], ALU.mult))
            then(dve.tensor_reduce(p_first[:, :], picked[:, :, :], X, ALU.add))
            then(dve.tensor_tensor(picked[:, :, :], prob[:, :, :], is_second[:, :, :], ALU.mult))
            then(dve.tensor_reduce(p_second[:, :], picked[:, :, :], X, ALU.add))
            dve.tensor_tensor(gap[:, :], p_second[:, :], p_first[:, :], ALU.subtract).then_inc(s["gap_ready"], 1)
            dve.wait_ge(s["ratio_done"], 1)
            then(dve.tensor_scalar(total[:, :], ratio[:, :], 1.0, None, ALU.add))
            then(dve.reciprocal(g_first[:, :], total[:, :]))
            then(dve.tensor_tensor(g_second[:, :], ratio[:, :], g_first[:, :], ALU.mult))
            dve.tensor_tensor(is_first[:, :, :], is_first[:, :, :], each(g_first[:, :]), ALU.mult)
            dve.tensor_tensor(is_second[:, :, :], is_second[:, :, :], each(g_second[:, :]), ALU.mult)
            dve.memset(coef[:, :, NE + 1], 0.1)
            then(dve.tensor_tensor(coef[:, :, NE], g_first[:, :], g_second[:, :], ALU.add))
            then(dve.tensor_tensor(coef[:, :, 0:NE], is_first[:, :, :], is_second[:, :, :], ALU.add))
            dve.wait_ge(s["gelu_done"], 1)
            dve.wait_ge(s["cleared"], 1)
            for c in range(NCH):
                e = CHUNK_EXPERT[c]
                dve.tensor_scalar(spread[:, c, e:e + 1], gelu_b1[:, c:c + 1], -1.0, None, ALU.mult)
            dve.tensor_copy(spread[:, :, NE], gelu_b1[:, :]).then_inc(s["spread_ready"], 1)



def experts(nc, sem, w, out, x_sb, rows_t, coef, mix, w1, w2, b1, ident, tag="e"):
    CH = NCH + 1
    TR = TG * P
    units = NT // TG * CH
    NEX = NE + 1
    owner = [0] + [e + 1 for e in CHUNK_EXPERT]
    opens = [n == 0 or owner[n] != owner[n - 1] for n in range(CH)]
    closes = [n == CH - 1 or owner[n] != owner[n + 1] for n in range(CH)]
    NY = 3
    with ExitStack() as ctx:
        def sb(name, shape):
            return ctx.enter_context(nc.sbuf_tensor(f"{tag}_{name}", shape, F32))

        def ps(name):
            return ctx.enter_context(nc.psum_tensor(f"{tag}_{name}", [P, 512], F32))

        bias, bias2 = sb("bias", [P, D]), sb("bias2", [P, D])
        down_w, down_b = sb("down_w", [P, DC, FL]), sb("down_b", [P, 1])
        core_w, up_w = sb("core_w", [P, DC, D]), sb("up_w", [P, D])
        gelu_h = sb("gelu_h", [P, TR])
        hidden = [sb(f"hidden{k}", [P, TR]) for k in range(3)]
        gelu_x = sb("gelu_x", [P, DC, TR])
        coef_now = sb("coef_now", [P, TG, NE + 2])
        coef_t = sb("coef_t", [NE + 2, TG, P])
        acc, acc_t = sb("acc", [P, TG, FL]), sb("acc_t", [P, TG, P])
        hidden_ps = [ps(f"hidden_ps{k}") for k in range(2)]
        y_ps = [ps(f"y_ps{k}") for k in range(NY)]
        h_ps, turn_ps, out_ps = ps("h_ps"), ps("turn_ps"), ps("out_ps")

        names = ("loaded", "bias_loaded", "bias_ready", "bias_added", "h_done", "gelu_h_ready", "hidden_done", "hidden_ready", "y_chunk", "y_done", "y_added", "gelu_x_ready",
                 "coef_ready", "coef_turned", "coef_t_ready", "acc_turned", "acc_t_ready", "out_done", "x_ready", "stored")
        s = {n: sem(f"{tag}_{n}") for n in names}
        block = ctx.enter_context(nc.Block())
        out_rows = out.rearrange("b s d -> (b s) d").rearrange("(g k p) d -> g p k d", k=TG, p=P)
        assert CH % 3 == 0 and NEX % NY == 0

        @block.sync
        def _(sp):
            sp.dma_start(down_w[:, :, :], w["down_w"].rearrange("(c p) n -> p c n", p=P)).then_inc(s["loaded"], 16)
            sp.dma_start(core_w[:, :, :], w["core_w"].rearrange("(c p) n -> p c n", p=P)).then_inc(s["loaded"], 16)
            sp.dma_start(up_w[:, :], w["up_w"]).then_inc(s["loaded"], 16)
            sp.dma_start(down_b[:, :], w["down_b"].rearrange("(p o) -> p o", o=1)).then_inc(s["loaded"], 16)
            sp.dma_start(bias[:, :], w["core_b"].partition_broadcast(P)).then_inc(s["bias_loaded"], 16)
            sp.dma_start(bias2[:, :], w["up_b"].partition_broadcast(P)).then_inc(s["bias_loaded"], 16)

            def step(at):
                u, n, g = at(0)
                sp.wait_ge(s["x_ready"], 2 * (u + 1))
                sp.dma_start(out_rows[u], x_sb[:, bass.ds(u * TG, TG), :]).then_inc(s["stored"], 16)
            steps(sp, step, NT // TG, 2, 0, 0)
            sp.wait_ge(s["stored"], 16 * NT // TG)

        @block.gpsimd
        def _(pool):
            pool.wait_ge(s["bias_loaded"], 32)
            pool.tensor_tensor(bias[:, :], bias[:, :], bias2[:, :], ALU.add).then_inc(s["bias_ready"], 1)
            pool.wait_ge(s["bias_ready"], 1)
            pool.tensor_tensor(x_sb[:, :, :], x_sb[:, :, :], bias[:, :].unsqueeze(1).to_broadcast([P, NT, D]), ALU.add).then_inc(s["bias_added"], 1)

        @block.tensor
        def _(pe):
            pe.wait_ge(s["loaded"], 64)

            def step(at):
                if at(0):
                    u, n, g = at(0)
                    e = owner[n]
                    y = y_ps[e % NY]
                    pe.wait_ge(s["hidden_ready"], u + 1)
                    if opens[n]:
                        until(pe, s["y_added"], g * NEX + e - NY + 1)
                    if n == 0:
                        pe.wait_ge(s["coef_t_ready"], g + 1)
                    for k in range(TG):
                        last = pe.matmul(y[:, k * FL:(k + 1) * FL], hidden[n % 3][:, k * P:(k + 1) * P], w2[:, n, :],
                                         start=opens[n] and k == 0, stop=closes[n] and n > 0, skip_group_check=True)
                    if n == 0:
                        for k in range(TG):
                            last = pe.matmul(y[:, k * FL:(k + 1) * FL], coef_t[:, k, :], mix[:, :], start=False, stop=True,
                                             skip_group_check=True)
                    last.then_inc(s["y_chunk"], 1)
                if at(-1) and at(-1)[1] == CH - 1:
                    u, n, g = at(-1)
                    pe.wait_ge(s["y_added"], (g + 1) * NEX)
                    until(pe, s["coef_t_ready"], min(g + 2, NT // TG) if isinstance(g, int) else g + 2)
                    for k in range(TG):
                        last = pe.transpose(turn_ps[:, k * P:(k + 1) * P], acc[:, k, :], ident[:, :])
                    last.then_inc(s["acc_turned"], 1)
                if at(2):
                    u, n, g = at(2)
                    if n == 0:
                        pe.wait_ge(s["gelu_h_ready"], g + 1)
                    until(pe, s["hidden_ready"], u - 1 if n else u)
                    pe.matmul(hidden_ps[n % 2][:, :], w1[:, n, :], gelu_h[:, :], start=True, stop=True).then_inc(s["hidden_done"], 1)
                if at(-2) and at(-2)[1] == CH - 1:
                    u, n, g = at(-2)
                    pe.wait_ge(s["acc_t_ready"], g + 1)
                    pe.wait_ge(s["gelu_x_ready"], g + 1)
                    for r in range(2):
                        until(pe, s["x_ready"], 2 * g + r)
                        for q in range(2):
                            k = 2 * r + q
                            for c in range(DC):
                                pe.matmul(out_ps[:, q * D:(q + 1) * D], gelu_x[:, c, k * P:(k + 1) * P], core_w[:, c, :],
                                          start=c == 0, stop=False)
                            last = pe.matmul(out_ps[:, q * D:(q + 1) * D], acc_t[:, k, :], up_w[:, :], start=False, stop=True)
                        last.then_inc(s["out_done"], 1)
                if at(4) and at(4)[1] == 0:
                    u, n, g = at(4)
                    until(pe, s["gelu_h_ready"], g)
                    for c in range(DC):
                        last = pe.matmul(h_ps[:, :], down_w[:, c, :], rows_t[:, c, bass.ds(g * TR, TR)], start=c == 0, stop=c == DC - 1)
                    last.then_inc(s["h_done"], 1)
                if at(6) and at(6)[1] == 0:
                    u, n, g = at(6)
                    pe.wait_ge(s["coef_ready"], g + 1)
                    until(pe, s["acc_t_ready"], g - 1)
                    until(pe, s["coef_t_ready"], g)
                    for k in range(TG):
                        last = pe.transpose(turn_ps[0:NE + 2, k * P:(k + 1) * P], coef_now[:, k, :], ident[:, :])
                    last.then_inc(s["coef_turned"], 1)

            steps(pe, step, units, CH, 6, 2)

        @block.scalar
        def _(act):
            act.wait_ge(s["loaded"], 64)

            def step(at):
                if at(3) and at(3)[1] == 0:
                    u, n, g = at(3)
                    act.wait_ge(s["h_done"], g + 1)
                    until(act, s["hidden_done"], u)
                    act.activation(gelu_h[:, :], h_ps[:, :], ACT.Gelu, bias=down_b[:, 0:1]).then_inc(s["gelu_h_ready"], 1)
                if at(2):
                    u, n, g = at(2)
                    act.wait_ge(s["hidden_done"], u + 1)
                    until(act, s["y_chunk"], u - 2)
                    act.activation(hidden[n % 3][:, :], hidden_ps[n % 2][:, :], ACT.Gelu, bias=b1[:, n:n + 1]).then_inc(s["hidden_ready"], 1)
                if at(0) and at(0)[1] == 6:
                    u, n, g = at(0)
                    until(act, s["out_done"], 2 * g)
                    for c in range(DC):
                        last = act.activation(gelu_x[:, c, :], rows_t[:, c, bass.ds(g * TR, TR)], ACT.Gelu)
                    last.then_inc(s["gelu_x_ready"], 1)
            steps(act, step, units, CH, 3, 0)

        @block.vector
        def _(dve):
            dve.wait_ge(s["bias_added"], 1)

            def step(at):
                if at(0) and closes[at(0)[1]]:
                    u, n, g = at(0)
                    e = owner[n]
                    y = y_ps[e % NY][:, :].rearrange("p (k l) -> p k l", k=TG)
                    dve.wait_ge(s["y_chunk"], u + 1)
                    if e == 0:
                        until(dve, s["acc_turned"], g)
                        dve.tensor_copy(acc[:, :, :], y).then_inc(s["y_added"], 1)
                    else:
                        dve.wait_ge(s["y_added"], g * NEX + e)
                        for k in range(TG):
                            last = dve.scalar_tensor_tensor(acc[:, k, :], y[:, k, :], coef[:, g * TG + k, e - 1:e], acc[:, k, :],
                                                            ALU.mult, ALU.add)
                        last.then_inc(s["y_added"], 1)
                if at(-1) and at(-1)[1] == CH - 1:
                    u, n, g = at(-1)
                    dve.wait_ge(s["acc_turned"], g + 1)
                    until(dve, s["out_done"], 2 * g)
                    dve.tensor_copy(acc_t[:, :, :], turn_ps[:, :].rearrange("p (k r) -> p k r", k=TG)).then_inc(s["acc_t_ready"], 1)
                if at(-2) and at(-2)[1] == CH - 1:
                    u, n, g = at(-2)
                    for r in range(2):
                        dve.wait_ge(s["out_done"], 2 * g + r + 1)
                        rows = x_sb[:, bass.ds(g * TG + 2 * r, 2), :]
                        dve.tensor_tensor(rows, out_ps[:, :].rearrange("p (k d) -> p k d", k=2), rows, ALU.add).then_inc(s["x_ready"], 1)
                if at(8) and at(8)[1] == 0:
                    u, n, g = at(8)
                    until(dve, s["coef_turned"], g)
                    dve.tensor_scalar(coef_now[:, :, :], coef[:, bass.ds(g * TG, TG), :], 1.0, None, ALU.mult).then_inc(s["coef_ready"], 1)
                if at(5) and at(5)[1] == 0:
                    u, n, g = at(5)
                    dve.wait_ge(s["coef_turned"], g + 1)
                    until(dve, s["y_chunk"], g * CH - CH + 1)
                    dve.tensor_copy(coef_t[:, :, :], turn_ps[0:NE + 2, :].rearrange("p (k r) -> p k r", k=TG)).then_inc(s["coef_t_ready"], 1)
            steps(dve, step, units, CH, 8, 2)



CONSTANTS = {
    "ident": [P, P], "mask": [P, P], "minus_half": [P, NT],
    "cos_k": [LN, LC, CD], "sin_k": [LN, LC, CD], "cos_q": [QC, 2, S], "sin_q": [QC, 2, S],
}


def perceiver_block(nc, w, out):
    with ExitStack() as ctx:
        taken = []

        def sem(name):
            taken.append(nc.alloc_semaphore(name))
            return taken[-1]

        def semaphores_end():
            nc.clear_and_free_semaphores(taken)
            nc.all_engine_barrier()
            taken.clear()

        x_sb = ctx.enter_context(nc.sbuf_tensor("x_sb", [P, NT, D], F32))
        mean = ctx.enter_context(nc.sbuf_tensor("mean", [P, NT], F32))
        rstd = ctx.enter_context(nc.sbuf_tensor("rstd", [P, NT], F32))
        stats = ctx.enter_context(nc.sbuf_tensor("stats", [P, NT, 6], F32))
        const = {n: ctx.enter_context(nc.sbuf_tensor(n, shape, F32)) for n, shape in CONSTANTS.items()}
        ident, minus_half = const["ident"], const["minus_half"]

        wide = ctx.enter_context(nc.sbuf_tensor("wide", [P, DC * ROWS], F32))
        spare = ctx.enter_context(nc.sbuf_tensor("spare", [P, 2 * HH * D], F32))
        ws = ctx.enter_context(nc.sbuf_tensor("ws", [P, DC, AH * M], F32))
        assert DC * ROWS == 2 * DC * AH * DV and 2 * HH * D == 2 * DC * AH * DK
        wv, wg = (wide[:, k * DC * AH * DV:(k + 1) * DC * AH * DV].rearrange("p (c n) -> p c n", c=DC) for k in range(2))
        wq, wk = (spare[:, k * DC * AH * DK:(k + 1) * DC * AH * DK].rearrange("p (c n) -> p c n", c=DC) for k in range(2))

        x_loaded, const_loaded = [sem(f"x_loaded{j}") for j in range(4)], sem("const_loaded")
        with nc.Block() as block:
            @block.sync
            def _(sp):
                rows = w["x"].rearrange("b s d -> (b s) d").rearrange("(i p) d -> p i d", p=P)
                q = NT // len(x_loaded)
                for j, quarter_loaded in enumerate(x_loaded):
                    sp.dma_start(x_sb[:, j * q:(j + 1) * q, :], rows[:, j * q:(j + 1) * q, :]).then_inc(quarter_loaded, 16)

            @block.scalar
            def _(act):
                for n, shape in CONSTANTS.items():
                    act.dma_start(const[n][:], w[n]).then_inc(const_loaded, 16)
                act.wait_ge(const_loaded, 16 * len(CONSTANTS))

        with ExitStack() as one:
            def sb(name, shape):
                return one.enter_context(nc.sbuf_tensor(name, shape, F32))

            xnt = wide[:, :].rearrange("p (c s b) -> p c s b", c=DC, s=S)
            qmap = spare[0:QC, :].rearrange("p (k h d) -> p k h d", k=2, h=HH)
            queries = sb("queries", [P, NP, S, B])
            gmap, omap = sb("gmap", [QC, 2, HH, CD]), sb("omap", [P, NP, D])
            slot_weights = [(to, w[n].rearrange("(c p) n -> p c n", p=P))
                            for n, to in (("aws", ws[:, :, :]), ("awq", wq), ("awk", wk), ("awv", wv), ("awg", wg))]
            for hh in range(2):
                if hh == 0:
                    fold_weights(nc, sem, w, hh, qmap, gmap, omap, f"f{hh}", beside=lambda block, ctx: row_statistics(
                        sem, block, ctx, nc, stats, mean, rstd, minus_half, "n1", x_sb, x_loaded))
                    transposed_rows(nc, sem, x_sb, mean, rstd, ident,
                                    lambda i: xnt[:, :, :, bass.ds(i * BT, BT)].rearrange("p c s b -> p c b s"), "t1")
                else:
                    fold_weights(nc, sem, w, hh, qmap, gmap, omap, f"f{hh}")
                make_queries(nc, sem, qmap, gmap, const["cos_q"], const["sin_q"], xnt, queries, f"q{hh}")
                last = hh == 1
                attend(nc, sem, w, x_sb, queries, omap, const["cos_k"], const["sin_k"], ident, f"a{hh}",
                       stats=stats if last else None, ahead=slot_weights if last else ())

        semaphores_end()
        with ExitStack() as rest:
            def sb(name, shape):
                return rest.enter_context(nc.sbuf_tensor(name, shape, F32))

            with ExitStack() as two:
                def halves(name, shape):
                    return [two.enter_context(nc.sbuf_tensor(f"{name}_{half}", shape, F32R)) for half in ("high", "low")]

                wv_split, wg_split, wo_split = halves("wv", [P, DC, AH * DV]), halves("wg", [P, DC, AH * DV]), halves("wo", [DV, AH, D])
                with ExitStack() as temporary, nc.Block() as block:
                    row_statistics(sem, block, temporary, nc, stats, mean, rstd, minus_half, "n2")
                    split_weights(sem, block, temporary, nc, w, [(wv, wv_split), (wg, wg_split)], wo_split, w["norm_w"], "p")
                slot_attention(nc, sem, w, x_sb, mean, rstd, ident, const["mask"], (wq, wk, ws, wv_split, wg_split, wo_split), wide, stats)

            semaphores_end()
            w1, w2, b1 = sb("w1", [P, NCH + 1, P]), sb("w2", [P, NCH + 1, FL]), sb("b1", [P, NCH + 1])
            experts_loaded = sem("experts_loaded")
            with ExitStack() as temporary, nc.Block() as block:
                row_statistics(sem, block, temporary, nc, stats, mean, rstd, minus_half, "n3")

                @block.sync
                def _(sp):
                    sp.dma_start(b1[:, :], w["b1"]).then_inc(experts_loaded, 16)
                    sp.dma_start(w2[:, :, :], w["w2"].rearrange("(n p) l -> p n l", p=P)).then_inc(experts_loaded, 16)
                    sp.dma_start(w1[:, :, :], w["w1"].rearrange("p (n q) -> p n q", q=P)).then_inc(experts_loaded, 16)
            rows_t = wide[:, :].rearrange("p (c r) -> p c r", c=DC)
            coef, mix = sb("coef", [P, NT, NE + 2]), sb("mix", [NE + 2, FL])
            transposed_rows(nc, sem, x_sb, mean, rstd, ident,
                            lambda i: rows_t[:, :, bass.ds(i * P, P)].rearrange("p c (b s) -> p c b s", b=BT), "t3")
            route(nc, sem, w, rows_t, coef, mix, w2, b1, ident, experts_loaded)
            experts(nc, sem, w, out, x_sb, rows_t, coef, mix, w1, w2, b1, ident)



def constants():
    f32 = np.float32

    def tables(length, dim):
        inv = f32(1.0) / np.power(f32(10000.0), np.arange(0, dim, 2, dtype=f32) / f32(dim))
        f = np.arange(length, dtype=f32)[:, None] * inv[None, :].astype(f32)
        return np.repeat(np.sin(f), 2, axis=-1), np.repeat(np.cos(f), 2, axis=-1)

    row = np.arange(P)
    sin_k, cos_k = (np.concatenate([a[:L], np.zeros((LC * LN - L, CD), f32)]).reshape(LC, LN, CD).transpose(1, 0, 2)
                    for a in tables(L, CD))
    sign = np.where(np.arange(CD) < CD // 2, f32(-1), f32(1))
    sin_q, cos_q = (a.reshape(S, 2, QC).transpose(2, 1, 0) for a in tables(S, CQ))
    out = {
        "ident": np.eye(P), "minus_half": np.full((P, NT), -0.5),
        "mask": (row[:, None] // S == row[None, :] // S) & (row[:, None] <= row[None, :]),
        "cos_k": cos_k, "sin_k": sin_k * sign, "cos_q": cos_q,
        "cost": [2 * FL * h for h in HID],
        "lower": np.tril(np.ones((NE, NE)), -1),
        "b2_to": [[float(k == NE + (e == NE)) for k in range(NE + 2)] for e in range(NE + 1)],
        "sin_q": np.stack([sin_q[:, 1], -sin_q[:, 0]], axis=1),
    }
    return {n: np.ascontiguousarray(a, dtype=f32) for n, a in out.items()}


def lay_out(i):
    names = ["shared"] + [f"e{e}" for e in range(NE)]
    return {
        "x": i["x"], "ctx": i["ctx_512"],
        "wq": i["L0_xattn_Wq"], "wkq": i["L0_xattn_w_kc_q"], "wkv": i["L0_xattn_w_kc_kv"],
        "wqr_t": i["L0_xattn_W_qr"].transpose(0, 2, 1), "wkr_t": i["L0_xattn_W_kr"].transpose(0, 2, 1),
        "xwo_t": i["L0_xattn_Wo"].T,
        "awq": i["L0_attn_Wq"], "awk": i["L0_attn_Wk"], "aws": i["L0_attn_Ws"], "awv": i["L0_attn_Wv"],
        "awg": i["L0_attn_Wg"], "awo": i["L0_attn_Wo"], "norm_w": i["L0_attn_g_norm_weight"],
        **{n: i[f"L0_ffn_{n}"] for n in ("router_w", "router_b", "down_w", "down_b", "core_w", "core_b", "up_w", "up_b")},
        "w1": np.concatenate([i[f"L0_ffn_{e}_w1"] for e in names], axis=1),
        "b1": np.concatenate([i[f"L0_ffn_{e}_b1"] for e in names]).reshape(-1, P).T,
        "w2": np.concatenate([i[f"L0_ffn_{e}_w2"] for e in names]),
        "b2": np.stack([i[f"L0_ffn_{e}_b2"] for e in names[1:] + names[:1]]),
    }


def kernel(**inputs):
    import concourse.bacc as bacc
    from concourse.bass_utils import run_bass_kernel_spmd

    nc = bacc.Bacc("TRN2", target_bir_lowering=False, num_devices=1)
    inputs = {n: np.asarray(a) for n, a in inputs.items()}
    arrays, w = {}, {}
    for name, a in {**lay_out(inputs), **constants()}.items():
        arrays[f"in_{name}"] = np.ascontiguousarray(a)
        w[name] = nc.dram_tensor(f"in_{name}", a.shape, F32, kind="ExternalInput").ap()
    out = nc.dram_tensor("out", [B, S, D], F32, kind="ExternalOutput").ap()
    perceiver_block(nc, w, out)
    r = run_bass_kernel_spmd(nc, [arrays], core_ids=[0])
    return r.results[0]["out"]
```

```python
from contextlib import ExitStack

import numpy as np

import concourse.bass as bass
from concourse import mybir

F32 = mybir.dt.float32
F32R = mybir.dt.float32r
ALU = mybir.AluOpType
ACT = mybir.ActivationFunctionType
X = mybir.AxisListType.X

P = 128
B, S, D = 128, 32, 256
ROWS = B * S
NT = ROWS // P
BT = P // S
DC = D // P
EPS = 1e-5

L, H, HK, CD, CQ, R = 257, 16, 128, 64, 192, 64
QC = CQ // 2
HH = H // 2
NP = HH // 2
LC, LN = 3, 86
SG = 4

AH, DK, DV, M = 16, 64, 128, 64
GH = 4
NG = AH // GH

HID = [128, 256, 384, 512, 128, 256, 384, 512]
NE = len(HID)
FL = 128
NCH = sum(HID) // P
CHUNK_EXPERT = [e for e, h in enumerate(HID) for _ in range(h // P)]
TG = 4
COST_LAMBDA = 1e-07


def until(eng, sem, count):
    if not (isinstance(count, int) and count <= 0):
        eng.wait_ge(sem, count)


def split_product(pe, out, stationary, moving, start, stop, **options):
    (high, low), (moving_high, moving_low) = stationary, moving
    pe.matmul(out, high, moving_low, start=start, stop=False, **options)
    pe.matmul(out, low, moving_high, start=False, stop=False, **options)
    return pe.matmul(out, high, moving_high, start=False, stop=stop, **options)


def steps(eng, step, units, group, lead, lag, loop=True):
    assert lead <= group and lag <= group and units % group == 0

    def offset(t, b, i):
        def at(o):
            u = t + o
            if isinstance(u, int) and not 0 <= u < units:
                return None
            return u, (b + o) % group, i + (b + o) // group
        return at

    if not loop:
        for t in range(-lead, units + lag):
            step(offset(t, t % group, t // group))
        return
    for t in range(-lead, group):
        step(offset(t, t % group, t // group))
    with eng.Fori(1, units // group - 1) as i:
        for b in range(group):
            step(offset(i * group + b, b, i))
    for t in range(units - group, units + lag):
        step(offset(t, t % group, t // group))



def row_statistics(sem, block, ctx, nc, stats, mean, rstd, half, tag, x_sb=None, x_loaded=(), const_loaded=None, constants=0):
    diff = ctx.enter_context(nc.sbuf_tensor(f"{tag}_diff", [P, NT], F32))
    var = ctx.enter_context(nc.sbuf_tensor(f"{tag}_var", [P, NT], F32))
    stats_done, step_done, var_done, rstd_done = (
        sem(f"{tag}_stats_done"), sem(f"{tag}_step_done"), sem(f"{tag}_var_done"), sem(f"{tag}_rstd_done"))

    @block.vector
    def _(dve):
        if x_sb is not None:
            part = NT // len(x_loaded)
            for i in range(NT):
                if i % part == 0:
                    dve.wait_ge(x_loaded[i // part], 16)
                dve.bn_stats(stats[:, i, :], x_sb[:, i, :]).then_inc(stats_done, 1)
            dve.wait_ge(stats_done, NT)
        dve.tensor_tensor(mean[:, :], stats[:, :, 1], stats[:, :, 4], ALU.add).then_inc(step_done, 1)
        dve.tensor_tensor(diff[:, :], stats[:, :, 1], stats[:, :, 4], ALU.subtract).then_inc(step_done, 1)
        dve.tensor_tensor(var[:, :], stats[:, :, 2], stats[:, :, 5], ALU.add).then_inc(step_done, 1)
        dve.wait_ge(step_done, 3)
        dve.tensor_scalar(mean[:, :], mean[:, :], 0.5, None, ALU.mult).then_inc(step_done, 1)
        dve.scalar_tensor_tensor(diff[:, :], diff[:, :], 0.25, diff[:, :], ALU.mult, ALU.mult).then_inc(step_done, 1)
        dve.tensor_scalar(var[:, :], var[:, :], 1.0 / D, EPS, ALU.mult, ALU.add).then_inc(step_done, 1)
        dve.wait_ge(step_done, 6)
        dve.tensor_tensor(var[:, :], var[:, :], diff[:, :], ALU.add).then_inc(var_done, 1)

    @block.gpsimd
    def _(pool):
        if const_loaded is not None:
            pool.wait_ge(const_loaded, 16 * constants)
        pool.wait_ge(var_done, 1)
        pool.tensor_tensor(rstd[:, :], var[:, :], half[:, 0:NT], ALU.pow).then_inc(rstd_done, 1)


def transposed_rows(nc, sem, x_sb, mean, rstd, ident, place, tag):
    RING = 4
    with ExitStack() as ctx:
        xn = ctx.enter_context(nc.sbuf_tensor(f"{tag}_xn", [P, RING, D], F32))
        turned = ctx.enter_context(nc.psum_tensor(f"{tag}_turned", [P, RING, 512], F32))
        xn_ready, turn_done, place_done = sem(f"{tag}_xn_ready"), sem(f"{tag}_turn_done"), sem(f"{tag}_place_done")
        block = ctx.enter_context(nc.Block())

        @block.vector
        def _(dve):
            def step(at):
                i, b, _ = at(0)
                until(dve, turn_done, i - RING + 1)
                dve.tensor_scalar(xn[:, b, :], x_sb[:, i, :], mean[:, bass.ds(i, 1)], rstd[:, bass.ds(i, 1)],
                                  ALU.subtract, ALU.mult).then_inc(xn_ready, 1)
            steps(dve, step, NT, RING, 0, 0)

        @block.tensor
        def _(pe):
            def step(at):
                i, b, _ = at(0)
                until(pe, xn_ready, i + 1)
                until(pe, place_done, i - RING + 1)
                for c in range(DC):
                    last = pe.transpose(turned[:, b, c * P:(c + 1) * P], xn[:, b, c * P:(c + 1) * P], ident[:, :])
                last.then_inc(turn_done, 1)
            steps(pe, step, NT, RING, 0, 0)

        @block.scalar
        def _(act):
            def step(at):
                i, b, _ = at(0)
                until(act, turn_done, i + 1)
                act.activation(place(i), turned[:, b, 0:D].rearrange("p (c b s) -> p c b s", c=DC, b=BT),
                               ACT.Copy).then_inc(place_done, 1)
            steps(act, step, NT, RING, 0, 0)



def fold_weights(nc, sem, w, hh, qmap, gmap, omap, tag, beside=None):
    with ExitStack() as ctx:
        def sb(name, shape):
            return ctx.enter_context(nc.sbuf_tensor(f"{tag}_{name}", shape, F32))

        def banks(name):
            return [ctx.enter_context(nc.psum_tensor(f"{tag}_{name}{k}", [P, 512], F32)) for k in range(2)]

        wq, wkq, wkv, wo = sb("wq", [P, HH, D]), sb("wkq", [P, HH, CQ]), sb("wkv", [P, HH, CD]), sb("wo", [P, HH, D])
        wqr, wkr = sb("wqr", [R, HH, CQ]), sb("wkr", [R, HH, CD])
        q_ps, g_ps, o_ps = banks("q_ps"), banks("g_ps"), banks("o_ps")
        loaded = [sem(f"{tag}_{n}_loaded") for n in ("q", "g", "o")]
        product_done, q_copied, q_low_ready, g_copied, o_copied = (
            sem(f"{tag}_product_done"), sem(f"{tag}_q_copied"), sem(f"{tag}_q_low_ready"), sem(f"{tag}_g_copied"), sem(f"{tag}_o_copied"))
        block = ctx.enter_context(nc.Block())
        h0 = hh * HH

        if beside:
            beside(block, ctx)

        @block.sync
        def _(sp):
            sp.dma_start(wq[:, :, :], w["wq"][h0 * HK:(h0 + HH) * HK, :].rearrange("(h k) d -> k h d", k=HK)).then_inc(loaded[0], 16)
            sp.dma_start(wkq[:, :, :], w["wkq"][h0:h0 + HH].rearrange("h k q -> k h q")).then_inc(loaded[0], 16)
            sp.dma_start(wqr[:, :, :], w["wqr_t"][h0:h0 + HH].rearrange("h r q -> r h q")).then_inc(loaded[1], 16)
            sp.dma_start(wkr[:, :, :], w["wkr_t"][h0:h0 + HH].rearrange("h r d -> r h d")).then_inc(loaded[1], 16)
            sp.dma_start(wkv[:, :, :], w["wkv"][h0:h0 + HH].rearrange("h k d -> k h d")).then_inc(loaded[2], 16)
            sp.dma_start(wo[:, :, :], w["xwo_t"][h0 * HK:(h0 + HH) * HK, :].rearrange("(h k) d -> k h d", k=HK)).then_inc(loaded[2], 16)

        @block.tensor
        def _(pe):
            pe.wait_ge(loaded[0], 32)
            for h in range(HH):
                n = h % 2
                until(pe, q_low_ready, h - 1)
                for c in range(2):
                    last = pe.matmul(q_ps[n][0:QC, c * D:(c + 1) * D], wkq[:, h, c * QC:(c + 1) * QC], wq[:, h, :],
                                     start=True, stop=True)
                last.then_inc(product_done, 1)
                if h == 0:
                    pe.wait_ge(loaded[1], 32)
                    pe.wait_ge(loaded[2], 32)
                until(pe, g_copied, h - 1)
                for c in range(2):
                    last = pe.matmul(g_ps[n][0:QC, c * CD:(c + 1) * CD], wqr[:, h, c * QC:(c + 1) * QC], wkr[:, h, :],
                                     start=True, stop=True)
                last.then_inc(product_done, 1)
                e = h % 2 * CD
                until(pe, o_copied, h - 1)
                pe.matmul(o_ps[n][e:e + CD, 0:D], wkv[:, h, :], wo[:, h, :], start=True, stop=True).then_inc(product_done, 1)

        @block.scalar
        def _(act):
            for h in range(HH):
                n, e = h % 2, h % 2 * CD
                act.wait_ge(product_done, 3 * h + 1)
                act.activation(qmap[0][:, :, h, :], q_ps[n][0:QC, :].rearrange("p (c d) -> p c d", c=2), ACT.Copy).then_inc(q_copied, 1)
                act.wait_ge(product_done, 3 * h + 2)
                act.activation(gmap[:, :, h, :], g_ps[n][0:QC, 0:2 * CD].rearrange("p (c d) -> p c d", c=2), ACT.Copy).then_inc(g_copied, 1)
                act.wait_ge(product_done, 3 * h + 3)
                act.activation(omap[e:e + CD, h // 2, :], o_ps[n][e:e + CD, 0:D], ACT.Copy).then_inc(o_copied, 1)

        @block.vector
        def _(dve):
            for h in range(HH):
                dve.wait_ge(q_copied, h + 1)
                dve.tensor_tensor(qmap[1][:, :, h, :], q_ps[h % 2][0:QC, :].rearrange("p (c d) -> p c d", c=2),
                                  qmap[0][:, :, h, :].bitcast(F32), ALU.subtract).then_inc(q_low_ready, 1)


def make_queries(nc, sem, qmap, gmap, cos_q, sin_q, xnt, queries, tag):
    units = S // SG * NP
    with ExitStack() as ctx:
        def sb(name, shape):
            return ctx.enter_context(nc.sbuf_tensor(f"{tag}_{name}", shape, F32))

        turned = [sb(f"turned{n}", [QC, 2, 2, SG, CD]) for n in range(2)]
        turned_high, turned_low = ([ctx.enter_context(nc.sbuf_tensor(f"{tag}_turned_{half}{n}", [QC, 2, 2, SG, CD], F32R)) for n in range(2)]
                                   for half in ("high", "low"))
        maps = [sb(f"maps{n}", [P, DC, SG, 2, CD]) for n in range(2)]
        map_ps = [ctx.enter_context(nc.psum_tensor(f"{tag}_map_ps{n}", [P, DC, SG, CD], F32)) for n in range(2)]
        query_ps = [ctx.enter_context(nc.psum_tensor(f"{tag}_query_ps{n}", [P, SG, B], F32)) for n in range(2)]
        cos_done, turned_ready, high_ready, low_ready = (
            sem(f"{tag}_cos_done"), sem(f"{tag}_turned_ready"), sem(f"{tag}_high_ready"), sem(f"{tag}_low_ready"))
        map_done = [sem(f"{tag}_map_done{n}") for n in range(2)]
        map_copied = [sem(f"{tag}_map_copied{n}") for n in range(2)]
        query_done, query_copied = sem(f"{tag}_query_done"), sem(f"{tag}_query_copied")
        block = ctx.enter_context(nc.Block())

        def half(t, n, k):
            return t[n % 2][:, k, :, :, :].rearrange("p e s d -> p (e s d)")

        @block.scalar
        def _(act):
            def step(at):
                for k in range(2):
                    if at(2):
                        u, n, g = at(2)
                        act.wait_ge(turned_ready, 2 * u + k + 1)
                        until(act, low_ready, 2 * u)
                        until(act, map_done[1], u - 1)
                        act.activation(half(turned_high, n, k), half(turned, n, k), ACT.Copy).then_inc(high_ready, 1)
                    if k == 0 and at(1):
                        u, n, g = at(1)
                        act.wait_ge(map_done[0], u + 1)
                        until(act, query_done, u - 1)
                        act.activation(maps[n % 2][:, :, :, 0, :], map_ps[0][:, :, :, :], ACT.Copy).then_inc(map_copied[0], 1)
                if at(3):
                    u, n, g = at(3)
                    for k in range(2):
                        for s in range(SG):
                            s_at = g * SG + s
                            last = act.activation(turned[n % 2][:, k, :, s, :], gmap[:, k, 2 * n:2 * n + 2, :], ACT.Copy,
                                                  scale=cos_q[:, k, bass.ds(s_at, 1)])
                        last.then_inc(cos_done, 1)
            steps(act, step, units, NP, 3, 0)

        @block.gpsimd
        def _(pool):
            def step(at):
                if at(2):
                    u, n, g = at(2)
                    for k in range(2):
                        pool.wait_ge(high_ready, 2 * u + k + 1)
                        until(pool, map_done[1], u - 1)
                        pool.tensor_tensor(half(turned_low, n, k), half(turned, n, k), half(turned_high, n, k).bitcast(F32),
                                           ALU.subtract).then_inc(low_ready, 1)
            steps(pool, step, units, NP, 2, 0)

        @block.vector
        def _(dve):
            def step(at):
                if at(1):
                    u, n, g = at(1)
                    dve.wait_ge(map_done[1], u + 1)
                    until(dve, query_done, u - 1)
                    dve.tensor_copy(maps[n % 2][:, :, :, 1, :], map_ps[1][:, :, :, :]).then_inc(map_copied[1], 1)
                if at(3):
                    u, n, g = at(3)
                    for k in range(2):
                        dve.wait_ge(cos_done, 2 * u + k + 1)
                        for s in range(SG):
                            s_at = g * SG + s
                            out = turned[n % 2][:, k, :, s, :]
                            last = dve.scalar_tensor_tensor(out, gmap[:, 1 - k, 2 * n:2 * n + 2, :], sin_q[:, k, bass.ds(s_at, 1)],
                                                            out, ALU.mult, ALU.add)
                        last.then_inc(turned_ready, 1)
                if at(0):
                    u, n, g = at(0)
                    dve.wait_ge(query_done, u + 1)
                    s_at = g * SG
                    dve.tensor_copy(queries[:, n, bass.ds(s_at, SG), :], query_ps[n % 2][:, :, :]).then_inc(query_copied, 1)
            steps(dve, step, units, NP, 3, 0)

        @block.tensor
        def _(pe):
            def step(at):
                if at(1):
                    u, n, g = at(1)
                    for e in range(2):
                        until(pe, map_copied[e], u)
                        for k in range(2):
                            if e == 0:
                                pe.wait_ge(high_ready, 2 * u + k + 1)
                                pe.wait_ge(low_ready, 2 * u + k + 1)
                            for m in range(DC):
                                last = split_product(pe, map_ps[e][:, m, :, :], [half[:, k, 2 * n + e, m * P:(m + 1) * P] for half in qmap],
                                                     [half[n % 2][:, k, e, :, :] for half in (turned_high, turned_low)],
                                                     k == 0 and m == 0, k == 1, skip_group_check=True)
                        last.then_inc(map_done[e], 1)
                if at(0):
                    u, n, g = at(0)
                    for e in range(2):
                        pe.wait_ge(map_copied[e], u + 1)
                    until(pe, query_copied, u - 1)
                    for s in range(SG):
                        s_at = g * SG + s
                        for m in range(DC):
                            last = pe.matmul(query_ps[n % 2][:, s, :], maps[n % 2][:, m, s, :, :],
                                             xnt[:, m, bass.ds(s_at, 1), :], start=m == 0, stop=m == DC - 1)
                    last.then_inc(query_done, 1)
            steps(pe, step, units, NP, 1, 0)


def attend(nc, sem, w, x_sb, queries, omap, cos_k, sin_k, ident, tag, stats=None, ahead=()):
    with ExitStack() as ctx:
        def sb(name, shape):
            return ctx.enter_context(nc.sbuf_tensor(f"{tag}_{name}", shape, F32))

        def ps(name, shape):
            return ctx.enter_context(nc.psum_tensor(f"{tag}_{name}", shape, F32))

        raw = [sb(f"raw{n}", [LN, LC, CD]) for n in range(4)]
        swap = sb("swap", [LN, LC, CD])
        direct = sb("direct", [LN, LC, CD])
        keys = [sb(f"keys{n}", [P, LC, 2, CD]) for n in range(4)]
        keys_high, keys_low, query_high, query_low = (
            [ctx.enter_context(nc.sbuf_tensor(f"{tag}_{name}{n}", shape, F32R)) for n in range(2)]
            for name, shape in (("keys_high", [P, LC * LN]), ("keys_low", [P, LC * LN]),
                                ("query_high", [P, 2, NP * S]), ("query_low", [P, 2, NP * S])))
        peak = sb("peak", [P, 2, 2])
        total = sb("total", [P, 2, 2])
        inverse = sb("inverse", [P, 2, 2])
        weights = [sb(f"weights{n}", [P, 2, LC * LN]) for n in range(2)]
        weights_t = [sb(f"weights_t{n}", [P, 2, LC, P]) for n in range(2)]
        context = [sb(f"context{n}", [P, 2, CD]) for n in range(2)]
        context_t = sb("context_t", [P, NP, BT, S])

        turn_ps = ps("turn_ps", [P, 512])
        score_ps = [ps(f"score_ps{n}", [P, 2, 512]) for n in range(2)]
        project_ps = score_ps[1][:, :, 512 - P:512]
        weight_ps = ps("weight_ps", [P, 2, 512])
        sum_ps = ps("sum_ps", [P, 512])

        raw_loaded = [sem(f"{tag}_raw_loaded{n}") for n in range(4)]
        names = ("cleared", "rows_cleared", "product", "swapped", "keys_ready",
                 "query0_high_ready", "query0_low_ready", "query1_high_ready", "query1_low_ready", "keys_low_ready", "keys_turned", "keys_t_ready", "scored", "peak_ready",
                 "padded", "weighed", "weights_turned", "weights_t0", "weights_t1", "summed", "inverted", "context_ready",
                 "context_turned", "context_t_ready", "projected", "added", "stats_done", "ahead_loaded")
        s = {n: sem(f"{tag}_{n}") for n in names}
        block = ctx.enter_context(nc.Block())

        def of_pairs(ap):
            return ap.rearrange("p (a s) -> p a s", a=NP)

        @block.sync
        def _(sp):
            sp.wait_ge(s["cleared"], 1)
            def step(at):
                if at(4):
                    u, n, g = at(4)
                    until(sp, s["product"], u - 3)
                    until(sp, s["swapped"], u - 3)
                    full = (LC - 1) * LN
                    kv = w["ctx"][bass.ds(u, 1), :, :]
                    sp.dma_start(raw[n][:, 0:LC - 1, :], kv[:, 0:full, :].rearrange("o (c p) d -> p (o c) d", p=LN)).then_inc(raw_loaded[n], 16)
                    sp.dma_start(raw[n][0:L - full, LC - 1, :], kv[:, full:L, :].rearrange("o p d -> p (o d)")).then_inc(raw_loaded[n], 16)
                if at(0) and isinstance(at(0)[0], int) and at(0)[0] < len(ahead):
                    to, source = ahead[at(0)[0]]
                    sp.dma_start(to, source).then_inc(s["ahead_loaded"], 16)
            steps(sp, step, B, 4, 4, 0)
            until(sp, s["ahead_loaded"], 16 * len(ahead))

        @block.gpsimd
        def _(pool):
            for n in range(4):
                last = pool.memset(raw[n][:, LC - 1, :], 0.0)
            last.then_inc(s["cleared"], 1)
            for t in keys:
                pool.memset(t[:, :, :, :], 0.0)
            for t in query_high + query_low:
                last = pool.memset(t[:, :, :].bitcast(F32), 0.0)
            last.then_inc(s["rows_cleared"], 1)
            pool.wait_ge(s["rows_cleared"], 1)

            def step(at):
                if at(2):
                    u, n, g = at(2)
                    pool.wait_ge(s["query0_high_ready"], u + 1)
                    until(pool, s["scored"], u - 1)
                    pool.tensor_tensor(of_pairs(query_low[n % 2][0:CD, 0, :]), queries[0:CD, :, :, bass.ds(u, 1)].rearrange("p a s o -> p a (s o)"),
                                       of_pairs(query_high[n % 2][0:CD, 0, :].bitcast(F32)), ALU.subtract).then_inc(s["query0_low_ready"], 1)
                if at(3):
                    u, n, g = at(3)
                    pool.wait_ge(raw_loaded[n], g * 32 + 32)
                    until(pool, s["keys_ready"], u)
                    h = CD // 2
                    pool.tensor_tensor(direct[:, :, :], raw[n][:, :, :], cos_k[:, :, :], ALU.mult).then_inc(s["product"], 1)
                    pool.tensor_tensor(swap[:, :, 0:h], raw[n][:, :, h:CD], sin_k[:, :, 0:h], ALU.mult)
                    pool.tensor_tensor(swap[:, :, h:CD], raw[n][:, :, 0:h], sin_k[:, :, h:CD], ALU.mult).then_inc(s["swapped"], 1)
                    pool.wait_ge(s["product"], u + 1)
                    pool.wait_ge(s["swapped"], u + 1)
                    until(pool, s["summed"], u - 3)
                    for e in range(2):
                        last = pool.tensor_tensor(keys[n][0:LN, :, e, :], direct[:, :, :], swap[:, :, :], ALU.add)
                    last.then_inc(s["keys_ready"], 1)
            steps(pool, step, B, 4, 3, 0)

        @block.tensor
        def _(pe):
            def step(at):
                if at(1):
                    u, n, g = at(1)
                    pe.wait_ge(s["keys_t_ready"], u + 1)
                    pe.wait_ge(s["keys_low_ready"], u + 1)
                    pe.wait_ge(s["query0_low_ready"], u + 1)
                    pe.wait_ge(s["query1_low_ready"], u + 1)
                    until(pe, s["weighed"], u - 1)
                    if n == BT - 1:
                        until(pe, s["added"], g)
                    for e in range(2):
                        last = split_product(pe, score_ps[n % 2][:, e, 0:LC * LN], (query_high[n % 2][:, e, :], query_low[n % 2][:, e, :]),
                                             (keys_high[n % 2][:, :], keys_low[n % 2][:, :]), True, True)
                    last.then_inc(s["scored"], 1)
                if at(-2):
                    u, n, g = at(-2)
                    pe.wait_ge(s["context_ready"], u + 1)
                    pe.wait_ge(s["keys_low_ready"], min(u + 4, B) if isinstance(u, int) else u + 4)
                    until(pe, s["context_t_ready"], u)
                    pe.transpose(turn_ps[:, 0:P], context[n % 2][:, :, :].rearrange("p e d -> p (e d)"), ident[:, :]).then_inc(s["context_turned"], 1)
                if at(0):
                    u, n, g = at(0)
                    pe.wait_ge(s["weighed"], u + 1)
                    until(pe, s["weights_t0"], u)
                    until(pe, s["weights_t1"], u)
                    for e in range(2):
                        for c in range(LC):
                            last = pe.transpose(weight_ps[0:LN, e, c * P:(c + 1) * P], weights[n % 2][:, e, c * LN:(c + 1) * LN], ident[:, :])
                    last.then_inc(s["weights_turned"], 1)
                if at(2):
                    u, n, g = at(2)
                    pe.wait_ge(s["keys_ready"], u + 1)
                    until(pe, s["keys_low_ready"], u)
                    until(pe, s["context_t_ready"], u - 3)
                    for c in range(LC):
                        last = pe.transpose(turn_ps[:, c * LN:(c + 1) * LN], keys[n][0:LN, c, :, :].rearrange("p e d -> p (e d)"),
                                            ident[0:LN, 0:LN])
                    last.then_inc(s["keys_turned"], 1)
                if at(-2) and at(-2)[1] == BT - 1:
                    u, n, g = at(-2)
                    pe.wait_ge(s["context_t_ready"], u + 1)
                    pe.wait_ge(s["weighed"], min(u + 3, B) if isinstance(u, int) else u + 3)
                    for c in range(DC):
                        for a in range(NP):
                            last = pe.matmul(project_ps[:, c, :], context_t[:, a, :, :], omap[:, a, c * P:(c + 1) * P],
                                             start=a == 0, stop=a == NP - 1)
                    last.then_inc(s["projected"], 1)
                if at(-1):
                    u, n, g = at(-1)
                    pe.wait_ge(s["weights_t0"], u + 1)
                    pe.wait_ge(s["weights_t1"], u + 1)
                    until(pe, s["context_ready"], u)
                    for e in range(2):
                        for c in range(LC):
                            last = pe.matmul(sum_ps[:, e * CD:(e + 1) * CD], weights_t[n % 2][:, e, c, :], keys[n][:, c, 0, :],
                                             start=c == 0, stop=c == LC - 1)
                    last.then_inc(s["summed"], 1)
            pe.wait_ge(s["padded"], 1)
            pe.wait_ge(s["rows_cleared"], 1)
            steps(pe, step, B, 4, 2, 2)

        @block.scalar
        def _(act):
            act.wait_ge(s["padded"], 1)
            act.wait_ge(s["rows_cleared"], 1)

            def step(at):
                if at(2):
                    u, n, g = at(2)
                    act.activation(of_pairs(query_high[n % 2][0:CD, 0, :]), queries[0:CD, :, :, bass.ds(u, 1)].rearrange("p a s o -> p a (s o)"),
                                   ACT.Copy).then_inc(s["query0_high_ready"], 1)
                if at(-2):
                    u, n, g = at(-2)
                    act.wait_ge(s["context_turned"], u + 1)
                    if n == 0:
                        until(act, s["projected"], g)
                    act.activation(context_t[:, :, n, :], turn_ps[:, 0:P].rearrange("p (a s) -> p a s", a=NP), ACT.Copy).then_inc(s["context_t_ready"], 1)
                if at(2):
                    u, n, g = at(2)
                    act.wait_ge(s["keys_turned"], u + 1)
                    until(act, s["scored"], u - 1)
                    until(act, s["keys_low_ready"], u - 1)
                    act.activation(keys_high[n % 2][:, :], turn_ps[:, 0:LC * LN], ACT.Copy).then_inc(s["keys_t_ready"], 1)
                if at(0):
                    u, n, g = at(0)
                    act.wait_ge(s["weights_turned"], u + 1)
                    until(act, s["summed"], u - 1)
                    act.activation(weights_t[n % 2][0:LN, 0, :, :], weight_ps[0:LN, 0, 0:LC * P].rearrange("p (c q) -> p c q", c=LC), ACT.Copy).then_inc(s["weights_t0"], 1)
                if at(1):
                    u, n, g = at(1)
                    act.wait_ge(s["peak_ready"], u + 1)
                    until(act, s["weights_turned"], u - 1)
                    until(act, s["inverted"], u - 1)
                    for e in range(2):
                        last = act.activation(weights[n % 2][:, e, 0:L], score_ps[n % 2][:, e, 0:L], ACT.Exp, bias=peak[:, n % 2, e:e + 1],
                                              accum_out=total[:, n % 2, e:e + 1])
                    last.then_inc(s["weighed"], 1)
            steps(act, step, B, 4, 2, 2)

        @block.vector
        def _(dve):
            for n in range(2):
                dve.memset(weights_t[n][:, :, :, :], 0.0)
                last = dve.memset(weights[n][:, :, L:LC * LN], 0.0)
            last.then_inc(s["padded"], 1)
            dve.wait_ge(s["padded"], 1)
            dve.wait_ge(s["rows_cleared"], 1)

            def step(at):
                if at(-1):
                    u, n, g = at(-1)
                    dve.wait_ge(s["weighed"], u + 1)
                    dve.reciprocal(inverse[:, n % 2, :], total[:, n % 2, :]).then_inc(s["inverted"], 1)
                if at(2):
                    u, n, g = at(2)
                    until(dve, s["scored"], u - 1)
                    mine = queries[CD:P, :, :, bass.ds(u, 1)].rearrange("p a s o -> p a (s o)")
                    dve.tensor_scalar(of_pairs(query_high[n % 2][CD:P, 1, :]), mine, 1.0, None, ALU.mult).then_inc(s["query1_high_ready"], 1)
                    dve.wait_ge(s["query1_high_ready"], u + 1)
                    dve.tensor_tensor(of_pairs(query_low[n % 2][CD:P, 1, :]), mine, of_pairs(query_high[n % 2][CD:P, 1, :].bitcast(F32)),
                                      ALU.subtract).then_inc(s["query1_low_ready"], 1)
                if at(1):
                    u, n, g = at(1)
                    dve.wait_ge(s["scored"], u + 1)
                    until(dve, s["weighed"], u - 1)
                    dve.tensor_reduce(peak[:, n % 2, :], score_ps[n % 2][:, :, 0:L], X, ALU.max, negate=True).then_inc(s["peak_ready"], 1)
                if at(0):
                    u, n, g = at(0)
                    dve.wait_ge(s["weights_turned"], u + 1)
                    until(dve, s["summed"], u - 1)
                    dve.tensor_copy(weights_t[n % 2][0:LN, 1, :, :], weight_ps[0:LN, 1, 0:LC * P].rearrange("p (c q) -> p c q", c=LC)).then_inc(s["weights_t1"], 1)
                if at(2):
                    u, n, g = at(2)
                    dve.wait_ge(s["keys_t_ready"], u + 1)
                    dve.tensor_tensor(keys_low[n % 2][:, :], turn_ps[:, 0:LC * LN], keys_high[n % 2][:, :].bitcast(F32),
                                      ALU.subtract).then_inc(s["keys_low_ready"], 1)
                if at(-2) and at(-2)[1] == BT - 1:
                    u, n, g = at(-2)
                    dve.wait_ge(s["projected"], g + 1)
                    rows = x_sb[:, g, :].rearrange("p (c d) -> p c d", c=DC)
                    dve.tensor_tensor(rows, project_ps, rows, ALU.add).then_inc(s["added"], 1)
                    if stats is not None:
                        dve.wait_ge(s["added"], g + 1)
                if at(-1):
                    u, n, g = at(-1)
                    dve.wait_ge(s["summed"], u + 1)
                    dve.wait_ge(s["inverted"], u + 1)
                    until(dve, s["context_turned"], u - 1)
                    dve.tensor_tensor(context[n % 2][:, :, :], sum_ps[:, 0:2 * CD].rearrange("p (e d) -> p e d", e=2),
                                      inverse[:, n % 2, :].unsqueeze(2).to_broadcast([P, 2, CD]), ALU.mult).then_inc(s["context_ready"], 1)
                if stats is not None and at(-2) and at(-2)[1] == BT - 1:
                    u, n, g = at(-2)
                    dve.bn_stats(stats[:, g, :], x_sb[:, g, :]).then_inc(s["stats_done"], 1)
            steps(dve, step, B, 4, 2, 2)



def split_weights(sem, block, ctx, nc, w, raw, wo_split, norm_w, others, tag):
    wo = ctx.enter_context(nc.sbuf_tensor(f"{tag}_wo", [DV, AH, D], F32))
    scaled = ctx.enter_context(nc.sbuf_tensor(f"{tag}_norm_w", [DV, 1], F32))
    wo_loaded, wo_scaled = sem(f"{tag}_wo_loaded"), sem(f"{tag}_wo_scaled")
    high_ready, low_ready, others_loaded = sem(f"{tag}_high_ready"), sem(f"{tag}_low_ready"), sem(f"{tag}_others_loaded")
    parts = raw + [(wo, wo_split)]

    @block.sync
    def _(sp):
        sp.dma_start(wo[:, :, :], w["awo"].rearrange("(h v) n -> v h n", v=DV)).then_inc(wo_loaded, 16)
        sp.dma_start(scaled[:, :], norm_w.rearrange("(v o) -> v o", o=1)).then_inc(wo_loaded, 16)
        for to, source in others:
            sp.dma_start(to[:, :, :], source.rearrange("(c p) n -> p c n", p=P)).then_inc(others_loaded, 16)
        sp.wait_ge(others_loaded, 16 * len(others))

    @block.gpsimd
    def _(pool):
        pool.wait_ge(wo_loaded, 32)
        pool.tensor_scalar(wo[:, :, :], wo[:, :, :], scaled[:, 0:1], 0.5, ALU.mult, ALU.mult).then_inc(wo_scaled, 1)

    @block.scalar
    def _(act):
        for k, (full, (high, low)) in enumerate(parts):
            if k == len(raw):
                act.wait_ge(wo_scaled, 1)
            act.activation(high[:, :, :], full[:, :, :], ACT.Copy).then_inc(high_ready, 1)

    @block.vector
    def _(dve):
        for k, (full, (high, low)) in enumerate(parts):
            dve.wait_ge(high_ready, k + 1)
            dve.tensor_tensor(low[:, :, :], full[:, :, :], high[:, :, :].bitcast(F32), ALU.subtract).then_inc(low_ready, 1)


def slot_attention(nc, sem, w, x_sb, mean, rstd, ident, mask, weights, wide, stats, tag="s"):
    units = NT * NG
    with ExitStack() as ctx:
        def sb(name, shape):
            return ctx.enter_context(nc.sbuf_tensor(f"{tag}_{name}", shape, F32))

        def ring(name, n, shape):
            return [sb(f"{name}{k}", shape) for k in range(n)]

        def ps(name, shape):
            return ctx.enter_context(nc.psum_tensor(f"{tag}_{name}", shape, F32))

        GK, GM, GV = GH * DK, GH * M, GH * DV
        wq, wk, ws, wv, wg, wo = weights
        mask_q = sb("mask_q", [P, P])

        used = [0]

        def carve(count):
            used[0] += count
            return [wide[:, k * GV:(k + 1) * GV] for k in range(used[0] - count, used[0])]

        values, gate = carve(4), carve(4)
        qk = [t.rearrange("p (a j r) -> p a j r", a=2, j=2) for t in carve(2)]
        tanh, squares, heads = carve(3)
        first, second = (t.rearrange("p (e j r) -> p e j r", e=2, j=2) for t in carve(2))

        rows = sb("rows", [P, D])
        rows_t = sb("rows_t", [P, DC, P])
        rows_high, rows_low = (ctx.enter_context(nc.sbuf_tensor(f"{tag}_rows_{n}", [P, DC, P], F32R)) for n in ("high", "low"))
        slots = ring("slots", 2, [P, GM])
        slots_high, slots_low = (ctx.enter_context(nc.sbuf_tensor(f"{tag}_slots_{n}", [P, GM], F32R)) for n in ("high", "low"))
        mask_exact = ctx.enter_context(nc.sbuf_tensor(f"{tag}_mask_exact", [P, P], F32R))
        slots_t = ring("slots_t", 2, [P, 2, P])
        inv_z = ring("inv_z", 2, [P, GM])
        ok = sb("ok", [P, GM])
        peak = sb("peak", [P, GH])
        prob = sb("prob", [P, GM])
        total = ring("total", 2, [P, GH])
        prob_z = sb("prob_z", [P, GM])
        prob_t = sb("prob_t", [P, 2, P])
        square_sum, eps_sum, mean_sq, root = (sb(n, [P, GH]) for n in ("square_sum", "eps_sum", "mean_sq", "root"))
        minus_half = sb("power", [P, GH])
        heads_high, heads_low = (ctx.enter_context(nc.sbuf_tensor(f"{tag}_heads_{n}", [P, GH, P], F32R)) for n in ("high", "low"))

        s_ps, qk_ps, vg_ps, out_ps = ps("s_ps", [P, 512]), ps("qk_ps", [P, 512]), ps("vg_ps", [P, 512]), ps("out_ps", [P, 512])
        pair_ps = ps("pair_ps", [P, 2, 512])
        slot_ps = ps("slot_ps", [P, 512])
        head_ps = ps("head_ps", [P, 512])

        names = ("stats_done", "slots_high_ready", "slots_low_ready", "mask_exact_ready", "rows_high_ready", "rows_low_ready", "heads_high_ready", "heads_low_ready", "mask_ready", "power_ready",
                 "rows_ready", "rows_turned", "rows_t_ready", "s_done", "clipped_ready", "slots_ready",
                 "qk_done", "qk_ready", "v_done", "v_ready", "g_done", "tanh_ready", "gate_ready",
                 "z_done", "inv_z_ready", "first_done", "first_ready", "slots_turned", "slots_t_ready",
                 "ok_done", "ok_ready", "peak_ready", "shifted_ready", "prob_ready", "total_ready", "prob_z_ready",
                 "prob_turned", "prob_t_ready", "second_done", "second_ready", "head_done", "squared", "eps_ready",
                 "mean_sq_ready", "root_ready", "heads_ready", "heads_turned", "projected", "added")
        s = {n: sem(f"{tag}_{n}") for n in names}
        block = ctx.enter_context(nc.Block())

        def upto(n):
            return min(n, units) if isinstance(n, int) else n

        def by_head(ap, width):
            return ap.rearrange("p (h k) -> p h k", k=width)

        def over(ap, width):
            return ap.unsqueeze(2).to_broadcast([P, GH, width])

        @block.gpsimd
        def _(pool):
            pool.memset(minus_half[:, :], -0.5).then_inc(s["power_ready"], 1)
            pool.wait_ge(s["power_ready"], 1)

            def step(at):
                if at(-1):
                    u, n, g = at(-1)
                    pool.wait_ge(s["prob_ready"], u + 1)
                    until(pool, s["prob_turned"], u)
                    pool.tensor_tensor(prob_z[:, :], prob[:, :], inv_z[n % 2][:, :], ALU.mult).then_inc(s["prob_z_ready"], 1)
                if at(-2):
                    u, n, g = at(-2)
                    pool.wait_ge(s["mean_sq_ready"], u + 1)
                    until(pool, s["heads_ready"], u)
                    pool.tensor_tensor(root[:, :], mean_sq[:, :], minus_half[:, :], ALU.pow).then_inc(s["root_ready"], 1)
                if at(1):
                    u, n, g = at(1)
                    pool.wait_ge(s["slots_high_ready"], u + 1)
                    until(pool, s["z_done"], u)
                    pool.tensor_tensor(slots_low[:, :], slots[n % 2][:, :], slots_high[:, :].bitcast(F32), ALU.subtract).then_inc(s["slots_low_ready"], 1)
                if at(2) and at(2)[1] == 0:
                    u, n, g = at(2)
                    pool.wait_ge(s["rows_t_ready"], g + 1)
                    pool.wait_ge(s["rows_high_ready"], g + 1)
                    pool.wait_ge(s["rows_high_ready"], g + 1)
                    pool.tensor_tensor(rows_low[:, :, :], rows_t[:, :, :], rows_high[:, :, :].bitcast(F32), ALU.subtract).then_inc(s["rows_low_ready"], 1)
            steps(pool, step, units, NG, 2, 2)

        @block.tensor
        def _(pe):
            pe.wait_ge(s["mask_exact_ready"], 1)

            def step(at):
                if at(1):
                    u, n, g = at(1)
                    pe.wait_ge(s["rows_t_ready"], g + 1)
                    until(pe, s["inv_z_ready"], u - 1)
                    until(pe, s["clipped_ready"], u)
                    for c in range(DC):
                        last = pe.matmul(s_ps[:, 0:GM], rows_t[:, c, :], ws[:, c, n * GM:(n + 1) * GM], start=c == 0, stop=c == DC - 1)
                    last.then_inc(s["s_done"], 1)
                    until(pe, s["qk_ready"], u)
                    until(pe, s["heads_high_ready"], u - 3)
                    until(pe, s["heads_low_ready"], u - 3)
                    for a, weight in enumerate((wq, wk)):
                        for j in range(2):
                            for c in range(DC):
                                last = pe.matmul(qk_ps[:, (2 * a + j) * P:(2 * a + j + 1) * P],
                                                 weight[:, c, n * GK + j * P:n * GK + (j + 1) * P], rows_t[:, c, :],
                                                 start=c == 0, stop=c == DC - 1)
                    last.then_inc(s["qk_done"], 1)
                if at(-2):
                    u, n, g = at(-2)
                    pe.wait_ge(s["second_ready"], u + 1)
                    pe.wait_ge(s["v_ready"], u + 1)
                    until(pe, s["heads_ready"], u)
                    for h in range(GH):
                        last = pe.matmul(head_ps[:, h * DV:(h + 1) * DV], second[:, h % 2, h // 2, :],
                                         values[n][:, h * DV:(h + 1) * DV], start=True, stop=True)
                    last.then_inc(s["head_done"], 1)
                if at(0):
                    u, n, g = at(0)
                    pe.wait_ge(s["slots_ready"], u + 1)
                    pe.wait_ge(s["clipped_ready"], upto(u + 2))
                    until(pe, s["inv_z_ready"], u)
                    pe.wait_ge(s["slots_high_ready"], u + 1)
                    pe.wait_ge(s["slots_low_ready"], u + 1)
                    pe.matmul(s_ps[:, 256:256 + GM], mask_exact[:, :], slots_low[:, :], start=True, stop=False)
                    pe.matmul(s_ps[:, 256:256 + GM], mask_exact[:, :], slots_high[:, :], start=False, stop=True).then_inc(s["z_done"], 1)
                    pe.wait_ge(s["qk_ready"], u + 1)
                    until(pe, s["second_ready"], u - 1)
                    until(pe, s["first_ready"], u)
                    for j in range(2):
                        for e in range(2):
                            a = e * DK
                            last = pe.matmul(pair_ps[:, e, j * P:(j + 1) * P], qk[n % 2][a:a + DK, 1, j, :], qk[n % 2][a:a + DK, 0, j, :],
                                             start=True, stop=True)
                    last.then_inc(s["first_done"], 1)
                    until(pe, s["ok_ready"], u)
                    for j in range(2):
                        last = pe.transpose(slot_ps[:, j * P:(j + 1) * P], slots[n % 2][:, j * P:(j + 1) * P], ident[:, :])
                    last.then_inc(s["slots_turned"], 1)
                if at(1):
                    u, n, g = at(1)
                    until(pe, s["gate_ready"], u)
                    pe.wait_ge(s["rows_low_ready"], g + 1)
                    for c in range(DC):
                        last = split_product(pe, vg_ps[:, :], (rows_high[:, c, :], rows_low[:, c, :]),
                                             [half[:, c, n * GV:(n + 1) * GV] for half in wv], c == 0, c == DC - 1)
                    last.then_inc(s["v_done"], 1)
                if at(-3):
                    u, n, g = at(-3)
                    pe.wait_ge(s["heads_high_ready"], u + 1)
                    pe.wait_ge(s["heads_low_ready"], u + 1)
                    if n == 0:
                        until(pe, s["added"], g)
                    for h in range(GH):
                        last = split_product(pe, out_ps[:, 0:D], (heads_high[:, h, :], heads_low[:, h, :]),
                                             [half[:, n * GH + h, :] for half in wo], n == 0 and h == 0, n == NG - 1 and h == GH - 1)
                    last.then_inc(s["projected"], 1)
                if at(-1):
                    u, n, g = at(-1)
                    pe.wait_ge(s["prob_z_ready"], u + 1)
                    pe.wait_ge(s["slots_t_ready"], upto(u + 2))
                    for j in range(2):
                        last = pe.transpose(slot_ps[:, j * P:(j + 1) * P], prob_z[:, j * P:(j + 1) * P], ident[:, :])
                    last.then_inc(s["prob_turned"], 1)
                if at(1):
                    u, n, g = at(1)
                    pe.wait_ge(s["v_ready"], u + 1)
                    for c in range(DC):
                        last = split_product(pe, vg_ps[:, :], (rows_high[:, c, :], rows_low[:, c, :]),
                                             [half[:, c, n * GV:(n + 1) * GV] for half in wg], c == 0, c == DC - 1)
                    last.then_inc(s["g_done"], 1)
                if at(2) and at(2)[1] == 0:
                    u, n, g = at(2)
                    pe.wait_ge(s["rows_ready"], g + 1)
                    until(pe, s["inv_z_ready"], u - 1)
                    for c in range(DC):
                        last = pe.transpose(s_ps[:, c * P:(c + 1) * P], rows[:, c * P:(c + 1) * P], ident[:, :])
                    last.then_inc(s["rows_turned"], 1)
                if at(-2):
                    u, n, g = at(-2)
                    pe.wait_ge(s["heads_ready"], u + 1)
                    pe.wait_ge(s["qk_ready"], upto(u + 4))
                    until(pe, s["heads_high_ready"], u)
                    until(pe, s["heads_low_ready"], u)
                    for h in range(GH):
                        last = pe.transpose(qk_ps[:, h * P:(h + 1) * P], heads[:, h * DV:(h + 1) * DV], ident[:, :])
                    last.then_inc(s["heads_turned"], 1)
                if at(0):
                    u, n, g = at(0)
                    pe.wait_ge(s["first_ready"], u + 1)
                    pe.wait_ge(s["slots_t_ready"], u + 1)
                    until(pe, s["prob_t_ready"], u)
                    for h in range(GH):
                        last = pe.matmul(slot_ps[:, 256 + h * M:256 + (h + 1) * M], first[:, h % 2, h // 2, :],
                                         slots[n % 2][:, h * M:(h + 1) * M], start=True, stop=True)
                    last.then_inc(s["ok_done"], 1)
                if at(-1):
                    u, n, g = at(-1)
                    pe.wait_ge(s["prob_t_ready"], u + 1)
                    pe.wait_ge(s["first_ready"], upto(u + 2))
                    until(pe, s["second_ready"], u)
                    for j in range(2):
                        for e in range(2):
                            a = e * M
                            last = pe.matmul(pair_ps[:, e, j * P:(j + 1) * P], slots_t[n % 2][a:a + M, j, :], prob_t[a:a + M, j, :],
                                             start=True, stop=True)
                    last.then_inc(s["second_done"], 1)
            steps(pe, step, units, NG, 2, 3)

        @block.scalar
        def _(act):
            def step(at):
                if at(-1):
                    u, n, g = at(-1)
                    act.wait_ge(s["shifted_ready"], u + 1)
                    until(act, s["prob_z_ready"], u)
                    until(act, s["total_ready"], u)
                    act.activation(prob[:, :], ok[:, :], ACT.Exp).then_inc(s["prob_ready"], 1)
                if at(1):
                    u, n, g = at(1)
                    act.wait_ge(s["qk_done"], u + 1)
                    until(act, s["first_done"], u - 1)
                    act.activation(qk[n % 2][:, :, :, :], qk_ps[:, :].rearrange("p (a j r) -> p a j r", a=2, j=2), ACT.Copy).then_inc(s["qk_ready"], 1)
                    act.wait_ge(s["clipped_ready"], u + 1)
                    act.activation(slots[n % 2][:, :], slots[n % 2][:, :], ACT.Exp).then_inc(s["slots_ready"], 1)
                if at(-2):
                    u, n, g = at(-2)
                    act.wait_ge(s["head_done"], u + 1)
                    until(act, s["mean_sq_ready"], u)
                    for h in range(GH):
                        last = act.activation(squares[:, h * DV:(h + 1) * DV], head_ps[:, h * DV:(h + 1) * DV], ACT.Square, accum_out=square_sum[:, h:h + 1])
                    last.then_inc(s["squared"], 1)
                if at(0):
                    u, n, g = at(0)
                    act.wait_ge(s["slots_turned"], u + 1)
                    until(act, s["second_done"], u - 1)
                    act.activation(slots_t[n % 2][:, :, :], slot_ps[:, 0:GM].rearrange("p (j r) -> p j r", j=2), ACT.Copy).then_inc(s["slots_t_ready"], 1)
                if at(1):
                    u, n, g = at(1)
                    act.wait_ge(s["slots_ready"], u + 1)
                    until(act, s["z_done"], u)
                    until(act, s["slots_low_ready"], u)
                    act.activation(slots_high[:, :], slots[n % 2][:, :], ACT.Copy).then_inc(s["slots_high_ready"], 1)
                if at(1):
                    u, n, g = at(1)
                    act.wait_ge(s["v_done"], u + 1)
                    until(act, s["head_done"], u - 3)
                    act.activation(values[n][:, :], vg_ps[:, :], ACT.Copy).then_inc(s["v_ready"], 1)
                if at(-1):
                    u, n, g = at(-1)
                    act.wait_ge(s["prob_turned"], u + 1)
                    until(act, s["second_done"], u)
                    act.activation(prob_t[:, :, :], slot_ps[:, 0:GM].rearrange("p (j r) -> p j r", j=2), ACT.Copy).then_inc(s["prob_t_ready"], 1)
                if at(1):
                    u, n, g = at(1)
                    act.wait_ge(s["g_done"], u + 1)
                    until(act, s["gate_ready"], u)
                    act.activation(tanh[:, :], vg_ps[:, :], ACT.Tanh, scale=0.5).then_inc(s["tanh_ready"], 1)
                if at(2) and at(2)[1] == 0:
                    u, n, g = at(2)
                    act.wait_ge(s["rows_turned"], g + 1)
                    act.activation(rows_t[:, :, :], s_ps[:, 0:D].rearrange("p (c r) -> p c r", c=DC), ACT.Copy).then_inc(s["rows_t_ready"], 1)
                if at(-2):
                    u, n, g = at(-2)
                    act.wait_ge(s["heads_turned"], u + 1)
                    until(act, s["projected"], u)
                    until(act, s["heads_low_ready"], u)
                    act.activation(heads_high[:, :, :], qk_ps[:, :].rearrange("p (h r) -> p h r", h=GH), ACT.Copy).then_inc(s["heads_high_ready"], 1)
            steps(act, step, units, NG, 2, 2)

        @block.vector
        def _(dve):
            dve.tensor_scalar(mask_exact[:, :], mask[:, :], 1.0, None, ALU.mult).then_inc(s["mask_exact_ready"], 1)
            dve.tensor_scalar(mask_q[:, :], mask[:, :], float(DK) ** -0.5, None, ALU.mult).then_inc(s["mask_ready"], 1)
            dve.wait_ge(s["mask_ready"], 1)

            def step(at):
                if at(1):
                    u, n, g = at(1)
                    dve.wait_ge(s["s_done"], u + 1)
                    until(dve, s["ok_done"], u - 1)
                    dve.tensor_scalar(slots[n % 2][:, :], s_ps[:, 0:GM], -32.0, 32.0, ALU.max, ALU.min).then_inc(s["clipped_ready"], 1)
                if at(-4) and at(-4)[1] == NG - 1:
                    dve.wait_ge(s["added"], at(-4)[2] + 1)
                if at(-1):
                    u, n, g = at(-1)
                    dve.wait_ge(s["ok_done"], u + 1)
                    dve.wait_ge(s["inv_z_ready"], u + 1)
                    until(dve, s["prob_ready"], u)
                    dve.tensor_tensor(ok[:, :], slot_ps[:, 256:256 + GM], inv_z[n % 2][:, :], ALU.mult).then_inc(s["ok_ready"], 1)
                    dve.wait_ge(s["ok_ready"], u + 1)
                    dve.tensor_reduce(peak[:, :], by_head(ok[:, :], M), X, ALU.max).then_inc(s["peak_ready"], 1)
                    dve.wait_ge(s["peak_ready"], u + 1)
                    dve.tensor_tensor(by_head(ok[:, :], M), by_head(ok[:, :], M), over(peak[:, :], M), ALU.subtract).then_inc(s["shifted_ready"], 1)
                if at(-4) and at(-4)[1] == NG - 1:
                    u, n, g = at(-4)
                    dve.bn_stats(stats[:, g, :], x_sb[:, g, :]).then_inc(s["stats_done"], 1)
                if at(-1):
                    u, n, g = at(-1)
                    dve.wait_ge(s["prob_ready"], u + 1)
                    dve.tensor_reduce(total[n % 2][:, :], by_head(prob[:, :], M), X, ALU.add).then_inc(s["total_ready"], 1)
                if at(-2):
                    u, n, g = at(-2)
                    dve.wait_ge(s["total_ready"], u + 1)
                    dve.scalar_tensor_tensor(eps_sum[:, :], total[n % 2][:, :], EPS, total[n % 2][:, :], ALU.mult, ALU.mult).then_inc(s["eps_ready"], 1)
                    dve.wait_ge(s["squared"], u + 1)
                    dve.wait_ge(s["eps_ready"], u + 1)
                    until(dve, s["root_ready"], u)
                    dve.scalar_tensor_tensor(mean_sq[:, :], square_sum[:, :], 1.0 / DV, eps_sum[:, :], ALU.mult, ALU.add).then_inc(s["mean_sq_ready"], 1)
                if at(0):
                    u, n, g = at(0)
                    dve.wait_ge(s["first_done"], u + 1)
                    until(dve, s["ok_done"], u)
                    dve.tensor_tensor(first[:, :, :, :], pair_ps[:, :, 0:2 * P].rearrange("p e (j r) -> p e j r", j=2),
                                      mask_q[:, :].unsqueeze(1).unsqueeze(1).to_broadcast([P, 2, 2, P]), ALU.mult).then_inc(s["first_ready"], 1)
                    dve.wait_ge(s["z_done"], u + 1)
                    until(dve, s["prob_z_ready"], u - 1)
                    dve.reciprocal(inv_z[n % 2][:, :], s_ps[:, 256:256 + GM]).then_inc(s["inv_z_ready"], 1)
                if at(-2):
                    u, n, g = at(-2)
                    dve.wait_ge(s["root_ready"], u + 1)
                    dve.wait_ge(s["gate_ready"], u + 1)
                    until(dve, s["heads_turned"], u)
                    for h in range(GH):
                        col = slice(h * DV, (h + 1) * DV)
                        last = dve.scalar_tensor_tensor(heads[:, col], head_ps[:, col], root[:, h:h + 1], gate[n][:, col], ALU.mult, ALU.mult)
                    last.then_inc(s["heads_ready"], 1)
                if at(-2):
                    u, n, g = at(-2)
                    dve.wait_ge(s["heads_high_ready"], u + 1)
                    dve.tensor_tensor(heads_low[:, :, :], qk_ps[:, :].rearrange("p (h r) -> p h r", h=GH),
                                      heads_high[:, :, :].bitcast(F32), ALU.subtract).then_inc(s["heads_low_ready"], 1)
                if at(1):
                    u, n, g = at(1)
                    dve.wait_ge(s["tanh_ready"], u + 1)
                    dve.scalar_tensor_tensor(gate[n][:, :], tanh[:, :], 1.0, vg_ps[:, :], ALU.add, ALU.mult).then_inc(s["gate_ready"], 1)
                if at(2) and at(2)[1] == 0:
                    u, n, g = at(2)
                    dve.wait_ge(s["rows_t_ready"], g + 1)
                    dve.tensor_copy(rows_high[:, :, :], rows_t[:, :, :]).then_inc(s["rows_high_ready"], 1)
                if at(-1):
                    u, n, g = at(-1)
                    dve.wait_ge(s["second_done"], u + 1)
                    until(dve, s["head_done"], u)
                    dve.tensor_tensor(second[:, :, :, :], pair_ps[:, :, 0:2 * P].rearrange("p e (j r) -> p e j r", j=2),
                                      mask[:, :].unsqueeze(1).unsqueeze(1).to_broadcast([P, 2, 2, P]), ALU.mult).then_inc(s["second_ready"], 1)
                if at(-3) and at(-3)[1] == NG - 1:
                    u, n, g = at(-3)
                    dve.wait_ge(s["projected"], u + 1)
                    dve.tensor_tensor(x_sb[:, g, :], out_ps[:, 0:D], x_sb[:, g, :], ALU.add).then_inc(s["added"], 1)
                if at(3) and at(3)[1] == 0:
                    u, n, g = at(3)
                    until(dve, s["rows_turned"], g)
                    dve.tensor_scalar(rows[:, :], x_sb[:, g, :], mean[:, bass.ds(g, 1)], rstd[:, bass.ds(g, 1)],
                                      ALU.subtract, ALU.mult).then_inc(s["rows_ready"], 1)
            steps(dve, step, units, NG, 3, 4)



def route(nc, sem, w, rows_t, coef, mix, w2, b1, ident, experts_loaded, w1, w1_split, tag="r"):
    groups = NT // TG
    with ExitStack() as ctx:
        def sb(name, shape):
            return ctx.enter_context(nc.sbuf_tensor(f"{tag}_{name}", shape, F32))

        def ps(name, shape):
            return ctx.enter_context(nc.psum_tensor(f"{tag}_{name}", shape, F32))

        router_w, router_b, cost = sb("router_w", [P, DC, NE]), sb("router_b", [P, NE]), sb("cost", [P, NE])
        falling = sb("falling", [P, NE])
        flat = [sb(f"flat{n}", [NE, TG, P]) for n in range(2)]
        logits, prob = sb("logits", [P, NT, NE]), sb("prob", [P, NT, NE])
        peak, total, inverse = (sb(n, [P, NT]) for n in ("peak", "total", "inverse"))
        is_first, is_second = sb("is_first", [P, NT, NE]), sb("is_second", [P, NT, NE])
        p_first, p_second, gap, ratio, g_first, g_second = (
            sb(n, [P, NT]) for n in ("p_first", "p_second", "gap", "ratio", "g_first", "g_second"))
        b2 = sb("b2", [NE + 1, FL])
        b2_to = sb("b2_to", [NE + 1, NE + 2])
        gelu_b1 = sb("gelu_b1", [P, NCH])
        spread = sb("spread", [P, NCH, NE + 2])
        flat_ps = [ps(f"flat_ps{n}", [P, 512]) for n in range(2)]
        logit_ps = [ps(f"logit_ps{n}", [P, 512]) for n in range(2)]
        mix_ps = ps("mix_ps", [P, 512])

        names = ("loaded", "w1_high_ready", "w1_low_ready", "flat_done", "flat_ready", "logit_done", "logit_ready",
                 "w2_scaled", "chain", "shifted", "exp_done", "gap_ready", "ratio_done", "cleared", "gelu_done",
                 "spread_ready", "mix_done", "mix_ready")
        s = {n: sem(f"{tag}_{n}") for n in names}
        block = ctx.enter_context(nc.Block())

        @block.sync
        def _(sp):
            sp.dma_start(router_w[:, :, :], w["router_w"].rearrange("(c p) e -> p c e", p=P)).then_inc(s["loaded"], 16)
            for t, n in ((router_b, "router_b"), (cost, "cost")):
                sp.dma_start(t[:, :], w[n].partition_broadcast(P)).then_inc(s["loaded"], 16)
            sp.dma_start(falling[:, :], w["falling"].partition_broadcast(P)).then_inc(s["loaded"], 16)
            sp.dma_start(b2[:, :], w["b2"]).then_inc(s["loaded"], 16)
            sp.dma_start(b2_to[:, :], w["b2_to"]).then_inc(s["loaded"], 16)

        @block.gpsimd
        def _(pool):
            pool.memset(spread[:, :, :], 0.0).then_inc(s["cleared"], 1)
            pool.wait_ge(s["w1_high_ready"], 1)
            pool.tensor_tensor(w1_split[1][:, :, :], w1[:, :, :], w1_split[0][:, :, :].bitcast(F32), ALU.subtract).then_inc(s["w1_low_ready"], 1)

        @block.tensor
        def _(pe):
            pe.wait_ge(s["loaded"], 16 * 6)

            def step(at):
                if at(0):
                    u, n, g = at(0)
                    until(pe, s["flat_ready"], u - 1)
                    for c in range(DC):
                        last = pe.matmul(flat_ps[n][0:NE, :], router_w[:, c, :], rows_t[:, c, bass.ds(u * TG * P, TG * P)],
                                         start=c == 0, stop=c == DC - 1)
                    last.then_inc(s["flat_done"], 1)
                if at(-1):
                    u, n, g = at(-1)
                    pe.wait_ge(s["flat_ready"], u + 1)
                    until(pe, s["logit_ready"], u - 1)
                    for k in range(TG):
                        last = pe.transpose(logit_ps[n][:, k * NE:(k + 1) * NE], flat[n][:, k, :], ident[0:NE, 0:NE])
                    last.then_inc(s["logit_done"], 1)
            steps(pe, step, groups, 2, 0, 1, loop=False)
            pe.wait_ge(s["spread_ready"], 1)
            pe.matmul(mix_ps[0:NE + 2, 0:FL], b2_to[:, :], b2[:, :], start=True, stop=False)
            for c in range(NCH):
                last = pe.matmul(mix_ps[0:NE + 2, 0:FL], spread[:, c, :], w2[:, c + 1, :], start=False, stop=c == NCH - 1)
            last.then_inc(s["mix_done"], 1)

        @block.scalar
        def _(act):
            act.wait_ge(experts_loaded, 48)
            act.activation(gelu_b1[:, :], b1[:, 1:NCH + 1], ACT.Gelu).then_inc(s["gelu_done"], 1)

            def step(at):
                u, n, g = at(0)
                act.wait_ge(s["flat_done"], u + 1)
                until(act, s["logit_done"], u - 1)
                act.activation(flat[n][:, :, :], flat_ps[n][0:NE, :].rearrange("e (k r) -> e k r", k=TG), ACT.Copy).then_inc(s["flat_ready"], 1)
            steps(act, step, groups, 2, 0, 0, loop=False)
            act.activation(w1_split[0][:, :, :], w1[:, :, :], ACT.Copy).then_inc(s["w1_high_ready"], 1)
            act.wait_ge(s["shifted"], 1)
            act.activation(prob[:, :, :], logits[:, :, :], ACT.Exp).then_inc(s["exp_done"], 1)
            act.wait_ge(s["gap_ready"], 1)
            act.activation(ratio[:, :], gap[:, :], ACT.Exp).then_inc(s["ratio_done"], 1)
            act.wait_ge(s["mix_done"], 1)
            act.activation(mix[:, :], mix_ps[0:NE + 2, 0:FL], ACT.Copy).then_inc(s["mix_ready"], 1)

        @block.vector
        def _(dve):
            link = [0]

            def then(ins):
                link[0] += 1
                ins.then_inc(s["chain"], 1)
                dve.wait_ge(s["chain"], link[0])

            dve.wait_ge(s["loaded"], 16 * 6)
            dve.wait_ge(experts_loaded, 48)
            dve.tensor_scalar(w2[:, 0, :], w2[:, 0, :], 0.1, None, ALU.mult).then_inc(s["w2_scaled"], 1)
            then(dve.scalar_tensor_tensor(router_b[:, :], cost[:, :], -COST_LAMBDA, router_b[:, :], ALU.mult, ALU.add))

            dve.wait_ge(s["gelu_done"], 1)
            dve.wait_ge(s["cleared"], 1)
            for c in range(NCH):
                e = CHUNK_EXPERT[c]
                dve.tensor_scalar(spread[:, c, e:e + 1], gelu_b1[:, c:c + 1], -1.0, None, ALU.mult)
            dve.tensor_copy(spread[:, :, NE], gelu_b1[:, :]).then_inc(s["spread_ready"], 1)

            def step(at):
                u, n, g = at(0)
                dve.wait_ge(s["logit_done"], u + 1)
                dve.tensor_tensor(logits[:, bass.ds(u * TG, TG), :], logit_ps[n][:, 0:TG * NE].rearrange("p (k e) -> p k e", e=NE),
                                  router_b[:, :].unsqueeze(1).to_broadcast([P, TG, NE]), ALU.add).then_inc(s["logit_ready"], 1)
            steps(dve, step, groups, 2, 0, 0, loop=False)
            dve.wait_ge(s["logit_ready"], groups)

            def each(ap):
                return ap.unsqueeze(2).to_broadcast([P, NT, NE])

            then(dve.tensor_reduce(peak[:, :], logits[:, :, :], X, ALU.max))
            dve.tensor_tensor(logits[:, :, :], logits[:, :, :], each(peak[:, :]), ALU.subtract).then_inc(s["shifted"], 1)
            dve.wait_ge(s["exp_done"], 1)
            then(dve.tensor_reduce(total[:, :], prob[:, :, :], X, ALU.add))
            then(dve.reciprocal(inverse[:, :], total[:, :]))
            then(dve.tensor_tensor(prob[:, :, :], prob[:, :, :], each(inverse[:, :]), ALU.mult))
            for best, p_best in ((is_first, p_first), (is_second, p_second)):
                then(dve.tensor_reduce(p_best[:, :], prob[:, :, :], X, ALU.max))
                then(dve.tensor_tensor(best[:, :, :], prob[:, :, :], each(p_best[:, :]), ALU.is_equal))
                then(dve.tensor_tensor(best[:, :, :], best[:, :, :], falling[:, :].unsqueeze(1).to_broadcast([P, NT, NE]), ALU.mult))
                then(dve.tensor_reduce(total[:, :], best[:, :, :], X, ALU.max))
                then(dve.tensor_tensor(best[:, :, :], best[:, :, :], each(total[:, :]), ALU.is_equal))
                if best is is_first:
                    then(dve.scalar_tensor_tensor(prob[:, :, :], best[:, :, :], -2.0, prob[:, :, :], ALU.mult, ALU.add))
            dve.tensor_tensor(gap[:, :], p_second[:, :], p_first[:, :], ALU.subtract).then_inc(s["gap_ready"], 1)
            dve.wait_ge(s["ratio_done"], 1)
            then(dve.tensor_scalar(total[:, :], ratio[:, :], 1.0, None, ALU.add))
            then(dve.reciprocal(g_first[:, :], total[:, :]))
            then(dve.tensor_tensor(g_second[:, :], ratio[:, :], g_first[:, :], ALU.mult))
            dve.tensor_tensor(is_first[:, :, :], is_first[:, :, :], each(g_first[:, :]), ALU.mult)
            dve.tensor_tensor(is_second[:, :, :], is_second[:, :, :], each(g_second[:, :]), ALU.mult)
            dve.memset(coef[:, :, NE + 1], 0.1)
            then(dve.tensor_tensor(coef[:, :, NE], g_first[:, :], g_second[:, :], ALU.add))
            then(dve.tensor_tensor(coef[:, :, 0:NE], is_first[:, :, :], is_second[:, :, :], ALU.add))



def experts(nc, sem, out, x_sb, rows_t, coef, mix, w1, w2, b1, dense, dense_loaded, ident, tag="e"):
    CH = NCH + 1
    TR = TG * P
    units = NT // TG * CH
    NEX = NE + 1
    owner = [0] + [e + 1 for e in CHUNK_EXPERT]
    opens = [n == 0 or owner[n] != owner[n - 1] for n in range(CH)]
    closes = [n == CH - 1 or owner[n] != owner[n + 1] for n in range(CH)]
    NY = 3
    with ExitStack() as ctx:
        def sb(name, shape):
            return ctx.enter_context(nc.sbuf_tensor(f"{tag}_{name}", shape, F32))

        def ps(name):
            return ctx.enter_context(nc.psum_tensor(f"{tag}_{name}", [P, 512], F32))

        bias, bias2, down_w, down_b, core_w, up_w = dense
        gelu_h = sb("gelu_h", [P, TR])
        gelu_high, gelu_low = (ctx.enter_context(nc.sbuf_tensor(f"{tag}_gelu_{half}", [P, TR], F32R)) for half in ("high", "low"))
        hidden = [sb(f"hidden{k}", [P, TR]) for k in range(3)]
        gelu_x = sb("gelu_x", [P, DC, TR])
        coef_now = sb("coef_now", [P, TG, NE + 2])
        coef_t = sb("coef_t", [NE + 2, TG, P])
        acc, acc_t = sb("acc", [P, TG, FL]), sb("acc_t", [P, TG, P])
        hidden_ps = [ps(f"hidden_ps{k}") for k in range(2)]
        y_ps = [ps(f"y_ps{k}") for k in range(NY)]
        h_ps, turn_ps, out_ps = ps("h_ps"), ps("turn_ps"), ps("out_ps")

        names = ("bias_ready", "bias_added", "h_done", "gelu_h_ready", "gelu_high_ready", "gelu_low_ready", "hidden_done", "hidden_ready", "y_chunk", "y_added", "gelu_x_ready",
                 "coef_ready", "coef_turned", "coef_t_ready", "acc_turned", "acc_t_ready", "out_done", "x_ready", "stored")
        s = {n: sem(f"{tag}_{n}") for n in names}
        block = ctx.enter_context(nc.Block())
        out_rows = out.rearrange("b s d -> (b s) d").rearrange("(g k p) d -> g p k d", k=2, p=P)
        assert CH % 3 == 0 and NEX % NY == 0

        @block.sync
        def _(sp):
            def step(at):
                u, n, g = at(0)
                sp.wait_ge(s["x_ready"], u + 1)
                sp.dma_start(out_rows[u], x_sb[:, bass.ds(u * 2, 2), :]).then_inc(s["stored"], 16)
            steps(sp, step, NT // 2, 2, 0, 0)
            sp.wait_ge(s["stored"], 16 * NT // 2)

        @block.gpsimd
        def _(pool):
            pool.wait_ge(dense_loaded, 16 * len(dense))
            pool.tensor_tensor(bias[:, :], bias[:, :], bias2[:, :], ALU.add).then_inc(s["bias_ready"], 1)
            pool.wait_ge(s["bias_ready"], 1)
            pool.tensor_tensor(x_sb[:, :, :], x_sb[:, :, :], bias[:, :].unsqueeze(1).to_broadcast([P, NT, D]), ALU.add).then_inc(s["bias_added"], 1)

        @block.tensor
        def _(pe):
            pe.wait_ge(dense_loaded, 16 * len(dense))

            def step(at):
                if at(0):
                    u, n, g = at(0)
                    e = owner[n]
                    y = y_ps[e % NY]
                    pe.wait_ge(s["hidden_ready"], u + 1)
                    if opens[n]:
                        until(pe, s["y_added"], g * NEX + e - NY + 1)
                    if n == 0:
                        pe.wait_ge(s["coef_t_ready"], g + 1)
                    for k in range(TG):
                        last = pe.matmul(y[:, k * FL:(k + 1) * FL], hidden[n % 3][:, k * P:(k + 1) * P], w2[:, n, :],
                                         start=opens[n] and k == 0, stop=closes[n] and n > 0, skip_group_check=True)
                    if n == 0:
                        for k in range(TG):
                            last = pe.matmul(y[:, k * FL:(k + 1) * FL], coef_t[:, k, :], mix[:, :], start=False, stop=True,
                                             skip_group_check=True)
                    last.then_inc(s["y_chunk"], 1)
                if at(-1) and at(-1)[1] == CH - 1:
                    u, n, g = at(-1)
                    pe.wait_ge(s["y_added"], (g + 1) * NEX)
                    until(pe, s["coef_t_ready"], min(g + 2, NT // TG) if isinstance(g, int) else g + 2)
                    for k in range(TG):
                        last = pe.transpose(turn_ps[:, k * P:(k + 1) * P], acc[:, k, :], ident[:, :])
                    last.then_inc(s["acc_turned"], 1)
                if at(2):
                    u, n, g = at(2)
                    if n == 0:
                        pe.wait_ge(s["gelu_high_ready"], g + 1)
                        pe.wait_ge(s["gelu_low_ready"], g + 1)
                    until(pe, s["hidden_ready"], u - 1 if n else u)
                    split_product(pe, hidden_ps[n % 2][:, :], [half[:, n, :] for half in w1], (gelu_high[:, :], gelu_low[:, :]),
                                  True, True).then_inc(s["hidden_done"], 1)
                if at(-2) and at(-2)[1] == CH - 1:
                    u, n, g = at(-2)
                    pe.wait_ge(s["acc_t_ready"], g + 1)
                    pe.wait_ge(s["gelu_x_ready"], g + 1)
                    pe.wait_ge(s["gelu_h_ready"], min(g + 2, NT // TG) if isinstance(g, int) else g + 2)
                    for r in range(2):
                        bank = (out_ps, h_ps)[r]
                        for q in range(2):
                            k = 2 * r + q
                            for c in range(DC):
                                pe.matmul(bank[:, q * D:(q + 1) * D], gelu_x[:, c, k * P:(k + 1) * P], core_w[:, c, :],
                                          start=c == 0, stop=False)
                            last = pe.matmul(bank[:, q * D:(q + 1) * D], acc_t[:, k, :], up_w[:, :], start=False, stop=True)
                        last.then_inc(s["out_done"], 1)
                if at(5) and at(5)[1] == 0:
                    u, n, g = at(5)
                    until(pe, s["gelu_h_ready"], g)
                    until(pe, s["x_ready"], 2 * g - 2)
                    for c in range(DC):
                        last = pe.matmul(h_ps[:, :], down_w[:, c, :], rows_t[:, c, bass.ds(g * TR, TR)], start=c == 0, stop=c == DC - 1)
                    last.then_inc(s["h_done"], 1)
                if at(6) and at(6)[1] == 0:
                    u, n, g = at(6)
                    pe.wait_ge(s["coef_ready"], g + 1)
                    until(pe, s["acc_t_ready"], g - 1)
                    until(pe, s["coef_t_ready"], g)
                    for k in range(TG):
                        last = pe.transpose(turn_ps[0:NE + 2, k * P:(k + 1) * P], coef_now[:, k, :], ident[:, :])
                    last.then_inc(s["coef_turned"], 1)

            steps(pe, step, units, CH, 6, 2)

        @block.scalar
        def _(act):
            act.wait_ge(dense_loaded, 16 * len(dense))

            def step(at):
                if at(4) and at(4)[1] == 0:
                    u, n, g = at(4)
                    act.wait_ge(s["h_done"], g + 1)
                    until(act, s["gelu_low_ready"], g)
                    act.activation(gelu_h[:, :], h_ps[:, :], ACT.Gelu, bias=down_b[:, 0:1]).then_inc(s["gelu_h_ready"], 1)
                if at(3) and at(3)[1] == 0:
                    u, n, g = at(3)
                    act.wait_ge(s["gelu_h_ready"], g + 1)
                    until(act, s["hidden_done"], u)
                    act.activation(gelu_high[:, :], gelu_h[:, :], ACT.Copy).then_inc(s["gelu_high_ready"], 1)
                if at(2):
                    u, n, g = at(2)
                    act.wait_ge(s["hidden_done"], u + 1)
                    until(act, s["y_chunk"], u - 2)
                    act.activation(hidden[n % 3][:, :], hidden_ps[n % 2][:, :], ACT.Gelu, bias=b1[:, n:n + 1]).then_inc(s["hidden_ready"], 1)
                if at(0) and at(0)[1] == 6:
                    u, n, g = at(0)
                    until(act, s["out_done"], 2 * g)
                    for c in range(DC):
                        last = act.activation(gelu_x[:, c, :], rows_t[:, c, bass.ds(g * TR, TR)], ACT.Gelu)
                    last.then_inc(s["gelu_x_ready"], 1)
            steps(act, step, units, CH, 4, 0)

        @block.vector
        def _(dve):
            dve.wait_ge(s["bias_added"], 1)

            def step(at):
                if at(3) and at(3)[1] == 0:
                    u, n, g = at(3)
                    dve.wait_ge(s["gelu_high_ready"], g + 1)
                    dve.tensor_tensor(gelu_low[:, :], gelu_h[:, :], gelu_high[:, :].bitcast(F32), ALU.subtract).then_inc(s["gelu_low_ready"], 1)
                if at(0) and closes[at(0)[1]]:
                    u, n, g = at(0)
                    e = owner[n]
                    y = y_ps[e % NY][:, :].rearrange("p (k l) -> p k l", k=TG)
                    dve.wait_ge(s["y_chunk"], u + 1)
                    if e == 0:
                        until(dve, s["acc_turned"], g)
                        dve.tensor_copy(acc[:, :, :], y).then_inc(s["y_added"], 1)
                    else:
                        dve.wait_ge(s["y_added"], g * NEX + e)
                        for k in range(TG):
                            last = dve.scalar_tensor_tensor(acc[:, k, :], y[:, k, :], coef[:, g * TG + k, e - 1:e], acc[:, k, :],
                                                            ALU.mult, ALU.add)
                        last.then_inc(s["y_added"], 1)
                if at(-1) and at(-1)[1] == CH - 1:
                    u, n, g = at(-1)
                    dve.wait_ge(s["acc_turned"], g + 1)
                    dve.tensor_copy(acc_t[:, :, :], turn_ps[:, :].rearrange("p (k r) -> p k r", k=TG)).then_inc(s["acc_t_ready"], 1)
                if at(-2) and at(-2)[1] == CH - 1:
                    u, n, g = at(-2)
                    for r in range(2):
                        dve.wait_ge(s["out_done"], 2 * g + r + 1)
                        rows = x_sb[:, bass.ds(g * TG + 2 * r, 2), :]
                        dve.tensor_tensor(rows, (out_ps, h_ps)[r][:, :].rearrange("p (k d) -> p k d", k=2), rows, ALU.add).then_inc(s["x_ready"], 1)
                if at(8) and at(8)[1] == 0:
                    u, n, g = at(8)
                    until(dve, s["coef_turned"], g)
                    dve.tensor_scalar(coef_now[:, :, :], coef[:, bass.ds(g * TG, TG), :], 1.0, None, ALU.mult).then_inc(s["coef_ready"], 1)
                if at(5) and at(5)[1] == 0:
                    u, n, g = at(5)
                    dve.wait_ge(s["coef_turned"], g + 1)
                    until(dve, s["y_chunk"], g * CH - CH + 1)
                    dve.tensor_copy(coef_t[:, :, :], turn_ps[0:NE + 2, :].rearrange("p (k r) -> p k r", k=TG)).then_inc(s["coef_t_ready"], 1)
            steps(dve, step, units, CH, 8, 2)



CONSTANTS = {
    "ident": [P, P], "mask": [P, P], "minus_half": [P, NT],
}
ROTATIONS = {
    "cos_k": [LN, LC, CD], "sin_k": [LN, LC, CD], "cos_q": [QC, 2, S], "sin_q": [QC, 2, S],
}


def perceiver_block(nc, w, out):
    with ExitStack() as ctx:
        taken = []

        def sem(name):
            taken.append(nc.alloc_semaphore(name))
            return taken[-1]

        def semaphores_end():
            nc.clear_and_free_semaphores(taken)
            nc.all_engine_barrier()
            taken.clear()

        x_sb = ctx.enter_context(nc.sbuf_tensor("x_sb", [P, NT, D], F32))
        mean = ctx.enter_context(nc.sbuf_tensor("mean", [P, NT], F32))
        rstd = ctx.enter_context(nc.sbuf_tensor("rstd", [P, NT], F32))
        stats = ctx.enter_context(nc.sbuf_tensor("stats", [P, NT, 6], F32))
        const = {n: ctx.enter_context(nc.sbuf_tensor(n, shape, F32)) for n, shape in CONSTANTS.items()}
        ident, minus_half = const["ident"], const["minus_half"]

        wide = ctx.enter_context(nc.sbuf_tensor("wide", [P, DC * ROWS], F32))
        assert DC * ROWS == 2 * DC * AH * DV
        wv, wg = (wide[:, k * DC * AH * DV:(k + 1) * DC * AH * DV].rearrange("p (c n) -> p c n", c=DC) for k in range(2))

        with ExitStack() as one:
            def sb(name, shape):
                return one.enter_context(nc.sbuf_tensor(name, shape, F32))

            rotation = {n: sb(n, shape) for n, shape in ROTATIONS.items()}
            x_loaded, const_loaded = [sem(f"x_loaded{j}") for j in range(4)], sem("const_loaded")
            with nc.Block() as block:
                @block.sync
                def _(sp):
                    rows = w["x"].rearrange("b s d -> (b s) d").rearrange("(i p) d -> p i d", p=P)
                    q = NT // len(x_loaded)
                    for j, quarter_loaded in enumerate(x_loaded):
                        sp.dma_start(x_sb[:, j * q:(j + 1) * q, :], rows[:, j * q:(j + 1) * q, :]).then_inc(quarter_loaded, 16)

                @block.scalar
                def _(act):
                    for n, to in (const | rotation).items():
                        act.dma_start(to[:], w[n]).then_inc(const_loaded, 16)

            xnt = wide[:, :].rearrange("p (c s b) -> p c s b", c=DC, s=S)
            queries = sb("queries", [P, NP, S, B])
            gmap, omap = sb("gmap", [QC, 2, HH, CD]), sb("omap", [P, NP, D])
            slot_weights = [(to[:, c, :], w[n][c * P:(c + 1) * P, :]) for n, to in (("awv", wv), ("awg", wg)) for c in range(DC)]
            for hh in range(2):
                with ExitStack() as half:
                    qmap = [half.enter_context(nc.sbuf_tensor(f"qmap{hh}_{part}", [QC, 2, HH, D], F32R)) for part in ("high", "low")]
                    if hh == 0:
                        fold_weights(nc, sem, w, hh, qmap, gmap, omap, f"f{hh}", beside=lambda block, ctx: row_statistics(
                            sem, block, ctx, nc, stats, mean, rstd, minus_half, "n1", x_sb, x_loaded,
                            const_loaded, len(const | rotation)))
                        transposed_rows(nc, sem, x_sb, mean, rstd, ident,
                                        lambda i: xnt[:, :, :, bass.ds(i * BT, BT)].rearrange("p c s b -> p c b s"), "t1")
                    else:
                        fold_weights(nc, sem, w, hh, qmap, gmap, omap, f"f{hh}")
                    make_queries(nc, sem, qmap, gmap, rotation["cos_q"], rotation["sin_q"], xnt, queries, f"q{hh}")
                last = hh == 1
                attend(nc, sem, w, x_sb, queries, omap, rotation["cos_k"], rotation["sin_k"], ident, f"a{hh}",
                       stats=stats if last else None, ahead=slot_weights if last else ())

        semaphores_end()
        with ExitStack() as rest:
            def sb(name, shape):
                return rest.enter_context(nc.sbuf_tensor(name, shape, F32))

            with ExitStack() as two:
                def halves(name, shape):
                    return [two.enter_context(nc.sbuf_tensor(f"{name}_{half}", shape, F32R)) for half in ("high", "low")]

                wv_split, wg_split, wo_split = halves("wv", [P, DC, AH * DV]), halves("wg", [P, DC, AH * DV]), halves("wo", [DV, AH, D])
                wq, wk, ws = (two.enter_context(nc.sbuf_tensor(n, [P, DC, AH * DK], F32)) for n in ("wq", "wk", "ws"))
                with ExitStack() as temporary, nc.Block() as block:
                    row_statistics(sem, block, temporary, nc, stats, mean, rstd, minus_half, "n2")
                    split_weights(sem, block, temporary, nc, w, [(wv, wv_split), (wg, wg_split)], wo_split, w["norm_w"],
                                  [(ws, w["aws"]), (wq, w["awq"]), (wk, w["awk"])], "p")
                slot_attention(nc, sem, w, x_sb, mean, rstd, ident, const["mask"], (wq, wk, ws, wv_split, wg_split, wo_split), wide, stats)

            semaphores_end()
            w1_split = [rest.enter_context(nc.sbuf_tensor(f"w1_{half}", [P, NCH + 1, P], F32R)) for half in ("high", "low")]
            w1, w2, b1 = sb("w1", [P, NCH + 1, P]), sb("w2", [P, NCH + 1, FL]), sb("b1", [P, NCH + 1])
            dense = bias, bias2, down_w, down_b, core_w, up_w = (
                sb("bias", [P, D]), sb("bias2", [P, D]), sb("down_w", [P, DC, FL]), sb("down_b", [P, 1]),
                sb("core_w", [P, DC, D]), sb("up_w", [P, D]))
            experts_loaded, dense_loaded = sem("experts_loaded"), sem("dense_loaded")
            with ExitStack() as temporary, nc.Block() as block:
                row_statistics(sem, block, temporary, nc, stats, mean, rstd, minus_half, "n3")

                @block.sync
                def _(sp):
                    sp.dma_start(b1[:, :], w["b1"]).then_inc(experts_loaded, 16)
                    sp.dma_start(w2[:, :, :], w["w2"].rearrange("(n p) l -> p n l", p=P)).then_inc(experts_loaded, 16)
                    sp.dma_start(w1[:, :, :], w["w1"].rearrange("p (n q) -> p n q", q=P)).then_inc(experts_loaded, 16)
                    sp.dma_start(down_w[:, :, :], w["down_w"].rearrange("(c p) n -> p c n", p=P)).then_inc(dense_loaded, 16)
                    sp.dma_start(core_w[:, :, :], w["core_w"].rearrange("(c p) n -> p c n", p=P)).then_inc(dense_loaded, 16)
                    sp.dma_start(up_w[:, :], w["up_w"]).then_inc(dense_loaded, 16)
                    sp.dma_start(down_b[:, :], w["down_b"].rearrange("(p o) -> p o", o=1)).then_inc(dense_loaded, 16)
                    sp.dma_start(bias[:, :], w["core_b"].partition_broadcast(P)).then_inc(dense_loaded, 16)
                    sp.dma_start(bias2[:, :], w["up_b"].partition_broadcast(P)).then_inc(dense_loaded, 16)
            rows_t = wide[:, :].rearrange("p (c r) -> p c r", c=DC)
            coef, mix = sb("coef", [P, NT, NE + 2]), sb("mix", [NE + 2, FL])
            transposed_rows(nc, sem, x_sb, mean, rstd, ident,
                            lambda i: rows_t[:, :, bass.ds(i * P, P)].rearrange("p c (b s) -> p c b s", b=BT), "t3")
            route(nc, sem, w, rows_t, coef, mix, w2, b1, ident, experts_loaded, w1, w1_split)
            experts(nc, sem, out, x_sb, rows_t, coef, mix, w1_split, w2, b1, dense, dense_loaded, ident)



def constants():
    f32 = np.float32

    def tables(length, dim):
        inv = f32(1.0) / np.power(f32(10000.0), np.arange(0, dim, 2, dtype=f32) / f32(dim))
        f = np.arange(length, dtype=f32)[:, None] * inv[None, :].astype(f32)
        return np.repeat(np.sin(f), 2, axis=-1), np.repeat(np.cos(f), 2, axis=-1)

    row = np.arange(P)
    sin_k, cos_k = (np.concatenate([a[:L], np.zeros((LC * LN - L, CD), f32)]).reshape(LC, LN, CD).transpose(1, 0, 2)
                    for a in tables(L, CD))
    sign = np.where(np.arange(CD) < CD // 2, f32(-1), f32(1))
    sin_q, cos_q = (a.reshape(S, 2, QC).transpose(2, 1, 0) for a in tables(S, CQ))
    out = {
        "ident": np.eye(P), "minus_half": np.full((P, NT), -0.5),
        "mask": (row[:, None] // S == row[None, :] // S) & (row[:, None] <= row[None, :]),
        "cos_k": cos_k, "sin_k": sin_k * sign, "cos_q": cos_q,
        "cost": [2 * FL * h for h in HID],
        "falling": np.arange(NE, 0, -1),
        "b2_to": [[float(k == NE + (e == NE)) for k in range(NE + 2)] for e in range(NE + 1)],
        "sin_q": np.stack([sin_q[:, 1], -sin_q[:, 0]], axis=1),
    }
    return {n: np.ascontiguousarray(a, dtype=f32) for n, a in out.items()}


def lay_out(i):
    names = ["shared"] + [f"e{e}" for e in range(NE)]
    return {
        "x": i["x"], "ctx": i["ctx_512"],
        "wq": i["L0_xattn_Wq"], "wkq": i["L0_xattn_w_kc_q"], "wkv": i["L0_xattn_w_kc_kv"],
        "wqr_t": i["L0_xattn_W_qr"].transpose(0, 2, 1), "wkr_t": i["L0_xattn_W_kr"].transpose(0, 2, 1),
        "xwo_t": i["L0_xattn_Wo"].T,
        "awq": i["L0_attn_Wq"], "awk": i["L0_attn_Wk"], "aws": i["L0_attn_Ws"], "awv": i["L0_attn_Wv"],
        "awg": i["L0_attn_Wg"], "awo": i["L0_attn_Wo"], "norm_w": i["L0_attn_g_norm_weight"],
        **{n: i[f"L0_ffn_{n}"] for n in ("router_w", "router_b", "down_w", "down_b", "core_w", "core_b", "up_w", "up_b")},
        "w1": np.concatenate([i[f"L0_ffn_{e}_w1"] for e in names], axis=1),
        "b1": np.concatenate([i[f"L0_ffn_{e}_b1"] for e in names]).reshape(-1, P).T,
        "w2": np.concatenate([i[f"L0_ffn_{e}_w2"] for e in names]),
        "b2": np.stack([i[f"L0_ffn_{e}_b2"] for e in names[1:] + names[:1]]),
    }


def kernel(**inputs):
    import concourse.bacc as bacc
    from concourse.bass_utils import run_bass_kernel_spmd

    nc = bacc.Bacc("TRN2", target_bir_lowering=False, num_devices=1)
    inputs = {n: np.asarray(a) for n, a in inputs.items()}
    arrays, w = {}, {}
    for name, a in {**lay_out(inputs), **constants()}.items():
        arrays[f"in_{name}"] = np.ascontiguousarray(a)
        w[name] = nc.dram_tensor(f"in_{name}", a.shape, F32, kind="ExternalInput").ap()
    out = nc.dram_tensor("out", [B, S, D], F32, kind="ExternalOutput").ap()
    perceiver_block(nc, w, out)
    r = run_bass_kernel_spmd(nc, [arrays], core_ids=[0])
    return r.results[0]["out"]
```
